# Optimizing a Trainium2 kernel written in Bass

```python
import numpy as np
import jax
import jax.numpy as jnp

def _softmax(x, axis=-1):
    return jax.nn.softmax(x, axis=axis)

def _gelu(x):
    return jax.nn.gelu(x, approximate=True)

def _silu(x):
    return jax.nn.silu(x)

def _sigmoid(x):
    return jax.nn.sigmoid(x)

def _layernorm(x, axis=-1, eps=1e-05):
    m = jnp.mean(x, axis=axis, keepdims=True)
    v = jnp.var(x, axis=axis, keepdims=True)
    return (x - m) / jnp.sqrt(v + eps)

def _scatter_add(tgt, idx, src, axis=0):
    return tgt.at[idx].add(src)

def _segment_sum(src, seg, n):
    return jax.ops.segment_sum(src, seg, n)
kernel_name = 'mk_hybrid_d1_jaxref_r8_0f6c97'

def setup_inputs(seed: int=0):
    np.random.seed(seed)
    _w = jnp.asarray

    def _L0_attn_a_setup():
        import jax, jax.numpy as jnp
        import numpy as np
        B, N, D = (4, 512, 128)
        H, DH = (16, 64)
        DFF = 512
        M = 64
        EPS_KERN = 1e-06
        EPS_LN = 1e-06

        def _softmax_kernel_feats(data, proj, is_query):
            dn = 1.0 / jnp.sqrt(jnp.sqrt(jnp.float32(data.shape[-1])))
            ratio = 1.0 / jnp.sqrt(jnp.float32(proj.shape[0]))
            data_dash = jnp.einsum('bnhd,md->bnhm', data * dn, proj)
            diag = jnp.sum(jnp.square(data), axis=-1, keepdims=True) * (dn * dn) / 2.0
            if is_query:
                mx = jnp.max(data_dash, axis=-1, keepdims=True)
            else:
                mx = jnp.max(data_dash)
            return ratio * (jnp.exp(data_dash - diag - mx) + EPS_KERN)

        def _layernorm(x, g, b):
            mu = jnp.mean(x, axis=-1, keepdims=True)
            var = jnp.mean(jnp.square(x - mu), axis=-1, keepdims=True)
            return (x - mu) * jax.lax.rsqrt(var + EPS_LN) * g + b

        def _encoder_forward(x, Wq, Wk, Wv, Wo, proj, W1, b1, W2, b2, ln1_g, ln1_b, ln2_g, ln2_b):
            q = jnp.einsum('bnd,dhk->bnhk', x, Wq)
            k = jnp.einsum('bnd,dhk->bnhk', x, Wk)
            v = jnp.einsum('bnd,dhk->bnhk', x, Wv)
            qf = _softmax_kernel_feats(q, proj, True)
            kf = _softmax_kernel_feats(k, proj, False)
            kv = jnp.einsum('bnhm,bnhd->bhmd', kf, v)
            num = jnp.einsum('bnhm,bhmd->bnhd', qf, kv)
            den = jnp.einsum('bnhm,bhm->bnh', qf, jnp.sum(kf, axis=1))
            attn = num / den[..., None]
            attn_out = jnp.einsum('bnhd,hdo->bno', attn, Wo)
            out1 = _layernorm(x + attn_out, ln1_g, ln1_b)
            h = jax.nn.elu(out1 @ W1 + b1)
            ffn_out = h @ W2 + b2
            return _layernorm(out1 + ffn_out, ln2_g, ln2_b)
        key = jax.random.key(seed)
        ks = jax.random.split(key, 12)
        s = 0.02
        inp = {'x': jax.random.normal(ks[0], (B, N, D), jnp.float32), 'Wq': jax.random.normal(ks[1], (D, H, DH), jnp.float32) * s, 'Wk': jax.random.normal(ks[2], (D, H, DH), jnp.float32) * s, 'Wv': jax.random.normal(ks[3], (D, H, DH), jnp.float32) * s, 'Wo': jax.random.normal(ks[4], (H, DH, D), jnp.float32) * s, 'proj': jax.random.normal(ks[5], (M, DH), jnp.float32), 'W1': jax.random.normal(ks[6], (D, DFF), jnp.float32) * s, 'b1': jnp.zeros((DFF,), jnp.float32), 'W2': jax.random.normal(ks[7], (DFF, D), jnp.float32) * s, 'b2': jnp.zeros((D,), jnp.float32), 'ln1_g': jnp.ones((D,), jnp.float32), 'ln1_b': jnp.zeros((D,), jnp.float32), 'ln2_g': jnp.ones((D,), jnp.float32), 'ln2_b': jnp.zeros((D,), jnp.float32)}
        return inp
    _L0_attn_a_in = _L0_attn_a_setup()

    def _L0_attn_b_setup():
        import jax, jax.numpy as jnp
        import numpy as np
        D_MODEL = 128
        NUM_HEADS = 16
        HEAD_DIM = D_MODEL // NUM_HEADS
        MAX_SEQ_LEN = 256

        def _rope_tables(seq_len, head_dim):
            inv_freq = 1.0 / 10000.0 ** (jnp.arange(0, head_dim, 2, dtype=jnp.float32) / head_dim)
            pos = jnp.arange(seq_len, dtype=jnp.float32)
            freqs = jnp.einsum('i,j->ij', pos, inv_freq)
            return (jnp.cos(freqs), jnp.sin(freqs))

        def _apply_rope(x, cos_half, sin_half):
            x_even = x[..., ::2]
            x_odd = x[..., 1::2]
            rot_even = x_even * cos_half - x_odd * sin_half
            rot_odd = x_even * sin_half + x_odd * cos_half
            return jnp.stack([rot_even, rot_odd], axis=-1).reshape(x.shape)
        key = jax.random.key(seed)
        ks = jax.random.split(key, 9)
        B, S = (2, 256)
        glorot = lambda k: jax.random.normal(k, (D_MODEL, D_MODEL), dtype=jnp.float32) * (1.0 / np.sqrt(D_MODEL))
        return {'x': jax.random.normal(ks[0], (B, S, D_MODEL), dtype=jnp.float32), 'wq': glorot(ks[1]), 'bq': jnp.zeros((D_MODEL,), jnp.float32), 'wk': glorot(ks[2]), 'bk': jnp.zeros((D_MODEL,), jnp.float32), 'wv': glorot(ks[3]), 'bv': jnp.zeros((D_MODEL,), jnp.float32), 'wo': glorot(ks[4]), 'bo': jnp.zeros((D_MODEL,), jnp.float32)}
    _L0_attn_b_in = _L0_attn_b_setup()

    def _L0_ffn_setup():
        import jax, jax.numpy as jnp
        import numpy as np
        B, S, D, H, E, F, K = (2, 128, 128, 16, 8, 512, 2)
        EPS = 1e-05

        def _layernorm(x, g, b):
            mu = jnp.mean(x, axis=-1, keepdims=True)
            var = jnp.mean(jnp.square(x - mu), axis=-1, keepdims=True)
            return (x - mu) * jax.lax.rsqrt(var + EPS) * g + b
        key = jax.random.key(seed)
        ks = jax.random.split(key, 12)
        w = lambda k, shape: jax.random.normal(k, shape, dtype=jnp.float32) * 0.02
        return {'x': jax.random.normal(ks[0], (B, S, D), dtype=jnp.float32), 'ln1_g': jnp.ones((D,), jnp.float32), 'ln1_b': jnp.zeros((D,), jnp.float32), 'ln2_g': jnp.ones((D,), jnp.float32), 'ln2_b': jnp.zeros((D,), jnp.float32), 'Wq': w(ks[1], (D, D)), 'Wk': w(ks[2], (D, D)), 'Wv': w(ks[3], (D, D)), 'Wo': w(ks[4], (D, D)), 'Wg': w(ks[5], (D, E)), 'W1': w(ks[6], (E, D, F)), 'b1': jnp.zeros((E, F), jnp.float32), 'W2': w(ks[7], (E, F, D)), 'b2': jnp.zeros((E, D), jnp.float32)}
    _L0_ffn_in = _L0_ffn_setup()
    _d = {'L0_attn_a_x': _L0_attn_a_in['x'], 'L0_attn_a_Wq': _L0_attn_a_in['Wq'], 'L0_attn_a_Wk': _L0_attn_a_in['Wk'], 'L0_attn_a_Wv': _L0_attn_a_in['Wv'], 'L0_attn_a_Wo': _L0_attn_a_in['Wo'], 'L0_attn_a_proj': _L0_attn_a_in['proj'], 'L0_attn_a_W1': _L0_attn_a_in['W1'], 'L0_attn_a_b1': _L0_attn_a_in['b1'], 'L0_attn_a_W2': _L0_attn_a_in['W2'], 'L0_attn_a_b2': _L0_attn_a_in['b2'], 'L0_attn_a_ln1_g': _L0_attn_a_in['ln1_g'], 'L0_attn_a_ln1_b': _L0_attn_a_in['ln1_b'], 'L0_attn_a_ln2_g': _L0_attn_a_in['ln2_g'], 'L0_attn_a_ln2_b': _L0_attn_a_in['ln2_b'], 'L0_attn_b_wq': _L0_attn_b_in['wq'], 'L0_attn_b_bq': _L0_attn_b_in['bq'], 'L0_attn_b_wk': _L0_attn_b_in['wk'], 'L0_attn_b_bk': _L0_attn_b_in['bk'], 'L0_attn_b_wv': _L0_attn_b_in['wv'], 'L0_attn_b_bv': _L0_attn_b_in['bv'], 'L0_attn_b_wo': _L0_attn_b_in['wo'], 'L0_attn_b_bo': _L0_attn_b_in['bo'], 'L0_ffn_ln1_g': _L0_ffn_in['ln1_g'], 'L0_ffn_ln1_b': _L0_ffn_in['ln1_b'], 'L0_ffn_ln2_g': _L0_ffn_in['ln2_g'], 'L0_ffn_ln2_b': _L0_ffn_in['ln2_b'], 'L0_ffn_Wq': _L0_ffn_in['Wq'], 'L0_ffn_Wk': _L0_ffn_in['Wk'], 'L0_ffn_Wv': _L0_ffn_in['Wv'], 'L0_ffn_Wo': _L0_ffn_in['Wo'], 'L0_ffn_Wg': _L0_ffn_in['Wg'], 'L0_ffn_W1': _L0_ffn_in['W1'], 'L0_ffn_b1': _L0_ffn_in['b1'], 'L0_ffn_W2': _L0_ffn_in['W2'], 'L0_ffn_b2': _L0_ffn_in['b2']}
    _x0 = _d['L0_attn_a_x']
    _d['L0_attn_a_x'] = jax.random.normal(jax.random.fold_in(jax.random.key(seed), 1), (8, 512, 128), dtype=_x0.dtype)
    del _x0
    return _d

def reference(L0_attn_a_x, L0_attn_a_Wq, L0_attn_a_Wk, L0_attn_a_Wv, L0_attn_a_Wo, L0_attn_a_proj, L0_attn_a_W1, L0_attn_a_b1, L0_attn_a_W2, L0_attn_a_b2, L0_attn_a_ln1_g, L0_attn_a_ln1_b, L0_attn_a_ln2_g, L0_attn_a_ln2_b, L0_attn_b_wq, L0_attn_b_bq, L0_attn_b_wk, L0_attn_b_bk, L0_attn_b_wv, L0_attn_b_bv, L0_attn_b_wo, L0_attn_b_bo, L0_ffn_ln1_g, L0_ffn_ln1_b, L0_ffn_ln2_g, L0_ffn_ln2_b, L0_ffn_Wq, L0_ffn_Wk, L0_ffn_Wv, L0_ffn_Wo, L0_ffn_Wg, L0_ffn_W1, L0_ffn_b1, L0_ffn_W2, L0_ffn_b2):

    def _L0_attn_a_ref(x, Wq, Wk, Wv, Wo, proj, W1, b1, W2, b2, ln1_g, ln1_b, ln2_g, ln2_b):
        import jax, jax.numpy as jnp
        import numpy as np
        B, N, D = (4, 512, 128)
        H, DH = (16, 64)
        DFF = 512
        M = 64
        EPS_KERN = 1e-06
        EPS_LN = 1e-06

        def _softmax_kernel_feats(data, proj, is_query):
            dn = 1.0 / jnp.sqrt(jnp.sqrt(jnp.float32(data.shape[-1])))
            ratio = 1.0 / jnp.sqrt(jnp.float32(proj.shape[0]))
            data_dash = jnp.einsum('bnhd,md->bnhm', data * dn, proj)
            diag = jnp.sum(jnp.square(data), axis=-1, keepdims=True) * (dn * dn) / 2.0
            if is_query:
                mx = jnp.max(data_dash, axis=-1, keepdims=True)
            else:
                mx = jnp.max(data_dash)
            return ratio * (jnp.exp(data_dash - diag - mx) + EPS_KERN)

        def _layernorm(x, g, b):
            mu = jnp.mean(x, axis=-1, keepdims=True)
            var = jnp.mean(jnp.square(x - mu), axis=-1, keepdims=True)
            return (x - mu) * jax.lax.rsqrt(var + EPS_LN) * g + b

        def _encoder_forward(x, Wq, Wk, Wv, Wo, proj, W1, b1, W2, b2, ln1_g, ln1_b, ln2_g, ln2_b):
            q = jnp.einsum('bnd,dhk->bnhk', x, Wq)
            k = jnp.einsum('bnd,dhk->bnhk', x, Wk)
            v = jnp.einsum('bnd,dhk->bnhk', x, Wv)
            qf = _softmax_kernel_feats(q, proj, True)
            kf = _softmax_kernel_feats(k, proj, False)
            kv = jnp.einsum('bnhm,bnhd->bhmd', kf, v)
            num = jnp.einsum('bnhm,bhmd->bnhd', qf, kv)
            den = jnp.einsum('bnhm,bhm->bnh', qf, jnp.sum(kf, axis=1))
            attn = num / den[..., None]
            attn_out = jnp.einsum('bnhd,hdo->bno', attn, Wo)
            out1 = _layernorm(x + attn_out, ln1_g, ln1_b)
            h = jax.nn.elu(out1 @ W1 + b1)
            ffn_out = h @ W2 + b2
            return _layernorm(out1 + ffn_out, ln2_g, ln2_b)
        return _encoder_forward(x, Wq, Wk, Wv, Wo, proj, W1, b1, W2, b2, ln1_g, ln1_b, ln2_g, ln2_b)

    def _L0_attn_b_ref(x, wq, bq, wk, bk, wv, bv, wo, bo):
        import jax, jax.numpy as jnp
        import numpy as np
        D_MODEL = 128
        NUM_HEADS = 16
        HEAD_DIM = D_MODEL // NUM_HEADS
        MAX_SEQ_LEN = 256

        def _rope_tables(seq_len, head_dim):
            inv_freq = 1.0 / 10000.0 ** (jnp.arange(0, head_dim, 2, dtype=jnp.float32) / head_dim)
            pos = jnp.arange(seq_len, dtype=jnp.float32)
            freqs = jnp.einsum('i,j->ij', pos, inv_freq)
            return (jnp.cos(freqs), jnp.sin(freqs))

        def _apply_rope(x, cos_half, sin_half):
            x_even = x[..., ::2]
            x_odd = x[..., 1::2]
            rot_even = x_even * cos_half - x_odd * sin_half
            rot_odd = x_even * sin_half + x_odd * cos_half
            return jnp.stack([rot_even, rot_odd], axis=-1).reshape(x.shape)
        B, S, _ = x.shape
        q = (x @ wq + bq).reshape(B, S, NUM_HEADS, HEAD_DIM)
        k = (x @ wk + bk).reshape(B, S, NUM_HEADS, HEAD_DIM)
        v = (x @ wv + bv).reshape(B, S, NUM_HEADS, HEAD_DIM)
        cos, sin = _rope_tables(S, HEAD_DIM)
        cos = cos[None, :, None, :]
        sin = sin[None, :, None, :]
        q = _apply_rope(q, cos, sin)
        k = _apply_rope(k, cos, sin)
        q = q.transpose(0, 2, 1, 3)
        k = k.transpose(0, 2, 1, 3)
        v = v.transpose(0, 2, 1, 3)
        scores = jnp.einsum('bhqd,bhkd->bhqk', q, k) / jnp.sqrt(jnp.float32(HEAD_DIM))
        causal = jnp.where(jnp.tril(jnp.ones((S, S), jnp.float32)) == 0, -1000000000.0, 0.0)
        scores = scores + causal
        attn = jax.nn.softmax(scores, axis=-1)
        out = jnp.einsum('bhqk,bhkd->bhqd', attn, v)
        out = out.transpose(0, 2, 1, 3).reshape(B, S, D_MODEL)
        return out @ wo + bo

    def _L0_ffn_ref(x, ln1_g, ln1_b, ln2_g, ln2_b, Wq, Wk, Wv, Wo, Wg, W1, b1, W2, b2):
        import jax, jax.numpy as jnp
        import numpy as np
        B, S, D, H, E, F, K = (2, 128, 128, 16, 8, 512, 2)
        EPS = 1e-05

        def _layernorm(x, g, b):
            mu = jnp.mean(x, axis=-1, keepdims=True)
            var = jnp.mean(jnp.square(x - mu), axis=-1, keepdims=True)
            return (x - mu) * jax.lax.rsqrt(var + EPS) * g + b
        Bb, Ss, Dd = x.shape
        Dh = Dd // H
        h = _layernorm(x, ln1_g, ln1_b)
        q = (h @ Wq).reshape(Bb, Ss, H, Dh)
        k = (h @ Wk).reshape(Bb, Ss, H, Dh)
        v = (h @ Wv).reshape(Bb, Ss, H, Dh)
        scores = jnp.einsum('bqhd,bkhd->bhqk', q, k) / jnp.sqrt(jnp.float32(Dh))
        attn = jax.nn.softmax(scores, axis=-1)
        ctx = jnp.einsum('bhqk,bkhd->bqhd', attn, v).reshape(Bb, Ss, Dd)
        x = x + ctx @ Wo
        m = _layernorm(x, ln2_g, ln2_b)
        xt = m.reshape(-1, Dd)
        T = xt.shape[0]
        probs = jax.nn.softmax(xt @ Wg, axis=-1)
        wts, idx = jax.lax.top_k(probs, K)
        wts = wts / jnp.sum(wts, axis=-1, keepdims=True)
        h1 = jax.nn.gelu(jnp.einsum('td,edf->etf', xt, W1) + b1[:, None, :])
        ye = jnp.einsum('etf,efd->etd', h1, W2) + b2[:, None, :]
        sel = ye[idx, jnp.arange(T)[:, None], :]
        moe_out = jnp.sum(wts[..., None] * sel, axis=1).reshape(Bb, Ss, Dd)
        return x + moe_out
    x = L0_attn_a_x
    x = x + _L0_attn_a_ref(_layernorm(x, axis=-1), L0_attn_a_Wq, L0_attn_a_Wk, L0_attn_a_Wv, L0_attn_a_Wo, L0_attn_a_proj, L0_attn_a_W1, L0_attn_a_b1, L0_attn_a_W2, L0_attn_a_b2, L0_attn_a_ln1_g, L0_attn_a_ln1_b, L0_attn_a_ln2_g, L0_attn_a_ln2_b)
    x = x + _L0_ffn_ref(_layernorm(x, axis=-1), L0_ffn_ln1_g, L0_ffn_ln1_b, L0_ffn_ln2_g, L0_ffn_ln2_b, L0_ffn_Wq, L0_ffn_Wk, L0_ffn_Wv, L0_ffn_Wo, L0_ffn_Wg, L0_ffn_W1, L0_ffn_b1, L0_ffn_W2, L0_ffn_b2)
    x = x + _L0_attn_b_ref(_layernorm(x, axis=-1), L0_attn_b_wq, L0_attn_b_bq, L0_attn_b_wk, L0_attn_b_bk, L0_attn_b_wv, L0_attn_b_bv, L0_attn_b_wo, L0_attn_b_bo)
    x = x + _L0_ffn_ref(_layernorm(x, axis=-1), L0_ffn_ln1_g, L0_ffn_ln1_b, L0_ffn_ln2_g, L0_ffn_ln2_b, L0_ffn_Wq, L0_ffn_Wk, L0_ffn_Wv, L0_ffn_Wo, L0_ffn_Wg, L0_ffn_W1, L0_ffn_b1, L0_ffn_W2, L0_ffn_b2)
    return x

_drawn_inputs = setup_inputs


def setup_inputs(seed=0):
    import zlib

    import numpy as np

    out = dict(_drawn_inputs(seed))
    spreads = {'L0_attn_a_b1': (0.0, 0.339),
     'L0_attn_a_b2': (0.0, 0.1),
     'L0_attn_a_ln1_g': (1.0, 0.2),
     'L0_attn_a_ln1_b': (0.0, 0.1),
     'L0_attn_a_ln2_g': (1.0, 0.2),
     'L0_attn_a_ln2_b': (0.0, 0.1),
     'L0_attn_b_bq': (0.0, 2.0),
     'L0_attn_b_bk': (0.0, 2.0),
     'L0_attn_b_bv': (0.0, 0.395),
     'L0_attn_b_bo': (0.0, 0.422),
     'L0_ffn_ln1_g': (1.0, 0.6),
     'L0_ffn_ln1_b': (0.0, 0.8),
     'L0_ffn_ln2_g': (1.0, 0.6),
     'L0_ffn_ln2_b': (0.0, 2.0),
     'L0_ffn_b1': (0.0, 0.8),
     'L0_ffn_b2': (0.0, 0.471)}
    factors = {'L0_attn_a_Wq': 64.0,
     'L0_attn_a_Wk': 64.0,
     'L0_attn_a_Wv': 8.0,
     'L0_attn_a_Wo': 8.0,
     'L0_attn_a_proj': 64.0,
     'L0_ffn_Wq': 8.0,
     'L0_ffn_Wk': 8.0,
     'L0_ffn_Wv': 8.0,
     'L0_ffn_Wo': 8.0,
     'L0_ffn_W1': 3.118}
    for name, (base, spread) in spreads.items():
        noise = np.random.default_rng([zlib.crc32(name.encode()), seed]).standard_normal(out[name].shape)
        drawn = base * np.exp(spread * noise) if base else spread * noise
        out[name] = jnp.asarray(drawn.astype(out[name].dtype))
    for name, factor in factors.items():
        out[name] = (out[name] * factor).astype(out[name].dtype)
    return out
```

```python
import math
from contextlib import ExitStack

import numpy as np
import concourse.bass as bass
from concourse import mybir

F32 = mybir.dt.float32
BF16 = mybir.dt.bfloat16
ALU = mybir.AluOpType
ACT = mybir.ActivationFunctionType
AX = mybir.AxisListType
RMAX = bass.bass_isa.ReduceOp.max

P = 128
BATCHES, SEQ = 8, 512
QT = SEQ // P
TILES = BATCHES * QT
HEADS = 16
PH, PD, PM = 16, 64, 64
CH = PH * PM // P
EPS_KERN = 1e-6
FF = 512
FC = FF // P
HD = P // HEADS
GROUPS = 4
GH = HEADS // GROUPS
STEPS = BATCHES * GROUPS
PARTS = 3
ROWS = HD * PARTS * PARTS
STACK = ROWS + PARTS
EPSILONS = (1e-5, 1e-6)
EXPERTS = 8


def at(eng, sem, value):
    if not isinstance(value, int) or value > 0:
        eng.wait_ge(sem, value)


class Store:

    def __init__(self, nc, ctx):
        self.nc, self.ctx, self.sems = nc, ctx, []

    def sb(self, name, shape, dt=F32):
        return self.ctx.enter_context(self.nc.sbuf_tensor(name, shape, dt))

    def sem(self, name):
        self.sems.append(self.nc.alloc_semaphore(name))
        return self.sems[-1]

    def clear(self):
        self.nc.clear_and_free_semaphores(self.sems)
        self.nc.all_engine_barrier()
        self.sems = []


def flat(ap):
    return ap.rearrange("p a c -> p (a c)")


def tile_of(buf, t):
    return flat(buf[:, bass.ds(t, 1), :])


def tiles_of(buf, b, n=QT):
    return buf[:, bass.ds(b * n, n), :]


class Norm:

    def __init__(self, st, c, name, eps):
        self.nc, self.eps, self.half = st.nc, c[f"eps{eps:g}"], c["half"]
        self.gate = st.sb(name + "_gate", [1, 1])
        self.var = st.sb(name + "_var", [P, QT])
        self.eps_done = st.sem(name + "_eps_done")
        self.stats = st.sb(name + "_stats", [P, QT, 6])
        self.mv = st.sb(name + "_mv", [P, QT, 2])
        self.rstd = st.sb(name + "_rstd", [P, QT])
        self.stats_done = st.sem(name + "_stats_done")
        self.var_done = st.sem(name + "_var_done")
        self.rstd_done = st.sem(name + "_rstd_done")

    def vector(self, dve, k, src, dst):
        nc = self.nc
        for i in range(QT):
            last = nc.vector.bn_stats(self.stats[:, i, :], src[i])
        last.then_inc(self.stats_done, 1)
        dve.wait_ge(self.stats_done, k + 1)
        nc.vector.tensor_copy(self.gate[:, :], self.half[0:1, 0:1])
        for i in range(QT):
            last = nc.vector.bn_aggr(self.mv[:, i, :], self.stats[:, i, :])
        last.then_inc(self.var_done, 1)
        dve.wait_ge(self.rstd_done, k + 1)
        dve.wait_ge(self.var_done, k + 1)
        for i in range(QT):
            last = nc.vector.tensor_scalar(dst[i], src[i], self.mv[:, i, 0:1], self.rstd[:, i:i + 1],
                                           ALU.subtract, ALU.mult)
        return last

    def pool(self, pool, k):
        pool.wait_ge(self.var_done, k + 1)
        self.nc.gpsimd.tensor_tensor(self.var[:, :], self.mv[:, :, 1], self.eps[:, :], ALU.add).then_inc(self.eps_done, 1)
        pool.wait_ge(self.eps_done, k + 1)
        self.nc.gpsimd.tensor_tensor(self.rstd[:, :], self.var[:, :], self.half[:, :], ALU.pow).then_inc(self.rstd_done, 1)


def build(nc, d, out, layers=3, probe=None):
    ctx = ExitStack()
    with ctx:
        st = Store(nc, ctx)
        ps = ctx.enter_context(nc.psum_tensor("ps", [P, 8, 512], F32))
        c = load_constants(nc, st, d)
        c["ps"] = ps
        x_res = st.sb("x_res", [P, TILES, P])
        y_all = st.sb("y_all", [P, TILES, P])
        load_x(nc, st, d, x_res)
        performer(nc, d, c, ps, x_res, y_all)
        with ExitStack() as rest:
            sm = Store(nc, rest)
            v_all = sm.sb("v_all", [P, TILES, P])
            ctx_all = sm.sb("ctx_all", [P, TILES, P])
            for layer in range(3):
                rope = layer == 1
                name = f"L{layer}"
                w = load_attention_weights(nc, d, c, name, rope, sm, layer)
                with ExitStack() as attention:
                    a = attention_memory(nc, Store(nc, attention), name)
                    attention_front(nc, name, rope, c, w, a, ps, x_res, y_all, v_all)
                    attention_main(nc, name, rope, c, a, ps, v_all, ctx_all)
                if rope:
                    attention_back(nc, name, c, w, ps, x_res, ctx_all)
                else:
                    experts(nc, name, d, c, w, ps, x_res, y_all, ctx_all, out if layer == 2 else None)


def load_constants(nc, st, d):
    c = {}
    c["ident"] = ident = st.sb("ident", [P, P])
    c["identb"] = identb = st.sb("identb", [P, P], BF16)
    c["ones"] = ones = st.sb("ones", [P, P])
    c["minus"] = st.sb("minus_one", [P, 1])
    for eps in EPSILONS:
        c[f"eps{eps:g}"] = st.sb(f"norm_eps{eps:g}", [P, QT])
    c["half"] = half = st.sb("minus_half", [P, QT])
    c["after_q"] = after_q = st.sb("after_q", [P, P], BF16)
    c["after_k"] = after_k = st.sb("after_k", [P, P], BF16)
    const_ready = st.sem("const_ready")
    with nc.Block() as block:
        @block.gpsimd
        def _(pool):
            g = nc.gpsimd
            g.memset(ident[:], 0.0).then_inc(const_ready, 1)
            g.memset(after_q[:], 0.0).then_inc(const_ready, 1)
            g.memset(after_k[:], 0.0).then_inc(const_ready, 1)
            g.memset(half[:], -0.5)
            g.memset(c["minus"][:], -1.0)
            for eps in EPSILONS:
                g.memset(c[f"eps{eps:g}"][:], eps)
            g.memset(ones[:], 1.0).then_inc(const_ready, 1)
            pool.wait_ge(const_ready, 4)
            g.affine_select(out=ident[:], in_=ident[:], compare_op=ALU.not_equal, fill=1.0, base=0,
                            pattern=[[-1, P]], channel_multiplier=1).then_inc(const_ready, 1)
            g.affine_select(out=after_q[:], in_=after_q[:], compare_op=ALU.is_ge, fill=-4e9, base=0,
                            pattern=[[-1, P]], channel_multiplier=1).then_inc(const_ready, 1)
            g.affine_select(out=after_k[:], in_=after_k[:], compare_op=ALU.is_ge, fill=-4e9, base=0,
                            pattern=[[1, P]], channel_multiplier=-1).then_inc(const_ready, 1)
            pool.wait_ge(const_ready, 7)
            g.tensor_copy(identb[:], ident[:]).then_inc(const_ready, 1)
    return c


def load_x(nc, st, d, x_res):
    x_loaded = st.sem("x_loaded")
    xv = d["L0_attn_a_x"].rearrange("b (n p) e -> p (b n) e", p=P)
    with nc.Block() as block:
        @block.sync
        def _(sp):
            for b in range(BATCHES):
                sp.dma_start(x_res[:, b * QT:(b + 1) * QT, :], xv[:, b * QT:(b + 1) * QT, :]).then_inc(x_loaded, 16)
            sp.wait_ge(x_loaded, 16 * BATCHES)


def performer(nc, d, c, ps, x_res, y_all):
    with ExitStack() as mem:
        st = Store(nc, mem)
        w = performer_weights(nc, st, d, c, ps)
        k = performer_keys(nc, st, c, w, ps, x_res, y_all)
        performer_queries(nc, st, c, w, k, ps, x_res, y_all)
        st.clear()


def performer_weights(nc, st, d, c, ps):
    w = {}
    wide = PH * PD
    w["wq"] = wq = st.sb("a_wq", [P, wide])
    w["wk"] = wk = st.sb("a_wk", [P, wide])
    w["wqp"] = wqp = st.sb("a_wqp", [P, wide])
    w["wkp"] = wkp = st.sb("a_wkp", [P, wide])
    w["wvo"] = wvo = st.sb("a_wvo", [P, PH, P])
    w["w1"] = w1 = st.sb("a_w1", [P, FF])
    w["w2"] = w2 = st.sb("a_w2", [P, FC, P])
    w["b1"] = b1 = st.sb("a_b1", [P, FC])
    w["eps"] = eps = st.sb("a_eps", [P, 1])
    w["mask"] = mask = st.sb("a_mask", [P, CH, 32])
    w["pick"] = pick = st.sb("a_pick", [P, CH, P])
    rows = {}
    for n in ("b2", "ln1_g", "ln1_b", "ln2_g", "ln2_b"):
        w[n] = rows[n] = st.sb("a_" + n, [P, P])
    with ExitStack() as temp:
        t = Store(nc, temp)
        wv = t.sb("a_wv", [P, wide])
        wo = t.sb("a_wo", [P, CH, P])
        wt = t.sb("a_wt", [P, 3, CH, P])
        projp = t.sb("a_projp", [P, P])
        projt = t.sb("a_projt", [P, P])
        loaded = st.sem("a_w_loaded")
        zeroed = st.sem("a_proj_zeroed")
        turned = st.sem("a_w_turned")
        copied = st.sem("a_w_copied")
        product = st.sem("a_w_product")
        n_loads = 15 + len(rows)
        with nc.Block() as block:
            @block.sync
            def _(sp):
                def load(dst, src):
                    sp.dma_start(dst, src).then_inc(loaded, 16)

                sp.wait_ge(zeroed, 1)
                for h in range(2):
                    load(projp[h * PM:(h + 1) * PM, h * PD:(h + 1) * PD], d["L0_attn_a_proj"])
                load(wq[:], d["L0_attn_a_Wq"].rearrange("e h k -> e (h k)"))
                load(wk[:], d["L0_attn_a_Wk"].rearrange("e h k -> e (h k)"))
                load(wv[:], d["L0_attn_a_Wv"].rearrange("e h k -> e (h k)"))
                load(wo[:], d["L0_attn_a_Wo"].rearrange("h k o -> (h k) o").rearrange("(c p) o -> p c o", p=P))
                load(w1[:], d["L0_attn_a_W1"])
                load(w2[:], d["L0_attn_a_W2"].rearrange("(c p) o -> p c o", p=P))
                for f in range(FC):
                    load(b1[:, f:f + 1], d["L0_attn_a_b1"][f * P:(f + 1) * P].rearrange("(p o) -> p o", o=1))
                load(mask[:], d["perf_mask"])
                load(pick[:, 0:CH // 2, :], d["perf_pick"][:, 0:CH // 2, :])
                load(pick[:, CH // 2:CH, :], d["perf_pick"][:, CH // 2:CH, :])
                for n, dst in rows.items():
                    load(dst[:], d["L0_attn_a_" + n].partition_broadcast(P))
                sp.wait_ge(loaded, 16 * n_loads)

            @block.gpsimd
            def _(pool):
                nc.gpsimd.memset(eps[:], EPS_KERN)
                nc.gpsimd.memset(projp[:], 0.0).then_inc(zeroed, 1)

            @block.tensor
            def _(pe):
                pe.wait_ge(loaded, 16 * n_loads)
                nc.tensor.transpose(ps[:, 0, 0:P], projp[:], c["ident"][:]).then_inc(turned, 1)
                for i, src in enumerate((wq, wk, wv)):
                    for j in range(CH):
                        last = nc.tensor.transpose(ps[:, 1 + 2 * i + j // 4, (j % 4) * P:(j % 4 + 1) * P],
                                                   src[:, j * P:(j + 1) * P], c["ident"][:])
                    last.then_inc(turned, 1)
                pe.wait_ge(copied, 4)
                for i in range(2):
                    for j in range(CH):
                        last = nc.tensor.matmul(ps[:, 2 * i + j // 4, (j % 4) * P:(j % 4 + 1) * P],
                                                wt[:, i, j, :], projt[:], start=True, stop=True)
                last.then_inc(product, 1)
                for half in range(2):
                    for j in range(CH):
                        last = nc.tensor.matmul(ps[:, 4 + 2 * half + j // 4, (j % 4) * P:(j % 4 + 1) * P],
                                                wt[half * PD:(half + 1) * PD, 2, j, :],
                                                wo[half * PD:(half + 1) * PD, j, :], start=True, stop=True)
                last.then_inc(product, 1)

            @block.vector
            def _(dve):
                dve.wait_ge(turned, 1)
                nc.vector.tensor_scalar(projt[:], ps[:, 0, 0:P], PD ** -0.25, None, ALU.mult).then_inc(copied, 1)
                for i in range(3):
                    dve.wait_ge(turned, 2 + i)
                    nc.vector.tensor_copy(wt[:, i, :, :].rearrange("p c e -> p (c e)"),
                                          ps[:, 1 + 2 * i:3 + 2 * i, :].rearrange("p a b -> p (a b)")).then_inc(copied, 1)
                dve.wait_ge(product, 2)
                for i, dst in enumerate((wqp, wkp)):
                    nc.vector.tensor_copy(dst[:], ps[:, 2 * i:2 * i + 2, :].rearrange("p a b -> p (a b)"))
                for half in range(2):
                    nc.vector.tensor_copy(wvo[:].rearrange("p (c two) o -> p two c o", two=2)[:, half, :, :],
                                          ps[:, 4 + 2 * half:6 + 2 * half, :].rearrange("p a (c o) -> p (a c) o", o=P))
    return w


def performer_keys(nc, st, c, w, ps, x_res, y_all):
    k = {}
    A = P + 1
    k["sums"] = sums = st.sb("a_sums", [P, BATCHES, CH * A])
    k["ysum"] = ysum = st.sb("a_ysum", [P, BATCHES, A])
    k["peak"] = peak = st.sb("a_peak", [P, BATCHES])
    temp = ExitStack()
    t = Store(nc, temp)
    ya = t.sb("k_ya", [P, 2, QT, A])
    yt = t.sb("k_yt", [P, 2, SEQ])
    sq = t.sb("k_sq", [P, 2, PH * PD])
    ssq = t.sb("k_ssq", [P, 2, PH])
    e = t.sb("k_e", [P, 2, QT, PH * PM])
    tmax = t.sb("k_tmax", [P, 2, QT])
    bmax = t.sb("k_bmax", [P, 2])
    gate = t.sb("k_gate", [1, 2])
    bpeak = t.sb("k_bpeak", [P, 2])
    nl = t.sb("k_nl", [P, 2])
    norm = Norm(t, c, "k_norm", 1e-5)
    y_ready = t.sem("k_y_ready")
    y_saved = t.sem("k_y_saved")
    yt_ps = t.sem("k_yt_in_psum")
    yt_ready = t.sem("k_yt_ready")
    k_ready = t.sem("k_k_in_psum")
    dd_ready = t.sem("k_dd_in_psum")
    sq_ready = t.sem("k_squares_ready")
    ssq_ready = t.sem("k_ssq_ready")
    max_done = t.sem("k_tile_max_done")
    e_ready = t.sem("k_exponent_ready")
    bmax_ready = t.sem("k_batch_max_ready")
    peak_ready = t.sem("k_batch_peak_ready")
    nl_ready = t.sem("k_neg_peak_ready")
    peak_saved = t.sem("k_peak_saved")
    exp_done = t.sem("k_exp_done")
    g_ready = t.sem("k_sums_in_psum")
    g_saved = t.sem("k_sums_saved")
    ones_set = t.sem("k_ones_set")

    with nc.Block() as block:
        @block.vector
        def _(dve):
            nc.vector.memset(ya[:, :, :, P:A], 1.0).then_inc(ones_set, 1)

            def normalise(b, par):
                at(dve, g_ready, b)
                at(dve, y_saved, b - 1)
                norm.vector(dve, b, [tile_of(x_res, b * QT + i) for i in range(QT)],
                            [ya[:, par, i, 0:P] for i in range(QT)]).then_inc(y_ready, 1)

            def batch(b, par, more):
                for i in range(QT):
                    n = b * QT + i
                    if i == 3 and more:
                        normalise(b + 1, 1 - par)
                    dve.wait_ge(dd_ready, n + 1)
                    nc.vector.tensor_reduce(tmax[:, par, i:i + 1], ps[:, 2:4, :].rearrange("p a b -> p (a b)"),
                                            AX.X, ALU.max).then_inc(max_done, 1)
                    dve.wait_ge(sq_ready, n + 1)
                    nc.vector.tensor_reduce(ssq[:, i % 2, :], sq[:, i % 2, :].rearrange("p (h k) -> p h k", h=PH),
                                            AX.X, ALU.add).then_inc(ssq_ready, 1)
                    dve.wait_ge(ssq_ready, n + 1)
                    if i == 0:
                        at(dve, g_ready, b)
                    nc.vector.scalar_tensor_tensor(
                        e[:, par, i, :].rearrange("p (h m) -> p h m", h=PH),
                        ssq[:, i % 2, :].rearrange("p (h o) -> p h o", o=1).to_broadcast([P, PH, PM]), -1.0 / 16,
                        ps[:, 2:4, :].rearrange("p a (h m) -> p (a h) m", m=PM), ALU.mult, ALU.add).then_inc(e_ready, 1)
                dve.wait_ge(max_done, b * QT + QT)
                nc.vector.reduce_max(bmax[:, par:par + 1], tmax[:, par, :], AX.X).then_inc(bmax_ready, 1)

            normalise(0, 0)
            batch(0, 0, True)
            with nc.vector.Fori(0, (BATCHES - 2) // 2) as u:
                for j in range(2):
                    batch(u * 2 + (1 + j), 1 - j, True)
            batch(BATCHES - 1, 1, False)

        @block.gpsimd
        def _(pool):
            def save_y(b, par):
                pool.wait_ge(y_ready, b + 1)
                nc.gpsimd.tensor_copy(tiles_of(y_all, b), ya[:, par, :, 0:P]).then_inc(y_saved, 1)

            def batch(b, par, more):
                if more:
                    norm.pool(pool, b + 1)
                    save_y(b + 1, 1 - par)
                pool.wait_ge(bmax_ready, b + 1)
                nc.gpsimd.tensor_tensor(gate[:, par:par + 1], c["minus"][0:1, :], c["minus"][0:1, :], ALU.mult)
                nc.gpsimd.partition_all_reduce(bpeak[:, par:par + 1], bmax[:, par:par + 1], P, RMAX).then_inc(peak_ready, 1)
                at(pool, exp_done, b)
                pool.wait_ge(peak_ready, b + 1)
                nc.gpsimd.tensor_tensor(nl[:, par:par + 1], bpeak[:, par:par + 1], c["minus"][:], ALU.mult).then_inc(nl_ready, 1)
                nc.gpsimd.tensor_copy(peak[:, bass.ds(b, 1)], bpeak[:, par:par + 1]).then_inc(peak_saved, 1)

            norm.pool(pool, 0)
            save_y(0, 0)
            batch(0, 0, True)
            with nc.gpsimd.Fori(0, (BATCHES - 2) // 2) as u:
                for j in range(2):
                    batch(u * 2 + (1 + j), 1 - j, True)
            batch(BATCHES - 1, 1, False)

        @block.scalar
        def _(act):
            def save_sums(b):
                act.wait_ge(g_ready, b + 2)
                flat_sums = flat(sums[:, bass.ds(b, 1), :])
                for i in range(3):
                    n = min(3, CH - 3 * i) * A
                    nc.scalar.copy(flat_sums[:, 3 * i * A:3 * i * A + n], ps[:, 4 + i, 0:n])
                nc.scalar.copy(flat(ysum[:, bass.ds(b, 1), :]), ps[:, 7, 0:A]).then_inc(g_saved, 1)

            def batch(b, par, before):
                act.wait_ge(yt_ps, b + 1)
                nc.scalar.copy(yt[:, par, :], ps[:, 7, :]).then_inc(yt_ready, 1)
                for i in range(QT):
                    n = b * QT + i
                    act.wait_ge(k_ready, n + 1)
                    at(act, ssq_ready, n - 1)
                    nc.scalar.activation(sq[:, i % 2, :], ps[:, 0:2, :].rearrange("p a b -> p (a b)"),
                                         ACT.Square).then_inc(sq_ready, 1)
                    if i == 1 and before:
                        save_sums(b - 1)
                act.wait_ge(nl_ready, b + 1)
                act.wait_ge(e_ready, b * QT + QT)
                whole = e[:, par, :, :].rearrange("p i f -> p (i f)")
                nc.scalar.activation(whole, whole, ACT.Exp, bias=nl[:, par:par + 1]).then_inc(exp_done, 1)

            act.sem_inc(exp_done, 1)
            act.sem_inc(g_saved, 1)
            batch(0, 0, False)
            with nc.scalar.Fori(0, (BATCHES - 2) // 2) as u:
                for j in range(2):
                    batch(u * 2 + (1 + j), 1 - j, True)
            batch(BATCHES - 1, 1, True)
            save_sums(BATCHES - 1)

        @block.tensor
        def _(pe):
            def add_up(b, par):
                pe.wait_ge(exp_done, b + 2)
                pe.wait_ge(y_ready, b + 1)
                pe.wait_ge(ones_set, 1)
                pe.wait_ge(g_saved, b + 1)
                for j in range(CH):
                    for i in range(QT):
                        nc.tensor.matmul(ps[:, 4 + j // 3, (j % 3) * A:(j % 3 + 1) * A],
                                         e[:, par, i, j * P:(j + 1) * P], ya[:, par, i, :],
                                         start=i == 0, stop=i == QT - 1)
                for i in range(QT):
                    last = nc.tensor.matmul(ps[:, 7, 0:A], c["ones"][:], ya[:, par, i, :],
                                            start=i == 0, stop=i == QT - 1)
                last.then_inc(g_ready, 1)

            def batch(b, par, before):
                pe.wait_ge(y_ready, b + 1)
                at(pe, g_saved, b)
                for i in range(QT):
                    last = nc.tensor.transpose(ps[:, 7, i * P:(i + 1) * P], ya[:, par, i, 0:P], c["ident"][:])
                last.then_inc(yt_ps, 1)
                pe.wait_ge(yt_ready, b + 1)
                for i in range(QT):
                    n = b * QT + i
                    tile = yt[:, par, i * P:(i + 1) * P]
                    at(pe, sq_ready, n)
                    for half in range(2):
                        last = nc.tensor.matmul(ps[:, half, :], tile, w["wk"][:, half * 512:(half + 1) * 512],
                                                start=True, stop=True)
                    last.then_inc(k_ready, 1)
                    at(pe, e_ready, n)
                    for half in range(2):
                        last = nc.tensor.matmul(ps[:, 2 + half, :], tile, w["wkp"][:, half * 512:(half + 1) * 512],
                                                start=True, stop=True)
                    last.then_inc(dd_ready, 1)
                    if i == 1 and before:
                        add_up(b - 1, 1 - par)

            pe.sem_inc(g_ready, 1)
            batch(0, 0, False)
            with nc.tensor.Fori(0, (BATCHES - 2) // 2) as u:
                for j in range(2):
                    batch(u * 2 + (1 + j), 1 - j, True)
            batch(BATCHES - 1, 1, True)
            add_up(BATCHES - 1, 1)
    t.clear()
    temp.close()
    return k


def performer_queries(nc, st, c, w, k, ps, x_res, y_all):
    A = P + 1
    sums, ysum, peak = k["sums"], k["ysum"], k["peak"]
    gmax = st.sb("q_gmax", [P, 1])
    shift = st.sb("q_shift", [P, BATCHES])
    y = st.sb("q_y", [P, QT, P])
    yt = st.sb("q_yt", [P, SEQ])
    es = st.sb("q_es", [P, A])
    gf = st.sb("q_gf", [P, CH, A])
    gt = st.sb("q_gt", [P, CH * P])
    ksd = st.sb("q_ksd", [P, CH, 32])
    pv = st.sb("q_pv", [P, CH, P])
    sq = st.sb("q_sq", [P, PH * PD])
    ssq = st.sb("q_ssq", [P, PH])
    mx = st.sb("q_mx", [P, PH])
    cc = st.sb("q_cc", [P, PH])
    e = st.sb("q_e", [P, 2, PH * PM])
    qf = st.sb("q_qf", [P, CH, SEQ])
    den = st.sb("q_den", [P, SEQ])
    rden = st.sb("q_rden", [P, SEQ])
    r1 = st.sb("q_r1", [P, QT, P])
    o1 = st.sb("q_o1", [P, QT, P])
    o1t = st.sb("q_o1t", [P, SEQ])
    pos = st.sb("q_pos", [P, 2, SEQ])
    neg = st.sb("q_neg", [P, 2, SEQ])
    ht = st.sb("q_ht", [P, FC, SEQ])
    f2 = st.sb("q_f2", [P, QT, P])
    norm = Norm(st, c, "q_norm", 1e-6)
    gmax_ready = st.sem("q_gmax_ready")
    gap_ready = st.sem("q_gap_ready")
    shift_ready = st.sem("q_shift_ready")
    y_ready = st.sem("q_y_ready")
    yt_ps = st.sem("q_yt_in_psum")
    yt_ready = st.sem("q_yt_ready")
    es_ready = st.sem("q_es_ready")
    gf_ready = st.sem("q_gf_ready")
    gt_ps = st.sem("q_gt_in_psum")
    gt_ready = st.sem("q_gt_ready")
    ksd_ready = st.sem("q_ksd_ready")
    pv_ps = st.sem("q_pv_in_psum")
    pv_ready = st.sem("q_pv_ready")
    q_ready = st.sem("q_q_in_psum")
    dd_ready = st.sem("q_dd_in_psum")
    sq_ready = st.sem("q_squares_ready")
    ssq_ready = st.sem("q_ssq_ready")
    mx_ready = st.sem("q_mx_ready")
    c_ready = st.sem("q_c_ready")
    e_ready = st.sem("q_e_ready")
    exp_done = st.sem("q_exp_done")
    turned = st.sem("q_features_in_psum")
    qf_ready = st.sem("q_features_ready")
    den_ps = st.sem("q_den_in_psum")
    den_ready = st.sem("q_den_ready")
    rden_ready = st.sem("q_rden_ready")
    spread = st.sem("q_rden_spread")
    scaled = st.sem("q_features_scaled")
    o_ps = st.sem("q_attention_in_psum")
    r1_ready = st.sem("q_r1_ready")
    n1_ready = st.sem("q_n1_ready")
    g1_ready = st.sem("q_g1_ready")
    o1_ready = st.sem("q_o1_ready")
    o1t_ps = st.sem("q_o1t_in_psum")
    o1t_ready = st.sem("q_o1t_ready")
    up_ps = st.sem("q_up_in_psum")
    neg_ready = st.sem("q_neg_ready")
    pos_ready = st.sem("q_pos_ready")
    elu_exp = st.sem("q_elu_exp_done")
    h_ready = st.sem("q_h_ready")
    down_ps = st.sem("q_down_in_psum")
    f_step = st.sem("q_f_step")
    x_done = st.sem("q_x_done")
    F_STEPS = 5

    with nc.Block() as block:
        @block.gpsimd
        def _(pool):
            with nc.gpsimd.Fori(0, BATCHES) as b:
                pool.wait_ge(r1_ready, b + 1)
                nc.gpsimd.tensor_copy(y[:], tiles_of(y_all, b)).then_inc(y_ready, 1)
                norm.pool(pool, b * 2)
                norm.pool(pool, b * 2 + 1)

        @block.vector
        def _(dve):
            nc.vector.reduce_max(gmax[:], peak[:], AX.X).then_inc(gmax_ready, 1)
            dve.wait_ge(gmax_ready, 1)
            nc.vector.tensor_scalar(shift[:], peak[:], gmax[:], None, ALU.subtract).then_inc(gap_ready, 1)
            dve.sem_inc(r1_ready, 1)
            dve.wait_ge(shift_ready, 1)
            with nc.vector.Fori(0, BATCHES) as b:
                nc.vector.tensor_scalar(es[:], flat(ysum[:, bass.ds(b, 1), :]), EPS_KERN, None,
                                        ALU.mult).then_inc(es_ready, 1)
                dve.wait_ge(es_ready, b + 1)
                nc.vector.scalar_tensor_tensor(
                    gf[:], sums[:, bass.ds(b, 1), :].rearrange("p a (c e) -> p (a c) e", c=CH),
                    shift[:, bass.ds(b, 1)], es[:].rearrange("p (o e) -> p o e", o=1).to_broadcast([P, CH, A]),
                    ALU.mult, ALU.add).then_inc(gf_ready, 1)
                dve.wait_ge(gf_ready, b + 1)
                nc.vector.tensor_tensor(ksd[:], w["mask"][:], gf[:, :, P:A].to_broadcast([P, CH, 32]),
                                        ALU.mult).then_inc(ksd_ready, 1)
                dve.wait_ge(gt_ps, b + 1)
                nc.vector.tensor_copy(gt[:], ps[:, 5:7, :].rearrange("p a b -> p (a b)")).then_inc(gt_ready, 1)
                dve.wait_ge(pv_ps, b + 1)
                nc.vector.tensor_copy(pv[:].rearrange("p c e -> p (c e)"),
                                      ps[:, 5:7, :].rearrange("p a b -> p (a b)")).then_inc(pv_ready, 1)
                for i in range(QT):
                    n = b * QT + i
                    dve.wait_ge(sq_ready, n + 1)
                    nc.vector.tensor_reduce(ssq[:], sq[:].rearrange("p (h k) -> p h k", h=PH),
                                            AX.X, ALU.add).then_inc(ssq_ready, 1)
                    dve.wait_ge(dd_ready, n + 1)
                    dd = ps[:, 2:4, :].rearrange("p a (h m) -> p (a h) m", m=PM)
                    nc.vector.tensor_reduce(mx[:], dd, AX.X, ALU.max).then_inc(mx_ready, 1)
                    dve.wait_ge(mx_ready, n + 1)
                    dve.wait_ge(ssq_ready, n + 1)
                    nc.vector.scalar_tensor_tensor(cc[:], ssq[:], 1.0 / 16, mx[:], ALU.mult, ALU.add).then_inc(c_ready, 1)
                    dve.wait_ge(c_ready, n + 1)
                    if i >= 2:
                        dve.wait_ge(turned, n - 1)
                    nc.vector.tensor_tensor(e[:, i % 2, :].rearrange("p (h m) -> p h m", h=PH), dd,
                                            cc[:].rearrange("p (h o) -> p h o", o=1).to_broadcast([P, PH, PM]),
                                            ALU.subtract).then_inc(e_ready, 1)
                dve.wait_ge(den_ready, b + 1)
                nc.vector.reciprocal(rden[:], den[:]).then_inc(rden_ready, 1)
                dve.wait_ge(qf_ready, b * QT + QT)
                for j in range(CH):
                    dve.wait_ge(spread, b * CH + (j + 1))
                    nc.vector.tensor_tensor(qf[:, j, :], qf[:, j, :], ps[:, j % 2, :], ALU.mult).then_inc(scaled, 1)
                dve.wait_ge(o_ps, b + 1)
                nc.vector.tensor_tensor(r1[:], y[:], ps[:, 4, :].rearrange("p (i e) -> p i e", i=QT), ALU.add).then_inc(r1_ready, 1)
                dve.wait_ge(r1_ready, b + 2)
                norm.vector(dve, b * 2, [r1[:, i, :] for i in range(QT)],
                            [r1[:, i, :] for i in range(QT)]).then_inc(n1_ready, 1)
                dve.wait_ge(n1_ready, b + 1)

                def wide_row(name):
                    return w[name][:].rearrange("p (o e) -> p o e", o=1).to_broadcast([P, QT, P])

                nc.vector.tensor_tensor(r1[:], r1[:], wide_row("ln1_g"), ALU.mult).then_inc(g1_ready, 1)
                dve.wait_ge(g1_ready, b + 1)
                nc.vector.tensor_tensor(o1[:], r1[:], wide_row("ln1_b"), ALU.add).then_inc(o1_ready, 1)
                for f in range(FC):
                    dve.wait_ge(up_ps, b * FC + (f + 1))
                    nc.vector.tensor_scalar(neg[:, f % 2, :], ps[:, 5 + f % 2, :], w["b1"][:, f:f + 1], 0.0,
                                            ALU.add, ALU.min).then_inc(neg_ready, 1)
                    dve.wait_ge(elu_exp, b * FC + (f + 1))
                    dve.wait_ge(pos_ready, b * FC + (f + 1))
                    nc.vector.scalar_tensor_tensor(ht[:, f, :], neg[:, f % 2, :], -1.0, pos[:, f % 2, :],
                                                   ALU.add, ALU.add).then_inc(h_ready, 1)
                dve.wait_ge(down_ps, b + 1)
                nc.vector.tensor_tensor(f2[:], ps[:, 4, :].rearrange("p (i e) -> p i e", i=QT), wide_row("b2"),
                                        ALU.add).then_inc(f_step, 1)
                dve.wait_ge(f_step, b * F_STEPS + 1)
                dve.wait_ge(o1_ready, b + 1)
                nc.vector.tensor_tensor(f2[:], f2[:], o1[:], ALU.add).then_inc(f_step, 1)
                dve.wait_ge(f_step, b * F_STEPS + 2)
                norm.vector(dve, b * 2 + 1, [f2[:, i, :] for i in range(QT)],
                            [f2[:, i, :] for i in range(QT)]).then_inc(f_step, 1)
                dve.wait_ge(f_step, b * F_STEPS + 3)
                nc.vector.tensor_tensor(f2[:], f2[:], wide_row("ln2_g"), ALU.mult).then_inc(f_step, 1)
                dve.wait_ge(f_step, b * F_STEPS + 4)
                nc.vector.tensor_tensor(f2[:], f2[:], wide_row("ln2_b"), ALU.add).then_inc(f_step, 1)
                dve.wait_ge(f_step, b * F_STEPS + 5)
                nc.vector.tensor_tensor(tiles_of(x_res, b), tiles_of(x_res, b), f2[:], ALU.add).then_inc(x_done, 1)

        @block.scalar
        def _(act):
            act.wait_ge(gap_ready, 1)
            nc.scalar.activation(shift[:], shift[:], ACT.Exp).then_inc(shift_ready, 1)
            with nc.scalar.Fori(0, BATCHES) as b:
                act.wait_ge(yt_ps, b + 1)
                nc.scalar.copy(yt[:], ps[:, 7, :]).then_inc(yt_ready, 1)

                def features(n, i):
                    act.wait_ge(turned, n + 1)
                    nc.scalar.activation(qf[:, :, i * P:(i + 1) * P], ps[:, 5:7, :].rearrange("p a (c e) -> p (a c) e", e=P),
                                         ACT.Identity, bias=w["eps"][:, 0:1]).then_inc(qf_ready, 1)

                for i in range(QT):
                    n = b * QT + i
                    act.wait_ge(q_ready, n + 1)
                    if i:
                        act.wait_ge(ssq_ready, n)
                    nc.scalar.activation(sq[:], ps[:, 0:2, :].rearrange("p a b -> p (a b)"), ACT.Square).then_inc(sq_ready, 1)
                    act.wait_ge(e_ready, n + 1)
                    nc.scalar.activation(e[:, i % 2, :], e[:, i % 2, :], ACT.Exp).then_inc(exp_done, 1)
                    if i:
                        features(n - 1, i - 1)
                features(b * QT + QT - 1, QT - 1)
                act.wait_ge(den_ps, b + 1)
                nc.scalar.copy(den[:], ps[:, 4, :]).then_inc(den_ready, 1)
                act.wait_ge(o1t_ps, b + 1)
                nc.scalar.copy(o1t[:], ps[:, 7, :]).then_inc(o1t_ready, 1)
                for f in range(FC):
                    n = b * FC + f
                    act.wait_ge(neg_ready, n + 1)
                    nc.scalar.activation(pos[:, f % 2, :], ps[:, 5 + f % 2, :], ACT.Relu, bias=w["b1"][:, f:f + 1]).then_inc(pos_ready, 1)
                    nc.scalar.activation(neg[:, f % 2, :], neg[:, f % 2, :], ACT.Exp).then_inc(elu_exp, 1)

        @block.tensor
        def _(pe):
            with nc.tensor.Fori(0, BATCHES) as b:
                pe.wait_ge(y_ready, b + 1)
                for i in range(QT):
                    last = nc.tensor.transpose(ps[:, 7, i * P:(i + 1) * P], y[:, i, :], c["ident"][:])
                last.then_inc(yt_ps, 1)
                pe.wait_ge(gf_ready, b + 1)
                for j in range(CH):
                    last = nc.tensor.transpose(ps[:, 5 + j // 4, (j % 4) * P:(j % 4 + 1) * P], gf[:, j, 0:P], c["ident"][:])
                last.then_inc(gt_ps, 1)
                pe.wait_ge(gt_ready, b + 1)
                for h in range(PH):
                    r, j = (h % 2) * PM, h // 2
                    last = nc.tensor.matmul(ps[r:r + PM, 5 + j // 4, (j % 4) * P:(j % 4 + 1) * P],
                                            gt[:, h * PM:(h + 1) * PM], w["wvo"][:, h, :], start=True, stop=True)
                last.then_inc(pv_ps, 1)

                def turn(n, i):
                    pe.wait_ge(exp_done, n + 1)
                    if i:
                        pe.wait_ge(qf_ready, n)
                    for j in range(CH):
                        last = nc.tensor.transpose(ps[:, 5 + j // 4, (j % 4) * P:(j % 4 + 1) * P],
                                                   e[:, i % 2, j * P:(j + 1) * P], c["ident"][:])
                    last.then_inc(turned, 1)

                pe.wait_ge(yt_ready, b + 1)
                for i in range(QT):
                    n = b * QT + i
                    tile = yt[:, i * P:(i + 1) * P]
                    if i:
                        pe.wait_ge(sq_ready, n)
                    for half in range(2):
                        last = nc.tensor.matmul(ps[:, half, :], tile, w["wq"][:, half * 512:(half + 1) * 512],
                                                start=True, stop=True)
                    last.then_inc(q_ready, 1)
                    if i:
                        pe.wait_ge(e_ready, n)
                    for half in range(2):
                        last = nc.tensor.matmul(ps[:, 2 + half, :], tile, w["wqp"][:, half * 512:(half + 1) * 512],
                                                start=True, stop=True)
                    last.then_inc(dd_ready, 1)
                    if i == 0:
                        pe.wait_ge(pv_ready, b + 1)
                    else:
                        turn(n - 1, i - 1)
                turn(b * QT + QT - 1, QT - 1)
                pe.wait_ge(qf_ready, b * QT + QT)
                pe.wait_ge(ksd_ready, b + 1)
                for j in range(CH):
                    g = j % 4
                    last = nc.tensor.matmul(ps[32 * g:32 * g + 32, 4, :], ksd[:, j, :], qf[:, j, :],
                                            start=j < 4, stop=j >= 4)
                last.then_inc(den_ps, 1)
                pe.wait_ge(rden_ready, b + 1)
                for j in range(CH):
                    if j >= 2:
                        pe.wait_ge(scaled, b * CH + (j - 1))
                    nc.tensor.matmul(ps[:, j % 2, :], w["pick"][:, j, :], rden[:], start=True, stop=True).then_inc(spread, 1)
                pe.wait_ge(scaled, b * CH + CH)
                pe.wait_ge(pv_ready, b + 1)
                pe.wait_ge(den_ready, b + 1)
                for i in range(QT):
                    for j in range(CH):
                        last = nc.tensor.matmul(ps[:, 4, i * P:(i + 1) * P], qf[:, j, i * P:(i + 1) * P], pv[:, j, :],
                                                start=j == 0, stop=j == CH - 1)
                last.then_inc(o_ps, 1)
                pe.wait_ge(o1_ready, b + 1)
                for i in range(QT):
                    last = nc.tensor.transpose(ps[:, 7, i * P:(i + 1) * P], o1[:, i, :], c["ident"][:])
                last.then_inc(o1t_ps, 1)
                pe.wait_ge(o1t_ready, b + 1)
                for f in range(FC):
                    if f >= 2:
                        pe.wait_ge(pos_ready, b * FC + (f - 1))
                    nc.tensor.matmul(ps[:, 5 + f % 2, :], w["w1"][:, f * P:(f + 1) * P], o1t[:], start=True, stop=True).then_inc(up_ps, 1)
                pe.wait_ge(h_ready, b * FC + FC)
                pe.wait_ge(r1_ready, b + 2)
                for i in range(QT):
                    for f in range(FC):
                        last = nc.tensor.matmul(ps[:, 4, i * P:(i + 1) * P], ht[:, f, i * P:(i + 1) * P], w["w2"][:, f, :],
                                                start=f == 0, stop=f == FC - 1)
                last.then_inc(down_ps, 1)
                pe.wait_ge(x_done, b + 1)


def attention_memory(nc, st, name):
    a = {}
    a["q_dram"] = nc.dram_tensor(name + "_q_stacks", [BATCHES, P, PARTS, PARTS, SEQ], BF16, kind="Internal").ap()
    a["k_dram"] = nc.dram_tensor(name + "_k_stacks", [BATCHES, P, PARTS, PARTS, SEQ], BF16, kind="Internal").ap()
    a["qs"] = st.sb(name + "_q_stack", [P, GROUPS, GH, SEQ], BF16)
    a["ks"] = st.sb(name + "_k_stack", [P, GROUPS, GH, SEQ], BF16)
    a["vs"] = st.sb(name + "_v_stack", [P, GROUPS, QT, GH, 32])
    a["pt"] = st.sb(name + "_probs_t", [P, 4, 2, SEQ])
    a["ot"] = st.sb(name + "_out_t", [P, SEQ])
    a["mx"] = st.sb(name + "_row_max", [P, 2, GH * QT])
    a["mp"] = st.sb(name + "_max_parts", [GH * QT, 2, PARTS, P], BF16)
    a["mr"] = st.sb(name + "_max_rest", [GH * QT, P])
    a["rec"] = st.sb(name + "_recip_sum", [P, QT, GH, 1])
    a["y"] = st.sb(name + "_front_y", [P, QT, P])
    a["z"] = st.sb(name + "_front_z", [P, QT, P])
    a["ht"] = st.sb(name + "_front_ht", [P, SEQ])
    a["full"] = st.sb(name + "_front_qk", [P, 2, SEQ])
    a["rest"] = st.sb(name + "_front_rest", [P, 2, SEQ])
    a["parts"] = st.sb(name + "_front_parts", [P, 2, PARTS, SEQ], BF16)
    constants = st.sem(name + "_stack_constants")
    with nc.Block() as block:
        @block.vector
        def _(dve):
            nc.vector.memset(a["ks"][64:P, :, :, :], 1.0)
            nc.vector.memset(a["vs"][:], 0.0).then_inc(constants, 1)
            dve.wait_ge(constants, 1)
            nc.vector.memset(a["vs"][:, :, :, :, HD:HD + 1], 1.0)
    return a


def load_attention_weights(nc, d, c, name, rope, st, layer):
    if layer == 2:
        return c["ffn"]
    w = {}
    pre = "L0_attn_b_w" if rope else "L0_ffn_W"
    loads = []

    def add(key, shape, src):
        w[key] = st.sb(f"{name}_{key}", shape)
        loads.append((w[key], src))

    def column(v):
        return v.rearrange("(p o) -> p o", o=1)

    for n in "qkvo":
        add("w" + n, [P, P], d[pre + n])
    if rope:
        add("cos", [P, SEQ], d["rope_cos"])
        add("sin", [P, SEQ], d["rope_sin"])
        add("bq", [P, 1], column(d["L0_attn_b_bq"]))
        add("bk", [P, 1], column(d["L0_attn_b_bk"]))
        add("bv", [P, P], d["L0_attn_b_bv"].partition_broadcast(P))
        add("bo", [P, P], d["L0_attn_b_bo"].partition_broadcast(P))
        for n in "qk":
            w["w" + n + "s"] = st.sb(f"{name}_w{n}s", [P, P])
            w["b" + n + "s"] = st.sb(f"{name}_b{n}s", [P, 1])
    else:
        for n in ("ln1_g", "ln1_b", "ln2_g", "ln2_b"):
            add(n, [P, 1], column(d["L0_ffn_" + n]))
        add("wg", [P, EXPERTS], d["L0_ffn_Wg"])
        add("w1", [P, EXPERTS, FF], d["L0_ffn_W1"].rearrange("e p f -> p e f"))
        add("w2", [P, EXPERTS * FC, P], d["L0_ffn_W2"].rearrange("e (c p) o -> p (e c) o", p=P))
        add("b2", [EXPERTS, P], d["L0_ffn_b2"])
        add("b1r", [EXPERTS * FC, P], d["L0_ffn_b1"].rearrange("e (c p) -> (e c) p", p=P))
        add("rev", [P, QT, EXPERTS], d["expert_rank"])
        w["b1"] = st.sb(f"{name}_b1", [P, EXPERTS * FC])
        c["ffn"] = w
    loaded = st.sem(name + "_w_loaded")
    turned = st.sem(name + "_b1_turned")
    n_loads = len(loads) + (4 if rope else 0)
    ps = st.ctx.enter_context(ExitStack())
    with nc.Block() as block:
        @block.sync
        def _(sp):
            for dst, src in loads:
                sp.dma_start(dst[:], src).then_inc(loaded, 16)
            if rope:
                for n in "qk":
                    pairs = d["L0_attn_b_b" + n].rearrange("(a two o) -> a two o", two=2, o=1)
                    dst = w["b" + n + "s"]
                    for half in range(2):
                        sp.dma_start(dst[half:P:2, :], pairs[:, 1 - half, :], allow_slow_non_contiguous=True).then_inc(loaded, 16)
            sp.wait_ge(loaded, 16 * n_loads)

        if rope:
            @block.vector
            def _(dve):
                dve.wait_ge(loaded, 16 * n_loads)
                for n in "qk":
                    src = w["w" + n][:].rearrange("p (a two) -> p a two", two=2)
                    dst = w["w" + n + "s"][:].rearrange("p (a two) -> p a two", two=2)
                    for half in range(2):
                        nc.vector.tensor_copy(dst[:, :, half], src[:, :, 1 - half])
        else:
            @block.tensor
            def _(pe):
                pe.wait_ge(loaded, 16 * n_loads)
                nc.tensor.transpose(c["ps"][:, 0, 0:EXPERTS * FC], w["b1r"][:], c["ident"][0:EXPERTS * FC, 0:EXPERTS * FC]).then_inc(turned, 1)

            @block.vector
            def _(dve):
                dve.wait_ge(turned, 1)
                nc.vector.tensor_copy(w["b1"][:], c["ps"][:, 0, 0:EXPERTS * FC])
    return w


def attention_front(nc, name, rope, c, w, a, ps, x_res, y_all, v_all):
    mem = ExitStack()
    st = Store(nc, mem)
    name += "f_"
    norm = Norm(st, c, name + "norm", 1e-5)
    norms = 1 if rope else 2
    y, z, ht, full, rest, parts = (a[n] for n in ("y", "z", "ht", "full", "rest", "parts"))
    if rope:
        z = y
    y_ready = st.sem(name + "y_ready")
    y_saved = st.sem(name + "y_saved")
    z_ready = st.sem(name + "z_ready")
    zt_ps = st.sem(name + "zt_in_psum")
    ht_ready = st.sem(name + "ht_ready")
    qk_ps = st.sem(name + "qk_in_psum")
    v_ps = st.sem(name + "v_in_psum")
    v_saved = st.sem(name + "v_saved")
    full_ready = st.sem(name + "qk_ready")
    turn_step = st.sem(name + "rope_step")
    part1 = st.sem(name + "part1_ready")
    rest_ready = st.sem(name + "rest_ready")
    part2 = st.sem(name + "part2_ready")
    part3 = st.sem(name + "part3_ready")
    sent = st.sem(name + "stacks_sent")
    SENDS = 2 * PARTS

    with nc.Block() as block:
        @block.vector
        def _(dve):
            def normalise(b, first=False):
                if not first:
                    if not rope:
                        dve.wait_ge(y_saved, b)
                    dve.wait_ge(zt_ps, b)
                ys = [y[:, i, :] for i in range(QT)]
                norm.vector(dve, b * norms, [tile_of(x_res, b * QT + i) for i in range(QT)],
                            ys).then_inc(z_ready if rope else y_ready, 1)
                if not rope:
                    dve.wait_ge(y_ready, b + 1)
                    norm.vector(dve, b * 2 + 1, ys, [z[:, i, :] for i in range(QT)]).then_inc(z_ready, 1)

            def split(b):
                if rope:
                    dve.wait_ge(qk_ps, b + 1)
                    for x in range(2):
                        bias, other = w["bq" if x == 0 else "bk"], w["bqs" if x == 0 else "bks"]
                        nc.vector.scalar_tensor_tensor(full[:, x, :], ps[:, 1 + x, :], bias[:, 0:1], w["cos"][:],
                                                       ALU.add, ALU.mult)
                        nc.vector.scalar_tensor_tensor(rest[:, x, :], ps[:, 4 + x, :], other[:, 0:1], w["sin"][:],
                                                       ALU.add, ALU.mult).then_inc(turn_step, 1)
                        dve.wait_ge(turn_step, b * 2 + (x + 1))
                        nc.vector.tensor_tensor(full[:, x, :], full[:, x, :], rest[:, x, :], ALU.add).then_inc(full_ready, 1)
                    dve.wait_ge(v_ps, b + 1)
                    nc.vector.tensor_tensor(tiles_of(v_all, b), ps[:, 3, :].rearrange("p (i e) -> p i e", i=QT),
                                            w["bv"][:].rearrange("p (o e) -> p o e", o=1).to_broadcast([P, QT, P]),
                                            ALU.add).then_inc(v_saved, 1)
                    dve.wait_ge(full_ready, b * 2 + 3)
                for x in range(2):
                    dve.wait_ge(part1, b * 2 + (x + 1))
                    nc.vector.tensor_tensor(rest[:, x, :], full[:, x, :], parts[:, x, 0, :], ALU.subtract).then_inc(rest_ready, 1)
                for x in range(2):
                    dve.wait_ge(part2, b * 2 + (x + 1))
                    nc.vector.tensor_tensor(parts[:, x, 2, :], rest[:, x, :], parts[:, x, 1, :], ALU.subtract).then_inc(part3, 1)
                dve.wait_ge(part3, b * 2 + 2)

            if rope:
                dve.sem_inc(full_ready, 1)
                dve.sem_inc(v_saved, 1)
            normalise(0, True)
            with nc.vector.Fori(0, BATCHES - 1) as b:
                normalise(b + 1)
                split(b)
            split(BATCHES - 1)

        @block.gpsimd
        def _(pool):
            def rstd(b):
                for i in range(norms):
                    norm.pool(pool, b * norms + i)
                    if i == 0 and not rope:
                        pool.wait_ge(y_ready, b + 1)
                        nc.gpsimd.tensor_copy(tiles_of(y_all, b), y[:]).then_inc(y_saved, 1)

            with nc.gpsimd.Fori(0, BATCHES) as b:
                rstd(b)

        @block.scalar
        def _(act):
            if not rope:
                act.sem_inc(full_ready, 1)
                act.sem_inc(v_saved, 1)
            with nc.scalar.Fori(0, BATCHES) as b:
                act.wait_ge(zt_ps, b + 1)
                if rope:
                    nc.scalar.copy(ht[:], ps[:, 0, :]).then_inc(ht_ready, 1)
                else:
                    nc.scalar.activation(ht[:], ps[:, 0, :], ACT.Identity, bias=w["ln1_b"][:, 0:1],
                                         scale=w["ln1_g"][:, 0:1]).then_inc(ht_ready, 1)
                    act.wait_ge(qk_ps, b + 1)
                    act.wait_ge(sent, b * (16 * SENDS) + 1)
                    for x in range(2):
                        nc.scalar.copy(full[:, x, :], ps[:, 1 + x, :]).then_inc(full_ready, 1)
                    act.wait_ge(v_ps, b + 1)
                    nc.scalar.copy(tiles_of(v_all, b), ps[:, 3, :].rearrange("p (i e) -> p i e", i=QT)).then_inc(v_saved, 1)
                act.wait_ge(sent, b * (16 * SENDS) + 1)
                for x in range(2):
                    act.wait_ge(full_ready, b * 2 + (x + 2))
                    nc.scalar.copy(parts[:, x, 0, :], full[:, x, :]).then_inc(part1, 1)
                for x in range(2):
                    act.wait_ge(rest_ready, b * 2 + (x + 1))
                    nc.scalar.copy(parts[:, x, 1, :], rest[:, x, :]).then_inc(part2, 1)

        @block.tensor
        def _(pe):
            with nc.tensor.Fori(0, BATCHES) as b:
                pe.wait_ge(z_ready, b + 1)
                for i in range(QT):
                    last = nc.tensor.transpose(ps[:, 0, i * P:(i + 1) * P], z[:, i, :], c["ident"][:])
                last.then_inc(zt_ps, 1)
                pe.wait_ge(ht_ready, b + 1)
                pe.wait_ge(full_ready, b * 2 + 1)
                for x, m in enumerate(("wq", "wk")):
                    last = nc.tensor.matmul(ps[:, 1 + x, :], w[m][:], ht[:], start=True, stop=True)
                    if rope:
                        last = nc.tensor.matmul(ps[:, 4 + x, :], w[m + "s"][:], ht[:], start=True, stop=True)
                last.then_inc(qk_ps, 1)
                pe.wait_ge(v_saved, b + 1)
                for i in range(QT):
                    last = nc.tensor.matmul(ps[:, 3, i * P:(i + 1) * P], ht[:, i * P:(i + 1) * P], w["wv"][:],
                                            start=True, stop=True)
                last.then_inc(v_ps, 1)

        @block.sync
        def _(sp):
            sp.sem_inc(sent, 1)
            with nc.sync.Fori(0, BATCHES) as b:
                sp.wait_ge(part1, b * 2 + 2)
                sp.wait_ge(part2, b * 2 + 2)
                sp.wait_ge(part3, b * 2 + 2)
                for j in range(PARTS):
                    sp.dma_start(a["q_dram"][bass.ds(b, 1), :, :, j, :].rearrange("a r i t -> (a r) i t"),
                                 parts[:, 0, :, :]).then_inc(sent, 16)
                    sp.dma_start(a["k_dram"][bass.ds(b, 1), :, j, :, :].rearrange("a r i t -> (a r) i t"),
                                 parts[:, 1, :, :]).then_inc(sent, 16)
            sp.wait_ge(sent, 16 * SENDS * BATCHES + 1)
    st.clear()
    mem.close()


def attention_main(nc, name, causal, c, a, ps, v_all, ctx_all):
    st = Store(nc, ExitStack())
    name += "m_"
    qs, ks, vs, pt, ot, mx, mp, mr, rec = (a[n] for n in ("qs", "ks", "vs", "pt", "ot", "mx", "mp", "mr", "rec"))
    UNITS = 2 * QT
    MAXES = GH * QT
    OUT_BANK, MISC = 6, 7
    scale = HD ** -0.5
    loaded = [st.sem(f"{name}stacks_loaded{g}") for g in range(GROUPS)]
    m_loaded = [st.sem(f"{name}max_loaded{g}") for g in range(GROUPS)]
    s_ready = st.sem(name + "scores_ready")
    max_done = st.sem(name + "max_done")
    mt_ready = st.sem(name + "max_transposed")
    m_step = st.sem(name + "max_split_step")
    m_split = st.sem(name + "max_split")
    st_ready = st.sem(name + "scores_t_ready")
    exp_done = st.sem(name + "exp_done")
    vs_ready = st.sem(name + "v_ready")
    pv_done = st.sem(name + "pv_done")
    ot_ready = st.sem(name + "out_copied")
    ott_ready = st.sem(name + "out_transposed")
    rec_ready = st.sem(name + "recip_ready")
    ctx_done = st.sem(name + "ctx_done")

    def keys(i):
        return (i + 1) * P if causal else SEQ

    def first_query(kt):
        return kt * P if causal else 0

    def steps(eng, step):
        step(0, 0)
        with eng.Fori(0, BATCHES - 1) as b:
            for g in range(GROUPS):
                step(b * GROUPS + (g + 1), (g + 1) % GROUPS)
        for t in range(STEPS - 3, STEPS):
            step(t, t % GROUPS)

    def has(t, ahead):
        return not isinstance(t, int) or 0 <= t + ahead < STEPS

    with nc.Block() as block:
        @block.sync
        def _(sp):
            def load(b, g):
                for stack, dram in ((qs, a["q_dram"]), (ks, a["k_dram"])):
                    src = dram[bass.ds(b, 1), g * GH * HD:(g + 1) * GH * HD, :, :, :].rearrange(
                        "a (h e) i j t -> (a e i j) h t", h=GH)
                    sp.dma_start(stack[0:ROWS, g, :, :], src).then_inc(loaded[g], 16)

            def send_max(s, g):
                sp.wait_ge(m_split, s + 1)
                for i in range(PARTS):
                    sp.dma_start(qs[ROWS + i:ROWS + i + 1, g, :, :].rearrange("p h (i q) -> p (h i) q", i=QT),
                                 mp[:, g % 2, i, :]).then_inc(m_loaded[g], 16)

            for g in range(GROUPS):
                load(0, g)
            send_max(0, 0)
            with nc.sync.Fori(0, BATCHES - 1) as b:
                for g in range(GROUPS):
                    t = b * GROUPS + g
                    send_max(t + 1, (g + 1) % GROUPS)
                    sp.wait_ge(st_ready, (t + 1) * UNITS)
                    load(b + 1, g)
            for t in range(STEPS - GROUPS, STEPS - 1):
                send_max(t + 1, (t + 1) % GROUPS)
            for g in range(GROUPS):
                sp.wait_ge(m_loaded[g], 16 * PARTS * BATCHES)

        @block.gpsimd
        def _(pool):
            def v_stack(b, g, wait):
                if wait:
                    pool.wait_ge(pv_done, (b * GROUPS + (g - GROUPS + 1)) * QT)
                last = nc.gpsimd.tensor_copy(
                    vs[:, g, :, :, 0:HD],
                    tiles_of(v_all, b)[:, :, g * GH * HD:(g + 1) * GH * HD].rearrange("p i (h e) -> p i h e", h=GH))
                last.then_inc(vs_ready, 1)

            for g in range(GROUPS):
                v_stack(0, g, False)
            with nc.gpsimd.Fori(0, BATCHES - 1) as b:
                for g in range(GROUPS):
                    v_stack(b + 1, g, True)

        @block.vector
        def _(dve):
            def maxima(s, g, u):
                i, h = u // GH, u % GH
                dve.wait_ge(s_ready, s * MAXES + (u + 1))
                if u == 0:
                    at(dve, mt_ready, s - 1)
                nc.vector.reduce_max(mx[:, g % 2, h * QT + i:h * QT + i + 1], ps[:, u % 2, 0:keys(i)], AX.X).then_inc(max_done, 1)

            def split_max(s, g):
                if not isinstance(s, int) or s >= 2:
                    g2 = (g - 2) % GROUPS
                    dve.wait_ge(m_loaded[g2], sent_before(s, g))
                dve.wait_ge(mt_ready, s + 1)
                m = ps[0:MAXES, MISC, 0:P]
                p1, p2, p3 = (mp[:, g % 2, i, :] for i in range(PARTS))
                nc.vector.tensor_scalar(p1, m, -1.0, None, ALU.mult).then_inc(m_step, 1)
                dve.wait_ge(m_step, s * 3 + 1)
                nc.vector.scalar_tensor_tensor(mr[:], m, -1.0, p1, ALU.mult, ALU.subtract).then_inc(m_step, 1)
                dve.wait_ge(m_step, s * 3 + 2)
                nc.vector.tensor_copy(p2, mr[:]).then_inc(m_step, 1)
                dve.wait_ge(m_step, s * 3 + 3)
                nc.vector.tensor_tensor(p3, mr[:], p2, ALU.subtract).then_inc(m_split, 1)

            def sent_before(s, g):
                if isinstance(s, int):
                    return 16 * PARTS * ((s - 2) // GROUPS + 1)
                return (s - (2 + (g - 2) % GROUPS)) * (16 * PARTS // GROUPS) + 16 * PARTS

            def context(t, g):
                dve.wait_ge(ott_ready, t + 2)
                o = ps[:, MISC, :].rearrange("p (i h e) -> p i h e", i=QT, h=GH)
                nc.vector.reciprocal(rec[:], o[:, :, :, HD:HD + 1]).then_inc(rec_ready, 1)
                dve.wait_ge(rec_ready, t + 1)
                dst = ctx_all[:, bass.ds(t - g, QT), g * GH * HD:(g + 1) * GH * HD].rearrange("p i (h e) -> p i h e", h=GH)
                nc.vector.tensor_tensor(dst, o[:, :, :, 0:HD], rec[:].to_broadcast([P, QT, GH, HD]), ALU.mult).then_inc(ctx_done, 1)

            def step(t, g):
                for u in range(UNITS):
                    if has(t, 2):
                        for n in range(2):
                            maxima(t + 2, (g + 2) % GROUPS, 2 * u + n)
                    if u == 0 and has(t, 1):
                        split_max(t + 1, (g + 1) % GROUPS)
                    if u == 4 and has(t, -1):
                        context(t - 1, (g - 1) % GROUPS)

            dve.sem_inc(ctx_done, 1)
            for u in range(MAXES):
                maxima(0, 0, u)
            split_max(0, 0)
            for u in range(MAXES):
                maxima(1, 1, u)
            steps(nc.vector, step)
            context(STEPS - 1, GROUPS - 1)

        @block.scalar
        def _(act):
            def exponential(t, g, u):
                kt, q0 = u // 2, first_query(u // 2)
                act.wait_ge(st_ready, t * UNITS + (u + 1))
                at(act, pv_done, t * QT + (kt - 1))
                nc.scalar.activation(pt[:, u % 4, :, q0:SEQ], ps[:, 2 + 2 * (u % 2):4 + 2 * (u % 2), q0:SEQ],
                                     ACT.Exp, scale=scale).then_inc(exp_done, 1)

            def copy_out(t):
                act.wait_ge(pv_done, (t + 1) * QT)
                act.wait_ge(ott_ready, t + 1)
                nc.scalar.copy(ot[:], ps[:, OUT_BANK, :]).then_inc(ot_ready, 1)

            def step(t, g):
                for u in range(UNITS):
                    exponential(t, g, u)
                    if u == 1 and has(t, -1):
                        copy_out(t - 1)

            steps(nc.scalar, step)
            copy_out(STEPS - 1)

        @block.tensor
        def _(pe):
            def first_pass(s, g, u, b_count):
                i, h = u // GH, u % GH
                if u == 0:
                    pe.wait_ge(loaded[g], b_count * 32)
                at(pe, max_done, s * MAXES + (u - 1))
                q = qs[0:ROWS, g, h, i * P:(i + 1) * P]
                last = nc.tensor.matmul(ps[:, u % 2, 0:keys(i)], q, ks[0:ROWS, g, h, 0:keys(i)],
                                        start=True, stop=not causal)
                if causal:
                    last = nc.tensor.matmul(ps[:, u % 2, i * P:(i + 1) * P], c["identb"][:], c["after_q"][:],
                                            start=False, stop=True)
                last.then_inc(s_ready, 1)

            def turn_max(s, g):
                pe.wait_ge(max_done, (s + 1) * MAXES)
                at(pe, ctx_done, s - 1)
                nc.tensor.transpose(ps[0:MAXES, MISC, 0:P], mx[:, g % 2, :], c["ident"][:]).then_inc(mt_ready, 1)

            def second_pass(t, g, u, b_count):
                kt, q0 = u // 2, first_query(u // 2)
                if u == 0:
                    pe.wait_ge(m_loaded[g], b_count * (16 * PARTS))
                at(pe, exp_done, t * UNITS + (u - 1))
                for n in range(2):
                    h = 2 * (u % 2) + n
                    bank = 2 + 2 * (u % 2) + n
                    last = nc.tensor.matmul(ps[:, bank, q0:SEQ], ks[0:STACK, g, h, kt * P:(kt + 1) * P],
                                            qs[0:STACK, g, h, q0:SEQ], start=True, stop=not causal)
                    if causal:
                        last = nc.tensor.matmul(ps[:, bank, q0:q0 + P], c["identb"][:], c["after_k"][:],
                                                start=False, stop=True)
                last.then_inc(st_ready, 1)

            def values(t, g, kt):
                q0 = first_query(kt)
                pe.wait_ge(exp_done, t * UNITS + (2 * kt + 2))
                if kt == 0:
                    pe.wait_ge(vs_ready, t + 1)
                    at(pe, ot_ready, t)
                for h in range(GH):
                    last = nc.tensor.matmul(ps[32 * h:32 * h + 32, OUT_BANK, q0:SEQ], vs[:, g, kt, h, :],
                                            pt[:, 2 * (kt % 2) + h // 2, h % 2, q0:SEQ],
                                            start=kt == 0, stop=kt == QT - 1)
                last.then_inc(pv_done, 1)

            def turn_out(t):
                pe.wait_ge(ot_ready, t + 1)
                pe.wait_ge(ctx_done, t + 1)
                at(pe, m_split, min(t + 3, STEPS) if isinstance(t, int) else t + 3)
                for i in range(QT):
                    last = nc.tensor.transpose(ps[:, MISC, i * P:(i + 1) * P], ot[:, i * P:(i + 1) * P], c["ident"][:])
                last.then_inc(ott_ready, 1)

            def step(t, g):
                for u in range(UNITS):
                    if has(t, 2):
                        for n in range(2):
                            first_pass(t + 2, (g + 2) % GROUPS, 2 * u + n, uses(t + 2, (g + 2) % GROUPS))
                    second_pass(t, g, u, uses(t, g))
                    if u == 0 and has(t, 1):
                        turn_max(t + 1, (g + 1) % GROUPS)
                    if u == 1 and has(t, -1):
                        values(t - 1, (g - 1) % GROUPS, QT - 1)
                    if u == 3 and has(t, -1):
                        turn_out(t - 1)
                    if u % 2 == 1 and u > 1:
                        values(t, g, u // 2 - 1)

            def uses(t, g):
                if isinstance(t, int):
                    return t // GROUPS + 1
                return Quotient(t - g)

            pe.sem_inc(ott_ready, 1)
            for u in range(MAXES):
                first_pass(0, 0, u, 1)
            turn_max(0, 0)
            for u in range(MAXES):
                first_pass(1, 1, u, 1)
            steps(nc.tensor, step)
            values(STEPS - 1, GROUPS - 1, QT - 1)
            turn_out(STEPS - 1)
    st.clear()


class Quotient:

    def __init__(self, t):
        self.t = t

    def __mul__(self, by):
        assert by % GROUPS == 0
        return self.t * (by // GROUPS) + by


def attention_back(nc, name, c, w, ps, x_res, ctx_all):
    mem = ExitStack()
    st = Store(nc, mem)
    name += "b_"
    cs = st.sb(name + "ctx", [P, QT, P])
    ct = st.sb(name + "ctx_t", [P, SEQ])
    sub = st.sb(name + "sum", [P, QT, P])
    cs_ready = st.sem(name + "ctx_ready")
    ct_ps = st.sem(name + "ctx_t_in_psum")
    ct_ready = st.sem(name + "ctx_t_ready")
    o_ps = st.sem(name + "out_in_psum")
    sub_ready = st.sem(name + "sum_ready")
    x_done = st.sem(name + "x_done")
    with nc.Block() as block:
        @block.gpsimd
        def _(pool):
            nc.gpsimd.tensor_copy(cs[:], tiles_of(ctx_all, 0)).then_inc(cs_ready, 1)
            with nc.gpsimd.Fori(1, BATCHES) as b:
                pool.wait_ge(ct_ps, b)
                nc.gpsimd.tensor_copy(cs[:], tiles_of(ctx_all, b)).then_inc(cs_ready, 1)

        @block.tensor
        def _(pe):
            with nc.tensor.Fori(0, BATCHES) as b:
                pe.wait_ge(cs_ready, b + 1)
                for i in range(QT):
                    last = nc.tensor.transpose(ps[:, 0, i * P:(i + 1) * P], cs[:, i, :], c["ident"][:])
                last.then_inc(ct_ps, 1)
                pe.wait_ge(ct_ready, b + 1)
                pe.wait_ge(sub_ready, b + 1)
                for i in range(QT):
                    last = nc.tensor.matmul(ps[:, 1, i * P:(i + 1) * P], ct[:, i * P:(i + 1) * P], w["wo"][:],
                                            start=True, stop=True)
                last.then_inc(o_ps, 1)

        @block.scalar
        def _(act):
            with nc.scalar.Fori(0, BATCHES) as b:
                act.wait_ge(ct_ps, b + 1)
                nc.scalar.copy(ct[:], ps[:, 0, :]).then_inc(ct_ready, 1)

        @block.vector
        def _(dve):
            dve.sem_inc(sub_ready, 1)
            with nc.vector.Fori(0, BATCHES) as b:
                dve.wait_ge(o_ps, b + 1)
                nc.vector.tensor_tensor(sub[:], ps[:, 1, :].rearrange("p (i e) -> p i e", i=QT),
                                        w["bo"][:].rearrange("p (o e) -> p o e", o=1).to_broadcast([P, QT, P]),
                                        ALU.add).then_inc(sub_ready, 1)
                dve.wait_ge(sub_ready, b + 2)
                nc.vector.tensor_tensor(tiles_of(x_res, b), tiles_of(x_res, b), sub[:], ALU.add).then_inc(x_done, 1)
                dve.wait_ge(x_done, b + 1)
    st.clear()
    mem.close()


def experts(nc, name, d, c, w, ps, x_res, y_all, ctx_all, out):
    mem = ExitStack()
    st = Store(nc, mem)
    name += "e_"
    SLOTS = EXPERTS
    cs = st.sb(name + "ctx", [P, QT, P])
    ct = st.sb(name + "ctx_t", [P, SEQ])
    x2 = st.sb(name + "x2", [P, QT, P])
    z = st.sb(name + "z", [P, QT, P])
    xt = st.sb(name + "xt", [P, 2, SEQ])
    acc = st.sb(name + "acc", [P, 2, QT, P])
    gate = st.sb(name + "gate", [P, 2, QT, EXPERTS])
    gt = st.sb(name + "gate_t", [EXPERTS, SEQ])
    ht = st.sb(name + "ht", [P, 2, FC, SEQ])
    lg = st.sb(name + "logits", [P, QT, EXPERTS])
    eq = st.sb(name + "equal", [P, QT, EXPERTS])
    key = st.sb(name + "key", [P, QT, EXPERTS])
    pick1 = st.sb(name + "pick1", [P, QT, EXPERTS])
    pick2 = st.sb(name + "pick2", [P, QT, EXPERTS])
    left = st.sb(name + "left", [P, QT, EXPERTS])
    top = st.sb(name + "top", [P, 2, QT])
    rank = st.sb(name + "rank", [P, 2, QT])
    gap = st.sb(name + "gap", [P, QT])
    share = st.sb(name + "share", [P, 2, QT])
    norm = Norm(st, c, name + "norm", 1e-5)
    cs_ready = st.sem(name + "ctx_ready")
    ct_ps = st.sem(name + "ctx_t_in_psum")
    ct_ready = st.sem(name + "ctx_t_ready")
    o_ps = st.sem(name + "out_in_psum")
    x2_ready = st.sem(name + "x2_ready")
    z_ready = st.sem(name + "z_ready")
    zt_ps = st.sem(name + "zt_in_psum")
    xt_ready = st.sem(name + "xt_ready")
    lg_ps = st.sem(name + "logits_in_psum")
    g_step = st.sem(name + "gate_step")
    gap_ready = st.sem(name + "gap_ready")
    tanh_done = st.sem(name + "tanh_done")
    share_done = st.sem(name + "share_done")
    gate_ready = st.sem(name + "gate_ready")
    gt_ps = st.sem(name + "gate_t_in_psum")
    gt_ready = st.sem(name + "gate_t_ready")
    b2_ps = st.sem(name + "bias_in_psum")
    sum_ready = st.sem(name + "acc_start")
    acc_ready = st.sem(name + "acc_ready")
    up_ps = st.sem(name + "up_in_psum")
    h_ready = st.sem(name + "h_ready")
    down_ps = st.sem(name + "down_in_psum")
    added = st.sem(name + "added")
    x_done = st.sem(name + "x_done")
    stored = st.sem(name + "stored")
    G_STEPS = 13

    def batches(eng, batch):
        with eng.Fori(0, (BATCHES - 2) // 2) as u:
            for j in range(2):
                batch(u * 2 + j, j, True)
        batch(BATCHES - 2, 0, True)
        batch(BATCHES - 1, 1, False)

    with nc.Block() as block:
        @block.gpsimd
        def _(pool):
            nc.gpsimd.tensor_copy(cs[:], tiles_of(ctx_all, 0)).then_inc(cs_ready, 1)
            norm.pool(pool, 0)
            with nc.gpsimd.Fori(1, BATCHES) as b:
                pool.wait_ge(ct_ps, b)
                nc.gpsimd.tensor_copy(cs[:], tiles_of(ctx_all, b)).then_inc(cs_ready, 1)
                norm.pool(pool, b)

        @block.tensor
        def _(pe):
            def prepare(b, par, slot):
                if slot == 0:
                    pe.wait_ge(cs_ready, b + 1)
                    at(pe, acc_ready, b)
                    for i in range(QT):
                        last = nc.tensor.transpose(ps[:, 0, i * P:(i + 1) * P], cs[:, i, :], c["ident"][:])
                    last.then_inc(ct_ps, 1)
                if slot == 1:
                    pe.wait_ge(ct_ready, b + 1)
                    at(pe, gt_ready, b)
                    for i in range(QT):
                        last = nc.tensor.matmul(ps[:, 1, i * P:(i + 1) * P], ct[:, i * P:(i + 1) * P], w["wo"][:],
                                                start=True, stop=True)
                    last.then_inc(o_ps, 1)
                if slot == 3:
                    pe.wait_ge(z_ready, b + 1)
                    for i in range(QT):
                        last = nc.tensor.transpose(ps[:, 0, i * P:(i + 1) * P], z[:, i, :], c["ident"][:])
                    last.then_inc(zt_ps, 1)
                if slot == 4:
                    pe.wait_ge(xt_ready, b + 1)
                    pe.wait_ge(x2_ready, b + 1)
                    for i in range(QT):
                        last = nc.tensor.matmul(ps[:, 1, i * EXPERTS:(i + 1) * EXPERTS], xt[:, par, i * P:(i + 1) * P],
                                                w["wg"][:], start=True, stop=True)
                    last.then_inc(lg_ps, 1)
                if slot == 6:
                    pe.wait_ge(gate_ready, b + 1)
                    for i in range(QT):
                        last = nc.tensor.transpose(ps[0:EXPERTS, 1, i * P:(i + 1) * P], gate[:, par, i, :], c["ident"][:])
                    last.then_inc(gt_ps, 1)
                if slot == 7:
                    pe.wait_ge(gt_ready, b + 1)
                    for i in range(QT):
                        last = nc.tensor.matmul(ps[:, 0, i * P:(i + 1) * P], gt[:, i * P:(i + 1) * P], w["b2"][:],
                                                start=True, stop=True)
                    last.then_inc(b2_ps, 1)

            def up(b, par, e, n):
                if e == 0:
                    pe.wait_ge(xt_ready, b + 1)
                for f in range(FC):
                    at(pe, h_ready, n * FC + (f - 1))
                    nc.tensor.matmul(ps[:, 2 + f % 2, :], w["w1"][:, e, f * P:(f + 1) * P], xt[:, par, :],
                                     start=True, stop=True).then_inc(up_ps, 1)

            def down(e, n):
                pe.wait_ge(h_ready, n * FC + FC)
                pe.wait_ge(added, n + 1)
                for i in range(QT):
                    for f in range(FC):
                        last = nc.tensor.matmul(ps[:, 4 + e % 2, i * P:(i + 1) * P], ht[:, e % 2, f, i * P:(i + 1) * P],
                                                w["w2"][:, e * FC + f, :], start=f == 0, stop=f == FC - 1)
                last.then_inc(down_ps, 1)

            def batch(b, par, more):
                for e in range(EXPERTS):
                    n = b * EXPERTS + e
                    if more and e < EXPERTS:
                        prepare(b + 1, 1 - par, e)
                    if e + 1 < EXPERTS:
                        up(b, par, e + 1, n + 1)
                    elif more:
                        up(b + 1, 1 - par, 0, n + 1)
                    down(e, n)

            pe.sem_inc(down_ps, 1)
            for slot in range(SLOTS):
                prepare(0, 0, slot)
            up(0, 0, 0, 0)
            batches(nc.tensor, batch)

        @block.scalar
        def _(act):
            def prepare(b, par, slot):
                if slot == 0:
                    act.wait_ge(ct_ps, b + 1)
                    nc.scalar.copy(ct[:], ps[:, 0, :]).then_inc(ct_ready, 1)
                if slot == 3:
                    act.wait_ge(zt_ps, b + 1)
                    nc.scalar.activation(xt[:, par, :], ps[:, 0, :], ACT.Identity, bias=w["ln2_b"][:, 0:1],
                                         scale=w["ln2_g"][:, 0:1]).then_inc(xt_ready, 1)
                if slot == 4:
                    act.wait_ge(gap_ready, b + 1)
                    nc.scalar.activation(gap[:], gap[:], ACT.Tanh, scale=0.5).then_inc(tanh_done, 1)
                if slot == 6:
                    act.wait_ge(gt_ps, b + 1)
                    nc.scalar.copy(gt[:], ps[0:EXPERTS, 1, :]).then_inc(gt_ready, 1)

            def gelu(e, n):
                at(act, down_ps, n)
                for f in range(FC):
                    act.wait_ge(up_ps, n * FC + (f + 1))
                    nc.scalar.activation(ht[:, e % 2, f, :], ps[:, 2 + f % 2, :], ACT.Gelu_apprx_tanh,
                                         bias=w["b1"][:, e * FC + f:e * FC + f + 1]).then_inc(h_ready, 1)

            def batch(b, par, more):
                for e in range(EXPERTS):
                    if more:
                        prepare(b + 1, 1 - par, e)
                    if e + 1 < EXPERTS or more:
                        gelu((e + 1) % EXPERTS, b * EXPERTS + (e + 1))

            for slot in range(SLOTS):
                prepare(0, 0, slot)
            gelu(0, 0)
            batches(nc.scalar, batch)

        @block.vector
        def _(dve):
            v = nc.vector

            def per_token(ap):
                return ap.rearrange("p (i o) -> p i o", o=1).to_broadcast([P, QT, EXPERTS])

            def choose(b, par):
                steps = [0]

                def step(ins):
                    steps[0] += 1
                    ins.then_inc(g_step, 1)
                    dve.wait_ge(g_step, b * G_STEPS + steps[0])

                dve.wait_ge(lg_ps, b + 1)
                step(v.tensor_copy(lg[:], ps[:, 1, 0:QT * EXPERTS].rearrange("p (i e) -> p i e", i=QT)))
                for j, (src, pick) in enumerate(((lg, pick1), (left, pick2))):
                    step(v.tensor_reduce(top[:, j, :], src[:], AX.X, ALU.max))
                    step(v.tensor_tensor(eq[:], src[:], per_token(top[:, j, :]), ALU.is_equal))
                    step(v.tensor_tensor(key[:], eq[:], w["rev"][:], ALU.mult))
                    step(v.tensor_reduce(rank[:, j, :], key[:], AX.X, ALU.max))
                    step(v.tensor_tensor(pick[:], key[:], per_token(rank[:, j, :]), ALU.is_equal))
                    if j == 0:
                        step(v.scalar_tensor_tensor(left[:], pick1[:], -3e38, lg[:], ALU.mult, ALU.add))
                v.tensor_tensor(gap[:], top[:, 0, :], top[:, 1, :], ALU.subtract).then_inc(gap_ready, 1)
                dve.wait_ge(tanh_done, b + 1)
                v.tensor_scalar(share[:, 0, :], gap[:], 0.5, 0.5, ALU.mult, ALU.add)
                step(v.tensor_scalar(share[:, 1, :], gap[:], -0.5, 0.5, ALU.mult, ALU.add))
                v.tensor_tensor(pick1[:], pick1[:], per_token(share[:, 0, :]), ALU.mult)
                v.tensor_tensor(pick2[:], pick2[:], per_token(share[:, 1, :]), ALU.mult).then_inc(share_done, 1)
                dve.wait_ge(share_done, b + 1)
                v.tensor_tensor(gate[:, par, :, :], pick1[:], pick2[:], ALU.add).then_inc(gate_ready, 1)
                assert steps[0] == G_STEPS, steps

            def prepare(b, par, slot):
                if slot == 1:
                    dve.wait_ge(o_ps, b + 1)
                    v.tensor_tensor(x2[:], tiles_of(y_all, b), ps[:, 1, :].rearrange("p (i e) -> p i e", i=QT),
                                    ALU.add).then_inc(x2_ready, 1)
                    dve.wait_ge(x2_ready, b + 1)
                    norm.vector(dve, b, [x2[:, i, :] for i in range(QT)], [z[:, i, :] for i in range(QT)]).then_inc(z_ready, 1)
                if slot == 4:
                    choose(b, par)
                if slot == 7:
                    dve.wait_ge(b2_ps, b + 1)
                    v.tensor_tensor(acc[:, par, :, :], x2[:], ps[:, 0, :].rearrange("p (i e) -> p i e", i=QT),
                                    ALU.add).then_inc(sum_ready, 1)
                    dve.wait_ge(sum_ready, b + 1)
                    v.tensor_tensor(acc[:, par, :, :], acc[:, par, :, :], tiles_of(x_res, b), ALU.add).then_inc(acc_ready, 1)

            def add(b, par, e, n):
                dve.wait_ge(down_ps, n + 2)
                if e == 0:
                    dve.wait_ge(acc_ready, b + 1)
                    dve.wait_ge(gate_ready, b + 1)
                else:
                    dve.wait_ge(added, n + 2)
                for i in range(QT):
                    dst = acc[:, par, i, :] if e < EXPERTS - 1 else tile_of(x_res, b * QT + i)
                    last = v.scalar_tensor_tensor(dst, ps[:, 4 + e % 2, i * P:(i + 1) * P], gate[:, par, i, e:e + 1],
                                                  acc[:, par, i, :], ALU.mult, ALU.add)
                last.then_inc(added, 1)

            def batch(b, par, more):
                for e in range(EXPERTS):
                    if more:
                        prepare(b + 1, 1 - par, e)
                    add(b, par, e, b * EXPERTS + e)

            dve.sem_inc(added, 2)
            for slot in range(SLOTS):
                prepare(0, 0, slot)
            batches(nc.vector, batch)

        if out is not None:
            out_v = out.rearrange("b (i p) e -> p b i e", p=P)

            @block.sync
            def _(sp):
                with nc.sync.Fori(0, BATCHES) as b:
                    sp.wait_ge(added, b * EXPERTS + (EXPERTS + 2))
                    sp.dma_start(out_v[:, bass.ds(b, 1), :, :].rearrange("p a i e -> p (a i) e"),
                                 tiles_of(x_res, b)).then_inc(stored, 16)
                sp.wait_ge(stored, 16 * BATCHES)
    st.clear()
    mem.close()


_INS = ["L0_attn_a_x", "L0_attn_a_Wq", "L0_attn_a_Wk", "L0_attn_a_Wv", "L0_attn_a_Wo", "L0_attn_a_proj",
        "L0_attn_a_W1", "L0_attn_a_b1", "L0_attn_a_W2", "L0_attn_a_b2", "L0_attn_a_ln1_g", "L0_attn_a_ln1_b",
        "L0_attn_a_ln2_g", "L0_attn_a_ln2_b", "L0_attn_b_wq", "L0_attn_b_bq", "L0_attn_b_wk", "L0_attn_b_bk",
        "L0_attn_b_wv", "L0_attn_b_bv", "L0_attn_b_wo", "L0_attn_b_bo", "L0_ffn_ln1_g", "L0_ffn_ln1_b",
        "L0_ffn_ln2_g", "L0_ffn_ln2_b", "L0_ffn_Wq", "L0_ffn_Wk", "L0_ffn_Wv", "L0_ffn_Wo", "L0_ffn_Wg",
        "L0_ffn_W1", "L0_ffn_b1", "L0_ffn_W2", "L0_ffn_b2"]


def tables():
    t = {}
    p, ch, m = np.arange(P)[:, None, None], np.arange(CH)[None, :, None], np.arange(P)[None, None, :]
    row = 2 * (ch // 4) + p // PM
    col = np.arange(32)[None, None, :]
    t["perf_mask"] = ((col == row) | (col >= 4)).astype(np.float32)
    t["perf_pick"] = (p == 32 * (ch % 4) + 2 * (ch // 4) + m // PM).astype(np.float32)
    inv_freq = (np.float32(1) / np.float32(10000) ** (np.arange(0, HD, 2, dtype=np.float32) / np.float32(HD)))
    angle = np.arange(SEQ, dtype=np.float32)[None, :] * inv_freq.astype(np.float32)[:, None]
    cos, sin = np.cos(angle).astype(np.float32), np.sin(angle).astype(np.float32)
    rows = np.arange(P)
    t["rope_cos"] = np.ascontiguousarray(cos[(rows % HD) // 2])
    t["rope_sin"] = np.ascontiguousarray(sin[(rows % HD) // 2] * np.where(rows % 2, 1, -1)[:, None].astype(np.float32))
    t["expert_rank"] = np.ascontiguousarray(np.broadcast_to(
        np.arange(EXPERTS, 0, -1, dtype=np.float32), (P, QT, EXPERTS)))
    return t


def kernel(**inputs):
    import concourse.bacc as bacc
    from concourse.bass_utils import run_bass_kernel_spmd

    nc = bacc.Bacc("TRN2", target_bir_lowering=False, num_devices=1)
    given = {n: np.ascontiguousarray(inputs[n]) for n in _INS} | tables()
    arrays, d = {}, {}
    for n, a in given.items():
        arrays[f"in_{n}"] = a
        d[n] = nc.dram_tensor(f"in_{n}", a.shape, mybir.dt.from_np(a.dtype), kind="ExternalInput").ap()
    out = nc.dram_tensor("out_x", (BATCHES, SEQ, P), F32, kind="ExternalOutput").ap()
    build(nc, d, out)
    r = run_bass_kernel_spmd(nc, [arrays], core_ids=[0])
    return r.results[0]["out_x"]
```

```python
import math
from contextlib import ExitStack

import numpy as np
import concourse.bass as bass
from concourse import mybir

F32 = mybir.dt.float32
BF16 = mybir.dt.bfloat16
ALU = mybir.AluOpType
ACT = mybir.ActivationFunctionType
AX = mybir.AxisListType
RMAX = bass.bass_isa.ReduceOp.max

P = 128
BATCHES, SEQ = 8, 512
QT = SEQ // P
TILES = BATCHES * QT
HEADS = 16
PH, PD, PM = 16, 64, 64
CH = PH * PM // P
EPS_KERN = 1e-6
FF = 512
FC = FF // P
HD = P // HEADS
GROUPS = 4
GH = HEADS // GROUPS
STEPS = BATCHES * GROUPS
PARTS = 3
ROWS = HD * PARTS * PARTS
STACK = ROWS + PARTS
EPSILONS = (1e-5, 1e-6)
EXPERTS = 8


def at(eng, sem, value):
    if not isinstance(value, int) or value > 0:
        eng.wait_ge(sem, value)


class Store:

    def __init__(self, nc, ctx):
        self.nc, self.ctx, self.sems = nc, ctx, []

    def sb(self, name, shape, dt=F32):
        return self.ctx.enter_context(self.nc.sbuf_tensor(name, shape, dt))

    def sem(self, name):
        self.sems.append(self.nc.alloc_semaphore(name))
        return self.sems[-1]

    def clear(self):
        self.nc.clear_and_free_semaphores(self.sems)
        self.nc.all_engine_barrier()
        self.sems = []


def flat(ap):
    return ap.rearrange("p a c -> p (a c)")


def tile_of(buf, t):
    return flat(buf[:, bass.ds(t, 1), :])


def tiles_of(buf, b, n=QT):
    return buf[:, bass.ds(b * n, n), :]


class Norm:

    def __init__(self, st, c, name, eps):
        self.nc, self.eps, self.half = st.nc, c[f"eps{eps:g}"], c["half"]
        self.gate = st.sb(name + "_gate", [1, 1])
        self.var = st.sb(name + "_var", [P, QT])
        self.eps_done = st.sem(name + "_eps_done")
        self.stats = st.sb(name + "_stats", [P, QT, 6])
        self.mv = st.sb(name + "_mv", [P, QT, 2])
        self.rstd = st.sb(name + "_rstd", [P, QT])
        self.stats_done = st.sem(name + "_stats_done")
        self.var_done = st.sem(name + "_var_done")
        self.rstd_done = st.sem(name + "_rstd_done")

    def vector(self, dve, k, src, dst):
        take_statistics(self, dve, k, src)
        return normalise(self, dve, k, src, dst)

    def pool(self, pool, k):
        pool.wait_ge(self.var_done, k + 1)
        self.nc.gpsimd.tensor_tensor(self.var[:, :], self.mv[:, :, 1], self.eps[:, :], ALU.add).then_inc(self.eps_done, 1)
        pool.wait_ge(self.eps_done, k + 1)
        self.nc.gpsimd.tensor_tensor(self.rstd[:, :], self.var[:, :], self.half[:, :], ALU.pow).then_inc(self.rstd_done, 1)


def take_statistics(norm, dve, k, src):
    nc = norm.nc
    for i in range(QT):
        last = nc.vector.bn_stats(norm.stats[:, i, :], src[i])
    last.then_inc(norm.stats_done, 1)
    dve.wait_ge(norm.stats_done, k + 1)
    nc.vector.tensor_copy(norm.gate[:, :], norm.half[0:1, 0:1])
    for i in range(QT):
        last = nc.vector.bn_aggr(norm.mv[:, i, :], norm.stats[:, i, :])
    last.then_inc(norm.var_done, 1)


def normalise(norm, dve, k, src, dst):
    dve.wait_ge(norm.rstd_done, k + 1)
    dve.wait_ge(norm.var_done, k + 1)
    for i in range(QT):
        last = norm.nc.vector.tensor_scalar(dst[i], src[i], norm.mv[:, i, 0:1], norm.rstd[:, i:i + 1],
                                            ALU.subtract, ALU.mult)
    return last


def build(nc, d, out, layers=3, probe=None):
    ctx = ExitStack()
    with ctx:
        st = Store(nc, ctx)
        ps = ctx.enter_context(nc.psum_tensor("ps", [P, 8, 512], F32))
        c = load_constants(nc, st, d)
        c["ps"] = ps
        x_res = st.sb("x_res", [P, TILES, P])
        y_ext = st.sb("y_all", [P, TILES, P + 1])
        y_all = y_ext[:, :, 0:P]
        load_x(nc, st, d, x_res)
        performer(nc, d, c, ps, x_res, y_ext, y_all)
        with ExitStack() as rest:
            sm = Store(nc, rest)
            v_all = sm.sb("v_all", [P, TILES, P])
            ctx_all = sm.sb("ctx_all", [P, TILES, P])
            for layer in range(3):
                rope = layer == 1
                name = f"L{layer}"
                w = load_attention_weights(nc, d, c, name, rope, sm, layer)
                with ExitStack() as attention:
                    a = attention_memory(nc, Store(nc, attention), name)
                    attention_front(nc, name, rope, c, w, a, ps, x_res, y_all, v_all)
                    attention_main(nc, name, rope, c, a, ps, v_all, ctx_all)
                if rope:
                    attention_back(nc, name, c, w, ps, x_res, ctx_all)
                else:
                    experts(nc, name, d, c, w, ps, x_res, y_all, ctx_all, out if layer == 2 else None)


def load_constants(nc, st, d):
    c = {}
    c["ident"] = ident = st.sb("ident", [P, P])
    c["identb"] = identb = st.sb("identb", [P, P], BF16)
    c["ones"] = ones = st.sb("ones", [P, P])
    c["minus"] = st.sb("minus_one", [P, 1])
    for eps in EPSILONS:
        c[f"eps{eps:g}"] = st.sb(f"norm_eps{eps:g}", [P, QT])
    c["half"] = half = st.sb("minus_half", [P, QT])
    c["after_q"] = after_q = st.sb("after_q", [P, P], BF16)
    c["after_k"] = after_k = st.sb("after_k", [P, P], BF16)
    const_ready = st.sem("const_ready")
    with nc.Block() as block:
        @block.gpsimd
        def _(pool):
            g = nc.gpsimd
            g.memset(ident[:], 0.0).then_inc(const_ready, 1)
            g.memset(after_q[:], 0.0).then_inc(const_ready, 1)
            g.memset(after_k[:], 0.0).then_inc(const_ready, 1)
            g.memset(half[:], -0.5)
            g.memset(c["minus"][:], -1.0)
            for eps in EPSILONS:
                g.memset(c[f"eps{eps:g}"][:], eps)
            g.memset(ones[:], 1.0).then_inc(const_ready, 1)
            pool.wait_ge(const_ready, 4)
            g.affine_select(out=ident[:], in_=ident[:], compare_op=ALU.not_equal, fill=1.0, base=0,
                            pattern=[[-1, P]], channel_multiplier=1).then_inc(const_ready, 1)
            g.affine_select(out=after_q[:], in_=after_q[:], compare_op=ALU.is_ge, fill=-4e9, base=0,
                            pattern=[[-1, P]], channel_multiplier=1).then_inc(const_ready, 1)
            g.affine_select(out=after_k[:], in_=after_k[:], compare_op=ALU.is_ge, fill=-4e9, base=0,
                            pattern=[[1, P]], channel_multiplier=-1).then_inc(const_ready, 1)
            pool.wait_ge(const_ready, 7)
            g.tensor_copy(identb[:], ident[:]).then_inc(const_ready, 1)
    return c


def load_x(nc, st, d, x_res):
    x_loaded = st.sem("x_loaded")
    xv = d["L0_attn_a_x"].rearrange("b (n p) e -> p (b n) e", p=P)
    with nc.Block() as block:
        @block.sync
        def _(sp):
            for b in range(BATCHES):
                sp.dma_start(x_res[:, b * QT:(b + 1) * QT, :], xv[:, b * QT:(b + 1) * QT, :]).then_inc(x_loaded, 16)
            sp.wait_ge(x_loaded, 16 * BATCHES)


def performer(nc, d, c, ps, x_res, y_ext, y_all):
    with ExitStack() as mem:
        st = Store(nc, mem)
        w = performer_weights(nc, st, d, c, ps)
        k = performer_keys(nc, st, c, w, ps, x_res, y_ext)
        performer_queries(nc, st, c, w, k, ps, x_res, y_all)
        st.clear()


def performer_weights(nc, st, d, c, ps):
    w = {}
    wide = PH * PD
    w["wq"] = wq = st.sb("a_wq", [P, wide])
    w["wk"] = wk = st.sb("a_wk", [P, wide])
    w["wqp"] = wqp = st.sb("a_wqp", [P, wide])
    w["wkp"] = wkp = st.sb("a_wkp", [P, wide])
    w["wvo"] = wvo = st.sb("a_wvo", [P, PH, P])
    w["w1"] = w1 = st.sb("a_w1", [P, FF])
    w["w2"] = w2 = st.sb("a_w2", [P, FC, P])
    w["b1"] = b1 = st.sb("a_b1", [P, FC])
    w["eps"] = eps = st.sb("a_eps", [P, 1])
    w["mask"] = mask = st.sb("a_mask", [P, CH, PH])
    rows = {}
    for n in ("b2", "ln1_g", "ln1_b", "ln2_g", "ln2_b"):
        w[n] = rows[n] = st.sb("a_" + n, [P, P])
    with ExitStack() as temp:
        t = Store(nc, temp)
        wv = t.sb("a_wv", [P, wide])
        wo = t.sb("a_wo", [P, CH, P])
        wt = t.sb("a_wt", [P, 3, CH, P])
        projp = t.sb("a_projp", [P, P])
        projt = t.sb("a_projt", [P, P])
        loaded = st.sem("a_w_loaded")
        zeroed = st.sem("a_proj_zeroed")
        turned = st.sem("a_w_turned")
        copied = st.sem("a_w_copied")
        product = st.sem("a_w_product")
        n_loads = 13 + len(rows)
        with nc.Block() as block:
            @block.sync
            def _(sp):
                def load(dst, src):
                    sp.dma_start(dst, src).then_inc(loaded, 16)

                sp.wait_ge(zeroed, 1)
                for h in range(2):
                    load(projp[h * PM:(h + 1) * PM, h * PD:(h + 1) * PD], d["L0_attn_a_proj"])
                load(wq[:], d["L0_attn_a_Wq"].rearrange("e h k -> e (h k)"))
                load(wk[:], d["L0_attn_a_Wk"].rearrange("e h k -> e (h k)"))
                load(wv[:], d["L0_attn_a_Wv"].rearrange("e h k -> e (h k)"))
                load(wo[:], d["L0_attn_a_Wo"].rearrange("h k o -> (h k) o").rearrange("(c p) o -> p c o", p=P))
                load(w1[:], d["L0_attn_a_W1"])
                load(w2[:], d["L0_attn_a_W2"].rearrange("(c p) o -> p c o", p=P))
                for f in range(FC):
                    load(b1[:, f:f + 1], d["L0_attn_a_b1"][f * P:(f + 1) * P].rearrange("(p o) -> p o", o=1))
                load(mask[:], d["perf_mask"])
                for n, dst in rows.items():
                    load(dst[:], d["L0_attn_a_" + n].partition_broadcast(P))
                sp.wait_ge(loaded, 16 * n_loads)

            @block.gpsimd
            def _(pool):
                nc.gpsimd.memset(eps[:], EPS_KERN)
                nc.gpsimd.memset(projp[:], 0.0).then_inc(zeroed, 1)

            @block.tensor
            def _(pe):
                pe.wait_ge(loaded, 16 * n_loads)
                nc.tensor.transpose(ps[:, 0, 0:P], projp[:], c["ident"][:]).then_inc(turned, 1)
                for i, src in enumerate((wq, wk, wv)):
                    for j in range(CH):
                        last = nc.tensor.transpose(ps[:, 1 + 2 * i + j // 4, (j % 4) * P:(j % 4 + 1) * P],
                                                   src[:, j * P:(j + 1) * P], c["ident"][:])
                    last.then_inc(turned, 1)
                pe.wait_ge(copied, 4)
                for i in range(2):
                    for j in range(CH):
                        last = nc.tensor.matmul(ps[:, 2 * i + j // 4, (j % 4) * P:(j % 4 + 1) * P],
                                                wt[:, i, j, :], projt[:], start=True, stop=True)
                last.then_inc(product, 1)
                for half in range(2):
                    for j in range(CH):
                        last = nc.tensor.matmul(ps[:, 4 + 2 * half + j // 4, (j % 4) * P:(j % 4 + 1) * P],
                                                wt[half * PD:(half + 1) * PD, 2, j, :],
                                                wo[half * PD:(half + 1) * PD, j, :], start=True, stop=True)
                last.then_inc(product, 1)

            @block.vector
            def _(dve):
                dve.wait_ge(turned, 1)
                nc.vector.tensor_scalar(projt[:], ps[:, 0, 0:P], PD ** -0.25, None, ALU.mult).then_inc(copied, 1)
                for i in range(3):
                    dve.wait_ge(turned, 2 + i)
                    nc.vector.tensor_copy(wt[:, i, :, :].rearrange("p c e -> p (c e)"),
                                          ps[:, 1 + 2 * i:3 + 2 * i, :].rearrange("p a b -> p (a b)")).then_inc(copied, 1)
                dve.wait_ge(product, 2)
                for i, dst in enumerate((wqp, wkp)):
                    nc.vector.tensor_copy(dst[:], ps[:, 2 * i:2 * i + 2, :].rearrange("p a b -> p (a b)"))
                for half in range(2):
                    nc.vector.tensor_copy(wvo[:].rearrange("p (c two) o -> p two c o", two=2)[:, half, :, :],
                                          ps[:, 4 + 2 * half:6 + 2 * half, :].rearrange("p a (c o) -> p (a c) o", o=P))
    return w


def performer_keys(nc, st, c, w, ps, x_res, y_ext):
    k = {}
    A = P + 1
    k["sums"] = sums = st.sb("a_sums", [P, BATCHES, CH * A])
    k["ysum"] = ysum = st.sb("a_ysum", [P, BATCHES, A])
    k["peak"] = peak = st.sb("a_peak", [P, BATCHES])
    temp = ExitStack()
    t = Store(nc, temp)
    y = t.sb("k_y", [P, QT, P])
    yt = t.sb("k_yt", [P, 2, SEQ])
    sq = t.sb("k_sq", [P, 2, PH * PD])
    ssq = t.sb("k_ssq", [P, 2, PH])
    e = t.sb("k_e", [P, 2, QT, PH * PM])
    tmax = t.sb("k_tmax", [P, 2, QT])
    bmax = t.sb("k_bmax", [P, 2])
    gate = t.sb("k_gate", [1, 2])
    bpeak = t.sb("k_bpeak", [P, 2])
    nl = t.sb("k_nl", [P, 2])
    norm = Norm(t, c, "k_norm", 1e-5)
    y_ready = t.sem("k_y_ready")
    y_saved = t.sem("k_y_saved")
    yt_ps = t.sem("k_yt_in_psum")
    yt_ready = t.sem("k_yt_ready")
    k_ready = t.sem("k_k_in_psum")
    dd_ready = t.sem("k_dd_in_psum")
    sq_ready = t.sem("k_squares_ready")
    ssq_ready = t.sem("k_ssq_ready")
    max_done = t.sem("k_tile_max_done")
    e_ready = t.sem("k_exponent_ready")
    bmax_ready = t.sem("k_batch_max_ready")
    peak_ready = t.sem("k_batch_peak_ready")
    nl_ready = t.sem("k_neg_peak_ready")
    peak_saved = t.sem("k_peak_saved")
    exp_done = t.sem("k_exp_done")
    g_ready = t.sem("k_sums_in_psum")
    g_saved = t.sem("k_sums_saved")
    ones_set = t.sem("k_ones_set")
    PIECES = [list(range(s, min(s + 3, CH))) for s in range(0, CH, 3)]
    N_PIECES = len(PIECES)

    def is_batch(b):
        return not isinstance(b, int) or 0 <= b < BATCHES

    def batches(eng, batch):
        batch(-1, 1)
        batch(0, 0)
        with eng.Fori(0, (BATCHES - 2) // 2) as u:
            for j in range(2):
                batch(u * 2 + (1 + j), 1 - j)
        batch(BATCHES - 1, 1)
        batch(BATCHES, 0)

    with nc.Block() as block:
        @block.vector
        def _(dve):
            def tile(b, par, i):
                if is_batch(b):
                    n = b * QT + i
                    dve.wait_ge(sq_ready, n + 1)
                    nc.vector.tensor_reduce(ssq[:, i % 2, :], sq[:, i % 2, :].rearrange("p (h k) -> p h k", h=PH),
                                            AX.X, ALU.add).then_inc(ssq_ready, 1)
                    dve.wait_ge(dd_ready, n + 1)
                    nc.vector.tensor_reduce(tmax[:, par, i:i + 1], ps[:, 2:4, :].rearrange("p a b -> p (a b)"),
                                            AX.X, ALU.max).then_inc(max_done, 1)
                    dve.wait_ge(ssq_ready, n + 1)
                    if i == 0:
                        at(dve, g_ready, b * N_PIECES)
                    nc.vector.scalar_tensor_tensor(
                        e[:, par, i, :].rearrange("p (h m) -> p h m", h=PH),
                        ssq[:, i % 2, :].rearrange("p (h o) -> p h o", o=1).to_broadcast([P, PH, PM]), -1.0 / 16,
                        ps[:, 2:4, :].rearrange("p a (h m) -> p (a h) m", m=PM), ALU.mult, ALU.add).then_inc(e_ready, 1)

            def batch(b, par):
                tile(b, par, 0)
                if is_batch(b + 1):
                    xs = [tile_of(x_res, (b + 1) * QT + i) for i in range(QT)]
                    take_statistics(norm, dve, b + 1, xs)
                tile(b, par, 1)
                if is_batch(b + 1):
                    at(dve, y_saved, b + 1)
                    at(dve, yt_ps, b + 1)
                    normalise(norm, dve, b + 1, xs, [y[:, i, :] for i in range(QT)]).then_inc(y_ready, 1)
                tile(b, par, 2)
                tile(b, par, 3)
                if is_batch(b):
                    dve.wait_ge(max_done, b * QT + QT)
                    nc.vector.reduce_max(bmax[:, par:par + 1], tmax[:, par, :], AX.X).then_inc(bmax_ready, 1)

            batches(nc.vector, batch)

        @block.gpsimd
        def _(pool):
            def batch(b, par):
                if is_batch(b + 1):
                    norm.pool(pool, b + 1)
                    pool.wait_ge(y_ready, b + 2)
                    nc.gpsimd.tensor_copy(tiles_of(y_ext, b + 1)[:, :, 0:P], y[:]).then_inc(y_saved, 1)
                if is_batch(b):
                    pool.wait_ge(bmax_ready, b + 1)
                    nc.gpsimd.tensor_tensor(gate[:, par:par + 1], c["minus"][0:1, :], c["minus"][0:1, :], ALU.mult)
                    nc.gpsimd.partition_all_reduce(bpeak[:, par:par + 1], bmax[:, par:par + 1], P, RMAX).then_inc(peak_ready, 1)
                    at(pool, exp_done, b)
                    pool.wait_ge(peak_ready, b + 1)
                    nc.gpsimd.tensor_tensor(nl[:, par:par + 1], bpeak[:, par:par + 1], c["minus"][:], ALU.mult).then_inc(nl_ready, 1)
                    nc.gpsimd.tensor_copy(peak[:, bass.ds(b, 1)], bpeak[:, par:par + 1]).then_inc(peak_saved, 1)

            nc.gpsimd.memset(y_ext[:, :, P:A], 1.0).then_inc(ones_set, 1)
            batches(nc.gpsimd, batch)

        @block.scalar
        def _(act):
            def square(b, i):
                if is_batch(b):
                    n = b * QT + i
                    act.wait_ge(k_ready, n + 1)
                    at(act, ssq_ready, n - 1)
                    nc.scalar.activation(sq[:, i % 2, :], ps[:, 0:2, :].rearrange("p a b -> p (a b)"),
                                         ACT.Square).then_inc(sq_ready, 1)

            def exponential(b, par, half):
                if is_batch(b):
                    act.wait_ge(nl_ready, b + 1)
                    act.wait_ge(e_ready, b * QT + QT)
                    two = e[:, par, 2 * half:2 * half + 2, :].rearrange("p i f -> p (i f)")
                    last = nc.scalar.activation(two, two, ACT.Exp, bias=nl[:, par:par + 1])
                    if half == 1:
                        last.then_inc(exp_done, 1)

            def save_sums(b, s):
                if is_batch(b):
                    act.wait_ge(g_ready, b * N_PIECES + (N_PIECES + s + 1))
                    mine = flat(sums[:, bass.ds(b, 1), :])[:, PIECES[s][0] * A:(PIECES[s][-1] + 1) * A]
                    last = nc.scalar.copy(mine, ps[:, 4 + s, 0:len(PIECES[s]) * A])
                    if s == N_PIECES - 1:
                        last = nc.scalar.copy(flat(ysum[:, bass.ds(b, 1), :]), ps[:, 7, 0:A])
                    last.then_inc(g_saved, 1)

            def batch(b, par):
                square(b, 0)
                exponential(b - 1, 1 - par, 0)
                square(b, 1)
                exponential(b - 1, 1 - par, 1)
                square(b, 2)
                save_sums(b - 1, 0)
                square(b, 3)
                if is_batch(b + 1):
                    act.wait_ge(yt_ps, b + 2)
                    nc.scalar.copy(yt[:, 1 - par, :], ps[:, 7, :]).then_inc(yt_ready, 1)
                save_sums(b - 1, 1)
                save_sums(b - 1, 2)

            act.sem_inc(exp_done, 1)
            act.sem_inc(g_saved, N_PIECES)
            batches(nc.scalar, batch)

        @block.tensor
        def _(pe):
            def tile(b, par, i):
                if is_batch(b):
                    n = b * QT + i
                    cols = yt[:, par, i * P:(i + 1) * P]
                    pe.wait_ge(yt_ready, b + 1)
                    at(pe, sq_ready, n)
                    for half in range(2):
                        last = nc.tensor.matmul(ps[:, half, :], cols, w["wk"][:, half * 512:(half + 1) * 512],
                                                start=True, stop=True)
                    last.then_inc(k_ready, 1)
                    at(pe, e_ready, n)
                    for half in range(2):
                        last = nc.tensor.matmul(ps[:, 2 + half, :], cols, w["wkp"][:, half * 512:(half + 1) * 512],
                                                start=True, stop=True)
                    last.then_inc(dd_ready, 1)

            def add_up(b, par, s):
                if is_batch(b):
                    pe.wait_ge(exp_done, b + 2)
                    pe.wait_ge(y_saved, b + 1)
                    pe.wait_ge(ones_set, 1)
                    pe.wait_ge(g_saved, b * N_PIECES + (s + 1))
                    ys = tiles_of(y_ext, b)
                    for at_col, j in enumerate(PIECES[s]):
                        for i in range(QT):
                            last = nc.tensor.matmul(ps[:, 4 + s, at_col * A:(at_col + 1) * A],
                                                    e[:, par, i, j * P:(j + 1) * P], ys[:, i, :],
                                                    start=i == 0, stop=i == QT - 1)
                    if s == N_PIECES - 1:
                        if is_batch(b + 2):
                            pe.wait_ge(yt_ready, b + 3)
                        for i in range(QT):
                            last = nc.tensor.matmul(ps[:, 7, 0:A], c["ones"][:], ys[:, i, :],
                                                    start=i == 0, stop=i == QT - 1)
                    last.then_inc(g_ready, 1)

            def batch(b, par):
                tile(b, par, 0)
                tile(b, par, 1)
                add_up(b - 1, 1 - par, 0)
                tile(b, par, 2)
                if is_batch(b + 1):
                    pe.wait_ge(y_ready, b + 2)
                    at(pe, g_saved, b * N_PIECES)
                    for i in range(QT):
                        last = nc.tensor.transpose(ps[:, 7, i * P:(i + 1) * P], y[:, i, :], c["ident"][:])
                    last.then_inc(yt_ps, 1)
                add_up(b - 1, 1 - par, 1)
                tile(b, par, 3)
                add_up(b - 1, 1 - par, 2)

            pe.sem_inc(g_ready, N_PIECES)
            batches(nc.tensor, batch)
    t.clear()
    temp.close()
    return k


def performer_queries(nc, st, c, w, k, ps, x_res, y_all):
    A = P + 1
    sums, ysum, peak = k["sums"], k["ysum"], k["peak"]
    gmax = st.sb("q_gmax", [P, 1])
    shift = st.sb("q_shift", [P, BATCHES])
    y = st.sb("q_y", [P, QT, P])
    yt = st.sb("q_yt", [P, SEQ])
    es = st.sb("q_es", [P, A])
    gf = st.sb("q_gf", [P, CH, A])
    gt = st.sb("q_gt", [P, CH * P])
    ksd = st.sb("q_ksd", [P, BATCHES * CH, PH])
    sq = st.sb("q_sq", [P, PH * PD])
    ssq = st.sb("q_ssq", [P, PH])
    mx = st.sb("q_mx", [P, PH])
    cc = st.sb("q_cc", [P, PH])
    e = st.sb("q_e", [P, 2, PH * PM])
    qf = st.sb("q_qf", [P, 2, CH, P])
    rec = st.sb("q_rec", [P, PH])
    wide = st.sb("q_wide", [P, PH * PM])
    r1 = st.sb("q_r1", [P, QT, P])
    kept = st.sb("q_kept", [P, QT, P])
    gate = st.sb("q_gate", [1, 1])
    o1 = st.sb("q_o1", [P, QT, P])
    o1t = st.sb("q_o1t", [P, SEQ])
    pos = st.sb("q_pos", [P, 2, SEQ])
    neg = st.sb("q_neg", [P, 2, SEQ])
    ht = st.sb("q_ht", [P, FC, SEQ])
    f2 = st.sb("q_f2", [P, QT, P])
    norm1 = Norm(st, c, "q_norm1", 1e-6)
    norm2 = Norm(st, c, "q_norm2", 1e-6)
    gmax_ready = st.sem("q_gmax_ready")
    gap_ready = st.sem("q_gap_ready")
    shift_ready = st.sem("q_shift_ready")
    y_ready = st.sem("q_y_ready")
    yt_ps = st.sem("q_yt_in_psum")
    yt_ready = st.sem("q_yt_ready")
    es_ready = st.sem("q_es_ready")
    gf_ready = st.sem("q_gf_ready")
    ksd_ready = st.sem("q_ksd_ready")
    gt_ps = st.sem("q_gt_in_psum")
    gt_ready = st.sem("q_gt_ready")
    pv_ps = st.sem("q_pv_in_psum")
    pv_ready = st.sem("q_pv_ready")
    r1_ready = st.sem("q_r1_ready")
    n1_ready = st.sem("q_n1_ready")
    g1_ready = st.sem("q_g1_ready")
    o1_ready = st.sem("q_o1_ready")
    o1_kept = st.sem("q_o1_kept")
    o1t_ps = st.sem("q_o1t_in_psum")
    o1t_ready = st.sem("q_o1t_ready")
    down_ps = st.sem("q_down_in_psum")
    f_ready = st.sem("q_f_ready")
    n2_ready = st.sem("q_n2_ready")
    g2_ready = st.sem("q_g2_ready")
    o2_ready = st.sem("q_o2_ready")
    x_done = st.sem("q_x_done")
    q_ready = st.sem("q_q_in_psum")
    dd_ready = st.sem("q_dd_in_psum")
    sq_ready = st.sem("q_squares_ready")
    ssq_ready = st.sem("q_ssq_ready")
    mx_ready = st.sem("q_mx_ready")
    c_ready = st.sem("q_c_ready")
    e_ready = st.sem("q_e_ready")
    exp_done = st.sem("q_exp_done")
    turned = st.sem("q_features_in_psum")
    qf_ready = st.sem("q_features_ready")
    den_ps = st.sem("q_den_in_psum")
    rec_ready = st.sem("q_rec_ready")
    wide_ready = st.sem("q_wide_ready")
    spread = st.sem("q_rec_spread")
    scaled = st.sem("q_features_scaled")
    out_ps = st.sem("q_attention_in_psum")
    up_ps = st.sem("q_up_in_psum")
    neg_ready = st.sem("q_neg_ready")
    pos_ready = st.sem("q_pos_ready")
    elu_exp = st.sem("q_elu_exp_done")
    h_ready = st.sem("q_h_ready")

    def is_batch(b):
        return not isinstance(b, int) or 0 <= b < BATCHES

    def is_tile(n):
        return not isinstance(n, int) or 0 <= n < TILES

    def batches(eng, batch):
        for b in (-1, 0, 1):
            batch(b)
        with eng.Fori(2, BATCHES - 1) as b:
            batch(b)
        for b in (BATCHES - 1, BATCHES, BATCHES + 1):
            batch(b)

    def wide_row(name):
        return w[name][:].rearrange("p (o e) -> p o e", o=1).to_broadcast([P, QT, P])

    with nc.Block() as block:
        @block.gpsimd
        def _(pool):
            g = nc.gpsimd

            def batch(b):
                if is_batch(b + 1):
                    at(pool, yt_ps, b + 1)
                    g.tensor_copy(y[:], tiles_of(y_all, b + 1)).then_inc(y_ready, 1)
                if is_batch(b - 1):
                    norm1.pool(pool, b - 1)
                    pool.wait_ge(n1_ready, b)
                    g.tensor_tensor(r1[:], r1[:], wide_row("ln1_g"), ALU.mult).then_inc(g1_ready, 1)
                    pool.wait_ge(g1_ready, b)
                    at(pool, o1t_ps, b - 1)
                    g.tensor_tensor(o1[:], r1[:], wide_row("ln1_b"), ALU.add).then_inc(o1_ready, 1)
                    pool.wait_ge(o1_ready, b)
                    at(pool, f_ready, b - 1)
                    g.tensor_tensor(kept[:], o1[:], wide_row("b2"), ALU.add).then_inc(o1_kept, 1)
                if is_batch(b - 2):
                    norm2.pool(pool, b - 2)
                    pool.wait_ge(n2_ready, b - 1)
                    g.tensor_tensor(f2[:], f2[:], wide_row("ln2_g"), ALU.mult).then_inc(g2_ready, 1)
                    pool.wait_ge(g2_ready, b - 1)
                    g.tensor_tensor(f2[:], f2[:], wide_row("ln2_b"), ALU.add).then_inc(o2_ready, 1)
                    pool.wait_ge(o2_ready, b - 1)
                    g.tensor_tensor(gate[:], c["minus"][0:1, :], c["minus"][0:1, :], ALU.mult)
                    g.tensor_tensor(tiles_of(x_res, b - 2), tiles_of(x_res, b - 2), f2[:], ALU.add).then_inc(x_done, 1)

            pool.sem_inc(x_done, 1)
            batches(pool, batch)

        @block.vector
        def _(dve):
            v = nc.vector
            dd = ps[:, 2:4, :].rearrange("p a (h m) -> p (a h) m", m=PM)

            def maximum(n):
                if is_tile(n):
                    dve.wait_ge(dd_ready, n + 1)
                    v.tensor_reduce(mx[:], dd, AX.X, ALU.max).then_inc(mx_ready, 1)

            def exponent(n, i):
                if is_tile(n):
                    dve.wait_ge(sq_ready, n + 1)
                    v.tensor_reduce(ssq[:], sq[:].rearrange("p (h k) -> p h k", h=PH), AX.X, ALU.add).then_inc(ssq_ready, 1)
                    dve.wait_ge(mx_ready, n + 1)
                    dve.wait_ge(ssq_ready, n + 1)
                    v.scalar_tensor_tensor(cc[:], ssq[:], 1.0 / 16, mx[:], ALU.mult, ALU.add).then_inc(c_ready, 1)
                    dve.wait_ge(c_ready, n + 1)
                    at(dve, turned, n - 1)
                    v.tensor_tensor(e[:, i % 2, :].rearrange("p (h m) -> p h m", h=PH), dd,
                                    cc[:].rearrange("p (h o) -> p h o", o=1).to_broadcast([P, PH, PM]),
                                    ALU.subtract).then_inc(e_ready, 1)

            def reciprocal(n):
                if is_tile(n):
                    dve.wait_ge(den_ps, n + 1)
                    at(dve, wide_ready, n)
                    v.reciprocal(rec[:], ps[:, 4, 0:PH]).then_inc(rec_ready, 1)

            def scale(n, i):
                if is_tile(n):
                    dve.wait_ge(spread, n + 1)
                    mine = qf[:, i % 2, :, :].rearrange("p c e -> p (c e)")
                    v.tensor_tensor(mine, mine, ps[:, 4:6, :].rearrange("p a b -> p (a b)"), ALU.mult).then_inc(scaled, 1)

            def keys_sums(b):
                v.tensor_scalar(es[:], flat(ysum[:, bass.ds(b, 1), :]), EPS_KERN, None, ALU.mult).then_inc(es_ready, 1)
                dve.wait_ge(es_ready, b + 1)
                at(dve, gt_ps, b)
                v.scalar_tensor_tensor(
                    gf[:], sums[:, bass.ds(b, 1), :].rearrange("p a (c e) -> p (a c) e", c=CH),
                    shift[:, bass.ds(b, 1)], es[:].rearrange("p (o e) -> p o e", o=1).to_broadcast([P, CH, A]),
                    ALU.mult, ALU.add).then_inc(gf_ready, 1)
                dve.wait_ge(gf_ready, b + 1)
                v.tensor_tensor(tiles_of(ksd, b, CH), w["mask"][:], gf[:, :, P:A].to_broadcast([P, CH, PH]),
                                ALU.mult).then_inc(ksd_ready, 1)

            def negatives(b, pair):
                for f in (pair, pair + 1):
                    dve.wait_ge(up_ps, b * FC + (f + 1))
                    dve.wait_ge(h_ready, b * FC + (pair + 1))
                    v.tensor_scalar(neg[:, f % 2, :], ps[:, f % 2, :], w["b1"][:, f:f + 1], 0.0,
                                    ALU.add, ALU.min).then_inc(neg_ready, 1)

            def elus(b, pair):
                dve.wait_ge(down_ps, b + 1)
                for f in (pair, pair + 1):
                    dve.wait_ge(elu_exp, b * FC + (f + 1))
                    dve.wait_ge(pos_ready, b * FC + (f + 1))
                    v.scalar_tensor_tensor(ht[:, f, :], neg[:, f % 2, :], -1.0, pos[:, f % 2, :],
                                           ALU.add, ALU.add).then_inc(h_ready, 1)

            def batch(b):
                n = b * QT
                first = [r1[:, i, :] for i in range(QT)]
                second = [f2[:, i, :] for i in range(QT)]
                maximum(n)
                scale(n - 2, 0)
                exponent(n, 0)
                reciprocal(n - 1)
                if is_batch(b - 2):
                    negatives(b - 2, 0)
                if is_batch(b + 1):
                    keys_sums(b + 1)
                maximum(n + 1)
                scale(n - 1, 1)
                if is_batch(b - 2):
                    elus(b - 2, 0)
                exponent(n + 1, 1)
                reciprocal(n)
                if is_batch(b - 2):
                    negatives(b - 2, 2)
                maximum(n + 2)
                scale(n, 0)
                if is_batch(b - 2):
                    elus(b - 2, 2)
                if is_batch(b - 1):
                    dve.wait_ge(out_ps, n)
                    at(dve, o1_ready, b - 1)
                    v.tensor_tensor(r1[:], tiles_of(y_all, b - 1),
                                    ps[:, 6, :].rearrange("p (i e) -> p i e", i=QT), ALU.add).then_inc(r1_ready, 1)
                    dve.wait_ge(r1_ready, b)
                    take_statistics(norm1, dve, b - 1, first)
                exponent(n + 2, 2)
                if is_batch(b - 1):
                    normalise(norm1, dve, b - 1, first, first).then_inc(n1_ready, 1)
                reciprocal(n + 1)
                maximum(n + 3)
                scale(n + 1, 1)
                if is_batch(b - 2):
                    dve.wait_ge(down_ps, b)
                    dve.wait_ge(o1_kept, b - 1)
                    dve.wait_ge(x_done, b - 1)
                    v.tensor_tensor(f2[:], kept[:], ps[:, 7, :].rearrange("p (i e) -> p i e", i=QT),
                                    ALU.add).then_inc(f_ready, 1)
                    dve.wait_ge(f_ready, b - 1)
                    take_statistics(norm2, dve, b - 2, second)
                exponent(n + 3, 3)
                if is_batch(b - 2):
                    normalise(norm2, dve, b - 2, second, second).then_inc(n2_ready, 1)
                reciprocal(n + 2)

            v.reduce_max(gmax[:], peak[:], AX.X).then_inc(gmax_ready, 1)
            dve.wait_ge(gmax_ready, 1)
            v.tensor_scalar(shift[:], peak[:], gmax[:], None, ALU.subtract).then_inc(gap_ready, 1)
            dve.wait_ge(shift_ready, 1)
            dve.sem_inc(h_ready, 1)
            batches(dve, batch)

        @block.scalar
        def _(act):
            s = nc.scalar

            def square(n):
                if is_tile(n):
                    act.wait_ge(q_ready, n + 1)
                    at(act, ssq_ready, n)
                    s.activation(sq[:], ps[:, 0:2, :].rearrange("p a b -> p (a b)"), ACT.Square).then_inc(sq_ready, 1)

            def features(n, i):
                if is_tile(n):
                    act.wait_ge(turned, n + 1)
                    at(act, out_ps, n - 1)
                    s.activation(qf[:, i % 2, :, :], ps[:, 4:6, :].rearrange("p a (c e) -> p (a c) e", e=P),
                                 ACT.Identity, bias=w["eps"][:, 0:1]).then_inc(qf_ready, 1)

            def exponential(n, i):
                if is_tile(n):
                    act.wait_ge(e_ready, n + 1)
                    s.activation(e[:, i % 2, :], e[:, i % 2, :], ACT.Exp).then_inc(exp_done, 1)

            def widen(n):
                if is_tile(n):
                    act.wait_ge(rec_ready, n + 1)
                    at(act, spread, n)
                    s.copy(wide[:].rearrange("p (h m) -> p h m", h=PH),
                           rec[:].rearrange("p (h o) -> p h o", o=1).to_broadcast([P, PH, PM])).then_inc(wide_ready, 1)

            def elu_parts(b, pair):
                if is_batch(b):
                    for f in (pair, pair + 1):
                        act.wait_ge(neg_ready, b * FC + (f + 1))
                        s.activation(pos[:, f % 2, :], ps[:, f % 2, :], ACT.Relu, bias=w["b1"][:, f:f + 1]).then_inc(pos_ready, 1)
                    for f in (pair, pair + 1):
                        s.activation(neg[:, f % 2, :], neg[:, f % 2, :], ACT.Exp).then_inc(elu_exp, 1)

            def batch(b):
                n = b * QT
                square(n)
                features(n - 1, 1)
                exponential(n, 0)
                widen(n - 1)
                elu_parts(b - 2, 0)
                square(n + 1)
                features(n, 0)
                exponential(n + 1, 1)
                widen(n)
                elu_parts(b - 2, 2)
                square(n + 2)
                features(n + 1, 1)
                if is_batch(b + 1):
                    act.wait_ge(gt_ps, b + 2)
                    s.copy(gt[:], ps[:, 0:2, :].rearrange("p a b -> p (a b)")).then_inc(gt_ready, 1)
                exponential(n + 2, 0)
                widen(n + 1)
                square(n + 3)
                if is_batch(b + 1):
                    act.wait_ge(yt_ps, b + 2)
                    s.copy(yt[:], ps[:, 7, :]).then_inc(yt_ready, 1)
                features(n + 2, 0)
                if is_batch(b + 1):
                    act.wait_ge(pv_ps, b + 2)
                    s.copy(flat(sums[:, bass.ds(b + 1, 1), 0:CH * P]),
                           ps[:, 0:2, :].rearrange("p a b -> p (a b)")).then_inc(pv_ready, 1)
                exponential(n + 3, 1)
                widen(n + 2)
                if is_batch(b - 1):
                    act.wait_ge(o1t_ps, b)
                    s.copy(o1t[:], ps[:, 7, :]).then_inc(o1t_ready, 1)

            act.wait_ge(gap_ready, 1)
            s.activation(shift[:], shift[:], ACT.Exp).then_inc(shift_ready, 1)
            batches(act, batch)

        @block.tensor
        def _(pe):
            def fill_used(b, i):
                if i == 0 and is_batch(b):
                    at(pe, pv_ready, b + 1)
                if i in (1, 2) and is_batch(b - 2):
                    pe.wait_ge(pos_ready, (b - 2) * FC + 2 * i)
                if i == 3 and is_batch(b + 1):
                    pe.wait_ge(gt_ready, b + 2)

            def spread_out(n):
                if is_tile(n):
                    pe.wait_ge(wide_ready, n + 1)
                    for j in range(CH):
                        last = nc.tensor.transpose(ps[:, 4 + j // 4, (j % 4) * P:(j % 4 + 1) * P],
                                                   wide[:, j * P:(j + 1) * P], c["ident"][:])
                    last.then_inc(spread, 1)

            def products(b, n, i):
                if is_tile(n):
                    tile = yt[:, i * P:(i + 1) * P]
                    pe.wait_ge(yt_ready, b + 1)
                    at(pe, e_ready, n)
                    for half in range(2):
                        last = nc.tensor.matmul(ps[:, 2 + half, :], tile, w["wqp"][:, half * 512:(half + 1) * 512],
                                                start=True, stop=True)
                    last.then_inc(dd_ready, 1)
                spread_out(n - 2)
                if is_tile(n):
                    at(pe, sq_ready, n)
                    fill_used(b, i)
                    for half in range(2):
                        last = nc.tensor.matmul(ps[:, half, :], tile, w["wq"][:, half * 512:(half + 1) * 512],
                                                start=True, stop=True)
                    last.then_inc(q_ready, 1)

            def before_fill(b, n, i):
                if is_tile(n):
                    pe.wait_ge(sq_ready, n + 1)
                else:
                    fill_used(b, i)

            def turn(n, i):
                if is_tile(n):
                    pe.wait_ge(exp_done, n + 1)
                    at(pe, scaled, n)
                    for j in range(CH):
                        last = nc.tensor.transpose(ps[:, 4 + j // 4, (j % 4) * P:(j % 4 + 1) * P],
                                                   e[:, i % 2, j * P:(j + 1) * P], c["ident"][:])
                    last.then_inc(turned, 1)

            def denominators(b, n, i):
                if is_tile(n):
                    pe.wait_ge(qf_ready, n + 1)
                    pe.wait_ge(ksd_ready, b + 1)
                    ks = tiles_of(ksd, b, CH)
                    for j in range(CH):
                        last = nc.tensor.matmul(ps[:, 4, 0:PH], qf[:, i % 2, j, :], ks[:, j, :],
                                                start=j == 0, stop=j == CH - 1)
                    last.then_inc(den_ps, 1)

            def attend(b, n, i):
                if is_tile(n):
                    pe.wait_ge(scaled, n + 1)
                    pe.wait_ge(pv_ready, b + 1)
                    if i == 0:
                        at(pe, r1_ready, b)
                    pv = sums[:, bass.ds(b, 1), 0:CH * P].rearrange("p a (c e) -> p (a c) e", c=CH)
                    for j in range(CH):
                        last = nc.tensor.matmul(ps[:, 6, i * P:(i + 1) * P], qf[:, i % 2, j, :], pv[:, j, :],
                                                start=j == 0, stop=j == CH - 1)
                    last.then_inc(out_ps, 1)

            def up(b, pair):
                pe.wait_ge(o1t_ready, b + 1)
                for f in (pair, pair + 1):
                    nc.tensor.matmul(ps[:, f % 2, :], w["w1"][:, f * P:(f + 1) * P], o1t[:],
                                     start=True, stop=True).then_inc(up_ps, 1)

            def batch(b):
                n = b * QT
                products(b, n, 0)
                turn(n - 1, 1)
                if is_batch(b - 2):
                    before_fill(b, n, 0)
                    up(b - 2, 0)
                denominators(b - 1, n - 1, 3)
                attend(b - 1, n - 2, 2)
                products(b, n + 1, 1)
                turn(n, 0)
                if is_batch(b - 2):
                    before_fill(b, n + 1, 1)
                    up(b - 2, 2)
                denominators(b, n, 0)
                attend(b - 1, n - 1, 3)
                products(b, n + 2, 2)
                turn(n + 1, 1)
                if is_batch(b + 1):
                    before_fill(b, n + 2, 2)
                    pe.wait_ge(gf_ready, b + 2)
                    for j in range(CH):
                        last = nc.tensor.transpose(ps[:, j // 4, (j % 4) * P:(j % 4 + 1) * P], gf[:, j, 0:P], c["ident"][:])
                    last.then_inc(gt_ps, 1)
                denominators(b, n + 1, 1)
                attend(b, n, 0)
                if is_batch(b - 2):
                    pe.wait_ge(h_ready, (b - 2) * FC + (FC + 1))
                    for i in range(QT):
                        for f in range(FC):
                            last = nc.tensor.matmul(ps[:, 7, i * P:(i + 1) * P], ht[:, f, i * P:(i + 1) * P], w["w2"][:, f, :],
                                                    start=f == 0, stop=f == FC - 1)
                    last.then_inc(down_ps, 1)
                products(b, n + 3, 3)
                if is_batch(b + 1):
                    pe.wait_ge(y_ready, b + 2)
                    if is_batch(b - 2):
                        pe.wait_ge(f_ready, b - 1)
                    elif is_batch(b - 1):
                        pe.wait_ge(o1t_ready, b - 1)
                    for i in range(QT):
                        last = nc.tensor.transpose(ps[:, 7, i * P:(i + 1) * P], y[:, i, :], c["ident"][:])
                    last.then_inc(yt_ps, 1)
                turn(n + 2, 0)
                if is_batch(b + 1):
                    before_fill(b, n + 3, 3)
                    pe.wait_ge(gt_ready, b + 2)
                    for h in range(PH):
                        r, j = (h % 2) * PM, h // 2
                        last = nc.tensor.matmul(ps[r:r + PM, j // 4, (j % 4) * P:(j % 4 + 1) * P],
                                                gt[:, h * PM:(h + 1) * PM], w["wvo"][:, h, :], start=True, stop=True)
                    last.then_inc(pv_ps, 1)
                denominators(b, n + 2, 2)
                attend(b, n + 1, 1)
                if is_batch(b - 1):
                    pe.wait_ge(o1_ready, b)
                    if is_batch(b + 1):
                        pe.wait_ge(yt_ready, b + 2)
                    elif is_batch(b - 2):
                        pe.wait_ge(f_ready, b - 1)
                    for i in range(QT):
                        last = nc.tensor.transpose(ps[:, 7, i * P:(i + 1) * P], o1[:, i, :], c["ident"][:])
                    last.then_inc(o1t_ps, 1)

            pe.sem_inc(down_ps, 1)
            batches(pe, batch)


def attention_memory(nc, st, name):
    a = {}
    a["q_dram"] = nc.dram_tensor(name + "_q_stacks", [BATCHES, P, PARTS, SEQ], BF16, kind="Internal").ap()
    a["k_dram"] = nc.dram_tensor(name + "_k_stacks", [BATCHES, PARTS, P, PARTS, SEQ], BF16, kind="Internal").ap()
    a["qs"] = st.sb(name + "_q_stack", [P, GROUPS, GH, SEQ], BF16)
    a["ks"] = st.sb(name + "_k_stack", [P, GROUPS, GH, SEQ], BF16)
    a["vs"] = st.sb(name + "_v_stack", [P, GROUPS, QT, GH, 32])
    a["pt"] = st.sb(name + "_probs_t", [P, 4, 2, SEQ])
    a["ot"] = st.sb(name + "_out_t", [P, SEQ])
    a["mx"] = st.sb(name + "_row_max", [P, 2, GH * QT])
    a["mp"] = st.sb(name + "_max_parts", [GH * QT, 2, PARTS, P], BF16)
    a["mr"] = st.sb(name + "_max_rest", [GH * QT, P])
    a["rec"] = st.sb(name + "_recip_sum", [P, QT, GH, 1])
    a["y"] = st.sb(name + "_front_y", [P, QT, P])
    a["z"] = st.sb(name + "_front_z", [P, QT, P])
    a["ht"] = st.sb(name + "_front_ht", [P, SEQ])
    a["full"] = st.sb(name + "_front_qk", [P, 2, SEQ])
    a["rest"] = st.sb(name + "_front_rest", [P, 2, SEQ])
    a["parts"] = st.sb(name + "_front_parts", [P, 2, 2, PARTS, SEQ], BF16)
    constants = st.sem(name + "_stack_constants")
    with nc.Block() as block:
        @block.vector
        def _(dve):
            nc.vector.memset(a["ks"][64:P, :, :, :], 1.0)
            nc.vector.memset(a["vs"][:], 0.0).then_inc(constants, 1)
            dve.wait_ge(constants, 1)
            nc.vector.memset(a["vs"][:, :, :, :, HD:HD + 1], 1.0)
    return a


def load_attention_weights(nc, d, c, name, rope, st, layer):
    if layer == 2:
        return c["ffn"]
    w = {}
    pre = "L0_attn_b_w" if rope else "L0_ffn_W"
    loads = []

    def add(key, shape, src):
        w[key] = st.sb(f"{name}_{key}", shape)
        loads.append((w[key], src))

    def column(v):
        return v.rearrange("(p o) -> p o", o=1)

    for n in "qkvo":
        add("w" + n, [P, P], d[pre + n])
    if rope:
        add("cos", [P, SEQ], d["rope_cos"])
        add("sin", [P, SEQ], d["rope_sin"])
        add("bq", [P, 1], column(d["L0_attn_b_bq"]))
        add("bk", [P, 1], column(d["L0_attn_b_bk"]))
        add("bv", [P, P], d["L0_attn_b_bv"].partition_broadcast(P))
        add("bo", [P, P], d["L0_attn_b_bo"].partition_broadcast(P))
        for n in "qk":
            w["w" + n + "s"] = st.sb(f"{name}_w{n}s", [P, P])
            w["b" + n + "s"] = st.sb(f"{name}_b{n}s", [P, 1])
    else:
        for n in ("ln1_g", "ln1_b", "ln2_g", "ln2_b"):
            add(n, [P, 1], column(d["L0_ffn_" + n]))
        add("wg", [P, EXPERTS], d["L0_ffn_Wg"])
        add("w1", [P, EXPERTS, FF], d["L0_ffn_W1"].rearrange("e p f -> p e f"))
        add("w2", [P, EXPERTS * FC, P], d["L0_ffn_W2"].rearrange("e (c p) o -> p (e c) o", p=P))
        add("b2", [EXPERTS, P], d["L0_ffn_b2"])
        add("b1r", [EXPERTS * FC, P], d["L0_ffn_b1"].rearrange("e (c p) -> (e c) p", p=P))
        add("rev", [P, QT, EXPERTS], d["expert_rank"])
        w["b1"] = st.sb(f"{name}_b1", [P, EXPERTS * FC])
        c["ffn"] = w
    loaded = st.sem(name + "_w_loaded")
    turned = st.sem(name + "_b1_turned")
    n_loads = len(loads) + (4 if rope else 0)
    ps = st.ctx.enter_context(ExitStack())
    with nc.Block() as block:
        @block.sync
        def _(sp):
            for dst, src in loads:
                sp.dma_start(dst[:], src).then_inc(loaded, 16)
            if rope:
                for n in "qk":
                    pairs = d["L0_attn_b_b" + n].rearrange("(a two o) -> a two o", two=2, o=1)
                    dst = w["b" + n + "s"]
                    for half in range(2):
                        sp.dma_start(dst[half:P:2, :], pairs[:, 1 - half, :], allow_slow_non_contiguous=True).then_inc(loaded, 16)
            sp.wait_ge(loaded, 16 * n_loads)

        if rope:
            @block.vector
            def _(dve):
                dve.wait_ge(loaded, 16 * n_loads)
                for n in "qk":
                    src = w["w" + n][:].rearrange("p (a two) -> p a two", two=2)
                    dst = w["w" + n + "s"][:].rearrange("p (a two) -> p a two", two=2)
                    for half in range(2):
                        nc.vector.tensor_copy(dst[:, :, half], src[:, :, 1 - half])
        else:
            @block.tensor
            def _(pe):
                pe.wait_ge(loaded, 16 * n_loads)
                nc.tensor.transpose(c["ps"][:, 0, 0:EXPERTS * FC], w["b1r"][:], c["ident"][0:EXPERTS * FC, 0:EXPERTS * FC]).then_inc(turned, 1)

            @block.vector
            def _(dve):
                dve.wait_ge(turned, 1)
                nc.vector.tensor_copy(w["b1"][:], c["ps"][:, 0, 0:EXPERTS * FC])
    return w


def attention_front(nc, name, rope, c, w, a, ps, x_res, y_all, v_all):
    mem = ExitStack()
    st = Store(nc, mem)
    name += "f_"
    norm = Norm(st, c, name + "norm", 1e-5)
    norms = 1 if rope else 2
    y, z, ht, full, rest, parts = (a[n] for n in ("y", "z", "ht", "full", "rest", "parts"))
    if rope:
        z = y
    y_ready = st.sem(name + "y_ready")
    y_saved = st.sem(name + "y_saved")
    z_ready = st.sem(name + "z_ready")
    zt_ps = st.sem(name + "zt_in_psum")
    ht_ready = st.sem(name + "ht_ready")
    qk_ps = st.sem(name + "qk_in_psum")
    v_ps = st.sem(name + "v_in_psum")
    v_saved = st.sem(name + "v_saved")
    full_ready = st.sem(name + "qk_ready")
    turn_step = st.sem(name + "rope_step")
    part1 = st.sem(name + "part1_ready")
    rest_ready = st.sem(name + "rest_ready")
    part2 = st.sem(name + "part2_ready")
    part3 = st.sem(name + "part3_ready")
    sent = [st.sem(f"{name}stacks_sent{par}") for par in range(2)]
    SENDS = 1 + PARTS

    with nc.Block() as block:
        @block.vector
        def _(dve):
            ys = [y[:, i, :] for i in range(QT)]
            zs = [z[:, i, :] for i in range(QT)]

            def measure_x(b):
                take_statistics(norm, dve, b * norms, [tile_of(x_res, b * QT + i) for i in range(QT)])

            def norm_x(b, first=False):
                if not first:
                    dve.wait_ge(zt_ps if rope else y_saved, b)
                normalise(norm, dve, b * norms, [tile_of(x_res, b * QT + i) for i in range(QT)],
                           ys).then_inc(z_ready if rope else y_ready, 1)

            def measure_y(b):
                dve.wait_ge(y_ready, b + 1)
                take_statistics(norm, dve, b * 2 + 1, ys)

            def norm_y(b, first=False):
                if not first:
                    dve.wait_ge(zt_ps, b)
                normalise(norm, dve, b * 2 + 1, ys, zs).then_inc(z_ready, 1)

            def rotate(b):
                dve.wait_ge(qk_ps, b + 1)
                for x in range(2):
                    bias, other = w["bq" if x == 0 else "bk"], w["bqs" if x == 0 else "bks"]
                    nc.vector.scalar_tensor_tensor(full[:, x, :], ps[:, 1 + x, :], bias[:, 0:1], w["cos"][:],
                                                   ALU.add, ALU.mult)
                    nc.vector.scalar_tensor_tensor(rest[:, x, :], ps[:, 4 + x, :], other[:, 0:1], w["sin"][:],
                                                   ALU.add, ALU.mult).then_inc(turn_step, 1)
                for x in range(2):
                    dve.wait_ge(turn_step, b * 2 + (x + 1))
                    nc.vector.tensor_tensor(full[:, x, :], full[:, x, :], rest[:, x, :], ALU.add).then_inc(full_ready, 1)
                dve.wait_ge(v_ps, b + 1)
                nc.vector.tensor_tensor(tiles_of(v_all, b), ps[:, 3, :].rearrange("p (i e) -> p i e", i=QT),
                                        w["bv"][:].rearrange("p (o e) -> p o e", o=1).to_broadcast([P, QT, P]),
                                        ALU.add).then_inc(v_saved, 1)
                dve.wait_ge(full_ready, b * 2 + 3)

            def second_part(b, par):
                for x in range(2):
                    dve.wait_ge(part1, b * 2 + (x + 1))
                    nc.vector.tensor_tensor(rest[:, x, :], full[:, x, :], parts[:, par, x, 0, :], ALU.subtract).then_inc(rest_ready, 1)

            def third_part(b, par):
                for x in range(2):
                    dve.wait_ge(part2, b * 2 + (x + 1))
                    nc.vector.tensor_tensor(parts[:, par, x, 2, :], rest[:, x, :], parts[:, par, x, 1, :],
                                            ALU.subtract).then_inc(part3, 1)
                dve.wait_ge(part3, b * 2 + 2)

            if rope:
                dve.sem_inc(full_ready, 1)
                dve.sem_inc(v_saved, 1)
            dve.sem_inc(rest_ready, 1)
            measure_x(0)
            norm_x(0, True)
            if not rope:
                measure_y(0)
                norm_y(0, True)
            def batch(b, par):
                measure_x(b + 1)
                if not rope:
                    norm_x(b + 1)
                    measure_y(b + 1)
                if not isinstance(b, int) or b > 0:
                    third_part(b - 1, 1 - par)
                if rope:
                    norm_x(b + 1)
                    rotate(b)
                else:
                    norm_y(b + 1)
                second_part(b, par)

            batch(0, 0)
            with nc.vector.Fori(0, BATCHES // 2 - 1) as u:
                for par in (1, 0):
                    batch(u * 2 + (2 - par), par)
            third_part(BATCHES - 2, 0)
            if rope:
                rotate(BATCHES - 1)
            second_part(BATCHES - 1, 1)
            third_part(BATCHES - 1, 1)

        @block.gpsimd
        def _(pool):
            with nc.gpsimd.Fori(0, BATCHES) as b:
                for i in range(norms):
                    norm.pool(pool, b * norms + i)
                if not rope:
                    pool.wait_ge(y_ready, b + 1)
                    nc.gpsimd.tensor_copy(tiles_of(y_all, b), y[:]).then_inc(y_saved, 1)

        @block.scalar
        def _(act):
            if not rope:
                act.sem_inc(full_ready, 1)
                act.sem_inc(v_saved, 1)

            def batch(u, par):
                b = u * 2 + par
                act.wait_ge(zt_ps, b + 1)
                if rope:
                    nc.scalar.copy(ht[:], ps[:, 0, :]).then_inc(ht_ready, 1)
                else:
                    nc.scalar.activation(ht[:], ps[:, 0, :], ACT.Identity, bias=w["ln1_b"][:, 0:1],
                                         scale=w["ln1_g"][:, 0:1]).then_inc(ht_ready, 1)
                    act.wait_ge(qk_ps, b + 1)
                    act.wait_ge(rest_ready, b * 2 + 1)
                    for x in range(2):
                        nc.scalar.copy(full[:, x, :], ps[:, 1 + x, :]).then_inc(full_ready, 1)
                act.wait_ge(sent[par], u * (16 * SENDS) + 1)
                for x in range(2):
                    act.wait_ge(full_ready, b * 2 + (x + 2))
                    nc.scalar.copy(parts[:, par, x, 0, :], full[:, x, :]).then_inc(part1, 1)
                if not rope:
                    act.wait_ge(v_ps, b + 1)
                    nc.scalar.copy(tiles_of(v_all, b), ps[:, 3, :].rearrange("p (i e) -> p i e", i=QT)).then_inc(v_saved, 1)
                for x in range(2):
                    act.wait_ge(rest_ready, b * 2 + (x + 2))
                    nc.scalar.copy(parts[:, par, x, 1, :], rest[:, x, :]).then_inc(part2, 1)

            with nc.scalar.Fori(0, BATCHES // 2) as u:
                for par in range(2):
                    batch(u, par)

        @block.tensor
        def _(pe):
            with nc.tensor.Fori(0, BATCHES) as b:
                pe.wait_ge(z_ready, b + 1)
                for i in range(QT):
                    last = nc.tensor.transpose(ps[:, 0, i * P:(i + 1) * P], z[:, i, :], c["ident"][:])
                last.then_inc(zt_ps, 1)
                pe.wait_ge(ht_ready, b + 1)
                pe.wait_ge(full_ready, b * 2 + 1)
                for x, m in enumerate(("wq", "wk")):
                    last = nc.tensor.matmul(ps[:, 1 + x, :], w[m][:], ht[:], start=True, stop=True)
                    if rope:
                        last = nc.tensor.matmul(ps[:, 4 + x, :], w[m + "s"][:], ht[:], start=True, stop=True)
                last.then_inc(qk_ps, 1)
                pe.wait_ge(v_saved, b + 1)
                for i in range(QT):
                    last = nc.tensor.matmul(ps[:, 3, i * P:(i + 1) * P], ht[:, i * P:(i + 1) * P], w["wv"][:],
                                            start=True, stop=True)
                last.then_inc(v_ps, 1)

        @block.sync
        def _(sp):
            for par in range(2):
                sp.sem_inc(sent[par], 1)
            q_pairs = a["q_dram"].rearrange("(u two) d i t -> u two d i t", two=2)
            k_pairs = a["k_dram"].rearrange("(u two) j d i t -> u two j d i t", two=2)
            with nc.sync.Fori(0, BATCHES // 2) as u:
                for par in range(2):
                    b = u * 2 + par
                    sp.wait_ge(part3, b * 2 + 2)
                    sp.dma_start(q_pairs[bass.ds(u, 1), par, :, :, :].rearrange("a d i t -> (a d) i t"),
                                 parts[:, par, 0, :, :]).then_inc(sent[par], 16)
                    for i in range(PARTS):
                        sp.dma_start(k_pairs[bass.ds(u, 1), par, :, :, i, :].rearrange("a j d t -> d (a j) t"),
                                     parts[:, par, 1, :, :]).then_inc(sent[par], 16)
            for par in range(2):
                sp.wait_ge(sent[par], 16 * SENDS * (BATCHES // 2) + 1)
    st.clear()
    mem.close()


def attention_main(nc, name, causal, c, a, ps, v_all, ctx_all):
    st = Store(nc, ExitStack())
    name += "m_"
    qs, ks, vs, pt, ot, mx, mp, mr, rec = (a[n] for n in ("qs", "ks", "vs", "pt", "ot", "mx", "mp", "mr", "rec"))
    UNITS = 2 * QT
    MAXES = GH * QT
    OUT_BANK, MISC = 6, 7
    scale = HD ** -0.5
    loaded = [st.sem(f"{name}stacks_loaded{g}") for g in range(GROUPS)]
    m_loaded = [st.sem(f"{name}max_loaded{g}") for g in range(GROUPS)]
    s_ready = st.sem(name + "scores_ready")
    max_done = st.sem(name + "max_done")
    mt_ready = st.sem(name + "max_transposed")
    m_step = st.sem(name + "max_split_step")
    m_split = st.sem(name + "max_split")
    st_ready = st.sem(name + "scores_t_ready")
    exp_done = st.sem(name + "exp_done")
    vs_ready = st.sem(name + "v_ready")
    pv_done = st.sem(name + "pv_done")
    ot_ready = st.sem(name + "out_copied")
    ott_ready = st.sem(name + "out_transposed")
    rec_ready = st.sem(name + "recip_ready")
    ctx_done = st.sem(name + "ctx_done")

    def keys(i):
        return (i + 1) * P if causal else SEQ

    def first_query(kt):
        return kt * P if causal else 0

    def steps(eng, step):
        step(0, 0)
        with eng.Fori(0, BATCHES - 1) as b:
            for g in range(GROUPS):
                step(b * GROUPS + (g + 1), (g + 1) % GROUPS)
        for t in range(STEPS - 3, STEPS):
            step(t, t % GROUPS)

    def has(t, ahead):
        return not isinstance(t, int) or 0 <= t + ahead < STEPS

    with nc.Block() as block:
        @block.sync
        def _(sp):
            def load(b, g):
                mine = slice(g * GH * HD, (g + 1) * GH * HD)
                for j in range(PARTS):
                    rows = slice(j * HD * PARTS, (j + 1) * HD * PARTS)
                    sp.dma_start(qs[rows, g, :, :], a["q_dram"][bass.ds(b, 1), mine, :, :].rearrange(
                        "a (h e) i t -> (a e i) h t", h=GH)).then_inc(loaded[g], 16)
                    sp.dma_start(ks[rows, g, :, :], a["k_dram"][bass.ds(b, 1), j, mine, :, :].rearrange(
                        "a (h e) i t -> (a e i) h t", h=GH)).then_inc(loaded[g], 16)

            def send_max(s, g):
                sp.wait_ge(m_split, s + 1)
                for i in range(PARTS):
                    sp.dma_start(qs[ROWS + i:ROWS + i + 1, g, :, :].rearrange("p h (i q) -> p (h i) q", i=QT),
                                 mp[:, g % 2, i, :]).then_inc(m_loaded[g], 16)

            for g in range(GROUPS):
                load(0, g)
            send_max(0, 0)
            with nc.sync.Fori(0, BATCHES - 1) as b:
                for g in range(GROUPS):
                    t = b * GROUPS + g
                    send_max(t + 1, (g + 1) % GROUPS)
                    sp.wait_ge(st_ready, (t + 1) * UNITS)
                    load(b + 1, g)
            for t in range(STEPS - GROUPS, STEPS - 1):
                send_max(t + 1, (t + 1) % GROUPS)
            for g in range(GROUPS):
                sp.wait_ge(m_loaded[g], 16 * PARTS * BATCHES)

        @block.gpsimd
        def _(pool):
            def v_stack(b, g, wait):
                if wait:
                    pool.wait_ge(pv_done, (b * GROUPS + (g - GROUPS + 1)) * QT)
                last = nc.gpsimd.tensor_copy(
                    vs[:, g, :, :, 0:HD],
                    tiles_of(v_all, b)[:, :, g * GH * HD:(g + 1) * GH * HD].rearrange("p i (h e) -> p i h e", h=GH))
                last.then_inc(vs_ready, 1)

            for g in range(GROUPS):
                v_stack(0, g, False)
            with nc.gpsimd.Fori(0, BATCHES - 1) as b:
                for g in range(GROUPS):
                    v_stack(b + 1, g, True)

        @block.vector
        def _(dve):
            def maxima(s, g, u):
                i, h = u // GH, u % GH
                dve.wait_ge(s_ready, s * MAXES + (u + 1))
                if u == 0:
                    at(dve, mt_ready, s - 1)
                nc.vector.reduce_max(mx[:, g % 2, h * QT + i:h * QT + i + 1], ps[:, u % 2, 0:keys(i)], AX.X).then_inc(max_done, 1)

            def split_max(s, g):
                if not isinstance(s, int) or s >= 2:
                    g2 = (g - 2) % GROUPS
                    dve.wait_ge(m_loaded[g2], sent_before(s, g))
                dve.wait_ge(mt_ready, s + 1)
                m = ps[0:MAXES, MISC, 0:P]
                p1, p2, p3 = (mp[:, g % 2, i, :] for i in range(PARTS))
                nc.vector.tensor_scalar(p1, m, -1.0, None, ALU.mult).then_inc(m_step, 1)
                dve.wait_ge(m_step, s * 3 + 1)
                nc.vector.scalar_tensor_tensor(mr[:], m, -1.0, p1, ALU.mult, ALU.subtract).then_inc(m_step, 1)
                dve.wait_ge(m_step, s * 3 + 2)
                nc.vector.tensor_copy(p2, mr[:]).then_inc(m_step, 1)
                dve.wait_ge(m_step, s * 3 + 3)
                nc.vector.tensor_tensor(p3, mr[:], p2, ALU.subtract).then_inc(m_split, 1)

            def sent_before(s, g):
                if isinstance(s, int):
                    return 16 * PARTS * ((s - 2) // GROUPS + 1)
                return (s - (2 + (g - 2) % GROUPS)) * (16 * PARTS // GROUPS) + 16 * PARTS

            def context(t, g):
                dve.wait_ge(ott_ready, t + 2)
                o = ps[:, MISC, :].rearrange("p (i h e) -> p i h e", i=QT, h=GH)
                nc.vector.reciprocal(rec[:], o[:, :, :, HD:HD + 1]).then_inc(rec_ready, 1)
                dve.wait_ge(rec_ready, t + 1)
                dst = ctx_all[:, bass.ds(t - g, QT), g * GH * HD:(g + 1) * GH * HD].rearrange("p i (h e) -> p i h e", h=GH)
                nc.vector.tensor_tensor(dst, o[:, :, :, 0:HD], rec[:].to_broadcast([P, QT, GH, HD]), ALU.mult).then_inc(ctx_done, 1)

            def step(t, g):
                for u in range(UNITS):
                    if has(t, 2):
                        for n in range(2):
                            maxima(t + 2, (g + 2) % GROUPS, 2 * u + n)
                    if u == 0 and has(t, 1):
                        split_max(t + 1, (g + 1) % GROUPS)
                    if u == 4 and has(t, -1):
                        context(t - 1, (g - 1) % GROUPS)

            dve.sem_inc(ctx_done, 1)
            for u in range(MAXES):
                maxima(0, 0, u)
            split_max(0, 0)
            for u in range(MAXES):
                maxima(1, 1, u)
            steps(nc.vector, step)
            context(STEPS - 1, GROUPS - 1)

        @block.scalar
        def _(act):
            def exponential(t, g, u):
                kt, q0 = u // 2, first_query(u // 2)
                act.wait_ge(st_ready, t * UNITS + (u + 1))
                at(act, pv_done, t * QT + (kt - 1))
                nc.scalar.activation(pt[:, u % 4, :, q0:SEQ], ps[:, 2 + 2 * (u % 2):4 + 2 * (u % 2), q0:SEQ],
                                     ACT.Exp, scale=scale).then_inc(exp_done, 1)

            def copy_out(t):
                act.wait_ge(pv_done, (t + 1) * QT)
                act.wait_ge(ott_ready, t + 1)
                nc.scalar.copy(ot[:], ps[:, OUT_BANK, :]).then_inc(ot_ready, 1)

            def step(t, g):
                for u in range(UNITS):
                    exponential(t, g, u)
                    if u == 1 and has(t, -1):
                        copy_out(t - 1)

            steps(nc.scalar, step)
            copy_out(STEPS - 1)

        @block.tensor
        def _(pe):
            def first_pass(s, g, u, b_count):
                i, h = u // GH, u % GH
                if u == 0:
                    pe.wait_ge(loaded[g], b_count * (2 * PARTS * 16))
                at(pe, max_done, s * MAXES + (u - 1))
                q = qs[0:ROWS, g, h, i * P:(i + 1) * P]
                last = nc.tensor.matmul(ps[:, u % 2, 0:keys(i)], q, ks[0:ROWS, g, h, 0:keys(i)],
                                        start=True, stop=not causal)
                if causal:
                    last = nc.tensor.matmul(ps[:, u % 2, i * P:(i + 1) * P], c["identb"][:], c["after_q"][:],
                                            start=False, stop=True)
                last.then_inc(s_ready, 1)

            def turn_max(s, g):
                pe.wait_ge(max_done, (s + 1) * MAXES)
                at(pe, ctx_done, s - 1)
                nc.tensor.transpose(ps[0:MAXES, MISC, 0:P], mx[:, g % 2, :], c["ident"][:]).then_inc(mt_ready, 1)

            def second_pass(t, g, u, b_count):
                kt, q0 = u // 2, first_query(u // 2)
                if u == 0:
                    pe.wait_ge(m_loaded[g], b_count * (16 * PARTS))
                at(pe, exp_done, t * UNITS + (u - 1))
                for n in range(2):
                    h = 2 * (u % 2) + n
                    bank = 2 + 2 * (u % 2) + n
                    last = nc.tensor.matmul(ps[:, bank, q0:SEQ], ks[0:STACK, g, h, kt * P:(kt + 1) * P],
                                            qs[0:STACK, g, h, q0:SEQ], start=True, stop=not causal)
                    if causal:
                        last = nc.tensor.matmul(ps[:, bank, q0:q0 + P], c["identb"][:], c["after_k"][:],
                                                start=False, stop=True)
                last.then_inc(st_ready, 1)

            def values(t, g, kt):
                q0 = first_query(kt)
                pe.wait_ge(exp_done, t * UNITS + (2 * kt + 2))
                if kt == 0:
                    pe.wait_ge(vs_ready, t + 1)
                    at(pe, ot_ready, t)
                for h in range(GH):
                    last = nc.tensor.matmul(ps[32 * h:32 * h + 32, OUT_BANK, q0:SEQ], vs[:, g, kt, h, :],
                                            pt[:, 2 * (kt % 2) + h // 2, h % 2, q0:SEQ],
                                            start=kt == 0, stop=kt == QT - 1)
                last.then_inc(pv_done, 1)

            def turn_out(t):
                pe.wait_ge(ot_ready, t + 1)
                pe.wait_ge(ctx_done, t + 1)
                at(pe, m_split, min(t + 3, STEPS) if isinstance(t, int) else t + 3)
                for i in range(QT):
                    last = nc.tensor.transpose(ps[:, MISC, i * P:(i + 1) * P], ot[:, i * P:(i + 1) * P], c["ident"][:])
                last.then_inc(ott_ready, 1)

            def step(t, g):
                for u in range(UNITS):
                    if has(t, 2):
                        for n in range(2):
                            first_pass(t + 2, (g + 2) % GROUPS, 2 * u + n, uses(t + 2, (g + 2) % GROUPS))
                    second_pass(t, g, u, uses(t, g))
                    if u == 0 and has(t, 1):
                        turn_max(t + 1, (g + 1) % GROUPS)
                    if u == 1 and has(t, -1):
                        values(t - 1, (g - 1) % GROUPS, QT - 1)
                    if u == 3 and has(t, -1):
                        turn_out(t - 1)
                    if u % 2 == 1 and u > 1:
                        values(t, g, u // 2 - 1)

            def uses(t, g):
                if isinstance(t, int):
                    return t // GROUPS + 1
                return Quotient(t - g)

            pe.sem_inc(ott_ready, 1)
            for u in range(MAXES):
                first_pass(0, 0, u, 1)
            turn_max(0, 0)
            for u in range(MAXES):
                first_pass(1, 1, u, 1)
            steps(nc.tensor, step)
            values(STEPS - 1, GROUPS - 1, QT - 1)
            turn_out(STEPS - 1)
    st.clear()


class Quotient:

    def __init__(self, t):
        self.t = t

    def __mul__(self, by):
        assert by % GROUPS == 0
        return self.t * (by // GROUPS) + by


def attention_back(nc, name, c, w, ps, x_res, ctx_all):
    mem = ExitStack()
    st = Store(nc, mem)
    name += "b_"
    cs = st.sb(name + "ctx", [P, QT, P])
    ct = st.sb(name + "ctx_t", [P, SEQ])
    sub = st.sb(name + "sum", [P, QT, P])
    cs_ready = st.sem(name + "ctx_ready")
    ct_ps = st.sem(name + "ctx_t_in_psum")
    ct_ready = st.sem(name + "ctx_t_ready")
    o_ps = st.sem(name + "out_in_psum")
    sub_ready = st.sem(name + "sum_ready")
    x_done = st.sem(name + "x_done")
    with nc.Block() as block:
        @block.gpsimd
        def _(pool):
            nc.gpsimd.tensor_copy(cs[:], tiles_of(ctx_all, 0)).then_inc(cs_ready, 1)
            with nc.gpsimd.Fori(1, BATCHES) as b:
                pool.wait_ge(ct_ps, b)
                nc.gpsimd.tensor_copy(cs[:], tiles_of(ctx_all, b)).then_inc(cs_ready, 1)

        @block.tensor
        def _(pe):
            with nc.tensor.Fori(0, BATCHES) as b:
                pe.wait_ge(cs_ready, b + 1)
                for i in range(QT):
                    last = nc.tensor.transpose(ps[:, 0, i * P:(i + 1) * P], cs[:, i, :], c["ident"][:])
                last.then_inc(ct_ps, 1)
                pe.wait_ge(ct_ready, b + 1)
                pe.wait_ge(sub_ready, b + 1)
                for i in range(QT):
                    last = nc.tensor.matmul(ps[:, 1, i * P:(i + 1) * P], ct[:, i * P:(i + 1) * P], w["wo"][:],
                                            start=True, stop=True)
                last.then_inc(o_ps, 1)

        @block.scalar
        def _(act):
            with nc.scalar.Fori(0, BATCHES) as b:
                act.wait_ge(ct_ps, b + 1)
                nc.scalar.copy(ct[:], ps[:, 0, :]).then_inc(ct_ready, 1)

        @block.vector
        def _(dve):
            dve.sem_inc(sub_ready, 1)
            with nc.vector.Fori(0, BATCHES) as b:
                dve.wait_ge(o_ps, b + 1)
                nc.vector.tensor_tensor(sub[:], ps[:, 1, :].rearrange("p (i e) -> p i e", i=QT),
                                        w["bo"][:].rearrange("p (o e) -> p o e", o=1).to_broadcast([P, QT, P]),
                                        ALU.add).then_inc(sub_ready, 1)
                dve.wait_ge(sub_ready, b + 2)
                nc.vector.tensor_tensor(tiles_of(x_res, b), tiles_of(x_res, b), sub[:], ALU.add).then_inc(x_done, 1)
                dve.wait_ge(x_done, b + 1)
    st.clear()
    mem.close()


def experts(nc, name, d, c, w, ps, x_res, y_all, ctx_all, out):
    mem = ExitStack()
    st = Store(nc, mem)
    name += "e_"
    SLOTS = EXPERTS
    cs = st.sb(name + "ctx", [P, QT, P])
    ct = st.sb(name + "ctx_t", [P, SEQ])
    x2 = st.sb(name + "x2", [P, QT, P])
    z = st.sb(name + "z", [P, QT, P])
    xt = st.sb(name + "xt", [P, 2, SEQ])
    acc = st.sb(name + "acc", [P, 2, QT, P])
    gate = st.sb(name + "gate", [P, 2, QT, EXPERTS])
    gt = st.sb(name + "gate_t", [EXPERTS, SEQ])
    ht = st.sb(name + "ht", [P, 2, FC, SEQ])
    lg = st.sb(name + "logits", [P, QT, EXPERTS])
    eq = st.sb(name + "equal", [P, QT, EXPERTS])
    key = st.sb(name + "key", [P, QT, EXPERTS])
    pick1 = st.sb(name + "pick1", [P, QT, EXPERTS])
    pick2 = st.sb(name + "pick2", [P, QT, EXPERTS])
    left = st.sb(name + "left", [P, QT, EXPERTS])
    top = st.sb(name + "top", [P, 2, QT])
    rank = st.sb(name + "rank", [P, 2, QT])
    gap = st.sb(name + "gap", [P, QT])
    share = st.sb(name + "share", [P, 2, QT])
    norm = Norm(st, c, name + "norm", 1e-5)
    cs_ready = st.sem(name + "ctx_ready")
    ct_ps = st.sem(name + "ctx_t_in_psum")
    ct_ready = st.sem(name + "ctx_t_ready")
    o_ps = st.sem(name + "out_in_psum")
    x2_ready = st.sem(name + "x2_ready")
    z_ready = st.sem(name + "z_ready")
    zt_ps = st.sem(name + "zt_in_psum")
    xt_ready = st.sem(name + "xt_ready")
    lg_ps = st.sem(name + "logits_in_psum")
    g_step = st.sem(name + "gate_step")
    gap_ready = st.sem(name + "gap_ready")
    tanh_done = st.sem(name + "tanh_done")
    share_done = st.sem(name + "share_done")
    gate_ready = st.sem(name + "gate_ready")
    gt_ps = st.sem(name + "gate_t_in_psum")
    gt_ready = st.sem(name + "gate_t_ready")
    b2_ps = st.sem(name + "bias_in_psum")
    sum_ready = st.sem(name + "acc_start")
    acc_ready = st.sem(name + "acc_ready")
    up_ps = st.sem(name + "up_in_psum")
    h_ready = st.sem(name + "h_ready")
    down_ps = st.sem(name + "down_in_psum")
    added = st.sem(name + "added")
    x_done = st.sem(name + "x_done")
    stored = st.sem(name + "stored")
    G_STEPS = 13

    def batches(eng, batch):
        with eng.Fori(0, (BATCHES - 2) // 2) as u:
            for j in range(2):
                batch(u * 2 + j, j, True)
        batch(BATCHES - 2, 0, True)
        batch(BATCHES - 1, 1, False)

    with nc.Block() as block:
        @block.gpsimd
        def _(pool):
            nc.gpsimd.tensor_copy(cs[:], tiles_of(ctx_all, 0)).then_inc(cs_ready, 1)
            norm.pool(pool, 0)
            with nc.gpsimd.Fori(1, BATCHES) as b:
                pool.wait_ge(ct_ps, b)
                nc.gpsimd.tensor_copy(cs[:], tiles_of(ctx_all, b)).then_inc(cs_ready, 1)
                norm.pool(pool, b)

        @block.tensor
        def _(pe):
            def prepare(b, par, slot):
                if slot == 0:
                    pe.wait_ge(cs_ready, b + 1)
                    at(pe, acc_ready, b)
                    for i in range(QT):
                        last = nc.tensor.transpose(ps[:, 0, i * P:(i + 1) * P], cs[:, i, :], c["ident"][:])
                    last.then_inc(ct_ps, 1)
                if slot == 1:
                    pe.wait_ge(ct_ready, b + 1)
                    at(pe, gt_ready, b)
                    for i in range(QT):
                        last = nc.tensor.matmul(ps[:, 1, i * P:(i + 1) * P], ct[:, i * P:(i + 1) * P], w["wo"][:],
                                                start=True, stop=True)
                    last.then_inc(o_ps, 1)
                if slot == 3:
                    pe.wait_ge(z_ready, b + 1)
                    for i in range(QT):
                        last = nc.tensor.transpose(ps[:, 0, i * P:(i + 1) * P], z[:, i, :], c["ident"][:])
                    last.then_inc(zt_ps, 1)
                if slot == 4:
                    pe.wait_ge(xt_ready, b + 1)
                    pe.wait_ge(x2_ready, b + 1)
                    for i in range(QT):
                        last = nc.tensor.matmul(ps[:, 1, i * EXPERTS:(i + 1) * EXPERTS], xt[:, par, i * P:(i + 1) * P],
                                                w["wg"][:], start=True, stop=True)
                    last.then_inc(lg_ps, 1)
                if slot == 6:
                    pe.wait_ge(gate_ready, b + 1)
                    for i in range(QT):
                        last = nc.tensor.transpose(ps[0:EXPERTS, 1, i * P:(i + 1) * P], gate[:, par, i, :], c["ident"][:])
                    last.then_inc(gt_ps, 1)
                if slot == 7:
                    pe.wait_ge(gt_ready, b + 1)
                    for i in range(QT):
                        last = nc.tensor.matmul(ps[:, 0, i * P:(i + 1) * P], gt[:, i * P:(i + 1) * P], w["b2"][:],
                                                start=True, stop=True)
                    last.then_inc(b2_ps, 1)

            def up(b, par, e, n):
                if e == 0:
                    pe.wait_ge(xt_ready, b + 1)
                for f in range(FC):
                    at(pe, h_ready, n * FC + (f - 1))
                    nc.tensor.matmul(ps[:, 2 + f % 2, :], w["w1"][:, e, f * P:(f + 1) * P], xt[:, par, :],
                                     start=True, stop=True).then_inc(up_ps, 1)

            def down(e, n):
                pe.wait_ge(h_ready, n * FC + FC)
                pe.wait_ge(added, n + 1)
                for i in range(QT):
                    for f in range(FC):
                        last = nc.tensor.matmul(ps[:, 4 + e % 2, i * P:(i + 1) * P], ht[:, e % 2, f, i * P:(i + 1) * P],
                                                w["w2"][:, e * FC + f, :], start=f == 0, stop=f == FC - 1)
                last.then_inc(down_ps, 1)

            def batch(b, par, more):
                for e in range(EXPERTS):
                    n = b * EXPERTS + e
                    if more and e < EXPERTS:
                        prepare(b + 1, 1 - par, e)
                    if e + 1 < EXPERTS:
                        up(b, par, e + 1, n + 1)
                    elif more:
                        up(b + 1, 1 - par, 0, n + 1)
                    down(e, n)

            pe.sem_inc(down_ps, 1)
            for slot in range(SLOTS):
                prepare(0, 0, slot)
            up(0, 0, 0, 0)
            batches(nc.tensor, batch)

        @block.scalar
        def _(act):
            def prepare(b, par, slot):
                if slot == 0:
                    act.wait_ge(ct_ps, b + 1)
                    nc.scalar.copy(ct[:], ps[:, 0, :]).then_inc(ct_ready, 1)
                if slot == 3:
                    act.wait_ge(zt_ps, b + 1)
                    nc.scalar.activation(xt[:, par, :], ps[:, 0, :], ACT.Identity, bias=w["ln2_b"][:, 0:1],
                                         scale=w["ln2_g"][:, 0:1]).then_inc(xt_ready, 1)
                if slot == 4:
                    act.wait_ge(gap_ready, b + 1)
                    nc.scalar.activation(gap[:], gap[:], ACT.Tanh, scale=0.5).then_inc(tanh_done, 1)
                if slot == 6:
                    act.wait_ge(gt_ps, b + 1)
                    nc.scalar.copy(gt[:], ps[0:EXPERTS, 1, :]).then_inc(gt_ready, 1)

            def gelu(e, n):
                at(act, down_ps, n)
                for f in range(FC):
                    act.wait_ge(up_ps, n * FC + (f + 1))
                    nc.scalar.activation(ht[:, e % 2, f, :], ps[:, 2 + f % 2, :], ACT.Gelu_apprx_tanh,
                                         bias=w["b1"][:, e * FC + f:e * FC + f + 1]).then_inc(h_ready, 1)

            def batch(b, par, more):
                for e in range(EXPERTS):
                    if more:
                        prepare(b + 1, 1 - par, e)
                    if e + 1 < EXPERTS or more:
                        gelu((e + 1) % EXPERTS, b * EXPERTS + (e + 1))

            for slot in range(SLOTS):
                prepare(0, 0, slot)
            gelu(0, 0)
            batches(nc.scalar, batch)

        @block.vector
        def _(dve):
            v = nc.vector

            def per_token(ap):
                return ap.rearrange("p (i o) -> p i o", o=1).to_broadcast([P, QT, EXPERTS])

            def choose(b, par):
                steps = [0]

                def step(ins):
                    steps[0] += 1
                    ins.then_inc(g_step, 1)
                    dve.wait_ge(g_step, b * G_STEPS + steps[0])

                dve.wait_ge(lg_ps, b + 1)
                step(v.tensor_copy(lg[:], ps[:, 1, 0:QT * EXPERTS].rearrange("p (i e) -> p i e", i=QT)))
                for j, (src, pick) in enumerate(((lg, pick1), (left, pick2))):
                    step(v.tensor_reduce(top[:, j, :], src[:], AX.X, ALU.max))
                    step(v.tensor_tensor(eq[:], src[:], per_token(top[:, j, :]), ALU.is_equal))
                    step(v.tensor_tensor(key[:], eq[:], w["rev"][:], ALU.mult))
                    step(v.tensor_reduce(rank[:, j, :], key[:], AX.X, ALU.max))
                    step(v.tensor_tensor(pick[:], key[:], per_token(rank[:, j, :]), ALU.is_equal))
                    if j == 0:
                        step(v.scalar_tensor_tensor(left[:], pick1[:], -3e38, lg[:], ALU.mult, ALU.add))
                v.tensor_tensor(gap[:], top[:, 0, :], top[:, 1, :], ALU.subtract).then_inc(gap_ready, 1)
                dve.wait_ge(tanh_done, b + 1)
                v.tensor_scalar(share[:, 0, :], gap[:], 0.5, 0.5, ALU.mult, ALU.add)
                step(v.tensor_scalar(share[:, 1, :], gap[:], -0.5, 0.5, ALU.mult, ALU.add))
                v.tensor_tensor(pick1[:], pick1[:], per_token(share[:, 0, :]), ALU.mult)
                v.tensor_tensor(pick2[:], pick2[:], per_token(share[:, 1, :]), ALU.mult).then_inc(share_done, 1)
                dve.wait_ge(share_done, b + 1)
                v.tensor_tensor(gate[:, par, :, :], pick1[:], pick2[:], ALU.add).then_inc(gate_ready, 1)
                assert steps[0] == G_STEPS, steps

            def prepare(b, par, slot):
                if slot == 1:
                    dve.wait_ge(o_ps, b + 1)
                    v.tensor_tensor(x2[:], tiles_of(y_all, b), ps[:, 1, :].rearrange("p (i e) -> p i e", i=QT),
                                    ALU.add).then_inc(x2_ready, 1)
                    dve.wait_ge(x2_ready, b + 1)
                    norm.vector(dve, b, [x2[:, i, :] for i in range(QT)], [z[:, i, :] for i in range(QT)]).then_inc(z_ready, 1)
                if slot == 4:
                    choose(b, par)
                if slot == 7:
                    dve.wait_ge(b2_ps, b + 1)
                    v.tensor_tensor(acc[:, par, :, :], x2[:], ps[:, 0, :].rearrange("p (i e) -> p i e", i=QT),
                                    ALU.add).then_inc(sum_ready, 1)
                    dve.wait_ge(sum_ready, b + 1)
                    v.tensor_tensor(acc[:, par, :, :], acc[:, par, :, :], tiles_of(x_res, b), ALU.add).then_inc(acc_ready, 1)

            def add(b, par, e, n):
                dve.wait_ge(down_ps, n + 2)
                if e == 0:
                    dve.wait_ge(acc_ready, b + 1)
                    dve.wait_ge(gate_ready, b + 1)
                else:
                    dve.wait_ge(added, n + 2)
                for i in range(QT):
                    dst = acc[:, par, i, :] if e < EXPERTS - 1 else tile_of(x_res, b * QT + i)
                    last = v.scalar_tensor_tensor(dst, ps[:, 4 + e % 2, i * P:(i + 1) * P], gate[:, par, i, e:e + 1],
                                                  acc[:, par, i, :], ALU.mult, ALU.add)
                last.then_inc(added, 1)

            def batch(b, par, more):
                for e in range(EXPERTS):
                    if more:
                        prepare(b + 1, 1 - par, e)
                    add(b, par, e, b * EXPERTS + e)

            dve.sem_inc(added, 2)
            for slot in range(SLOTS):
                prepare(0, 0, slot)
            batches(nc.vector, batch)

        if out is not None:
            out_v = out.rearrange("b (i p) e -> p b i e", p=P)

            @block.sync
            def _(sp):
                with nc.sync.Fori(0, BATCHES) as b:
                    sp.wait_ge(added, b * EXPERTS + (EXPERTS + 2))
                    sp.dma_start(out_v[:, bass.ds(b, 1), :, :].rearrange("p a i e -> p (a i) e"),
                                 tiles_of(x_res, b)).then_inc(stored, 16)
                sp.wait_ge(stored, 16 * BATCHES)
    st.clear()
    mem.close()


_INS = ["L0_attn_a_x", "L0_attn_a_Wq", "L0_attn_a_Wk", "L0_attn_a_Wv", "L0_attn_a_Wo", "L0_attn_a_proj",
        "L0_attn_a_W1", "L0_attn_a_b1", "L0_attn_a_W2", "L0_attn_a_b2", "L0_attn_a_ln1_g", "L0_attn_a_ln1_b",
        "L0_attn_a_ln2_g", "L0_attn_a_ln2_b", "L0_attn_b_wq", "L0_attn_b_bq", "L0_attn_b_wk", "L0_attn_b_bk",
        "L0_attn_b_wv", "L0_attn_b_bv", "L0_attn_b_wo", "L0_attn_b_bo", "L0_ffn_ln1_g", "L0_ffn_ln1_b",
        "L0_ffn_ln2_g", "L0_ffn_ln2_b", "L0_ffn_Wq", "L0_ffn_Wk", "L0_ffn_Wv", "L0_ffn_Wo", "L0_ffn_Wg",
        "L0_ffn_W1", "L0_ffn_b1", "L0_ffn_W2", "L0_ffn_b2"]


def tables():
    t = {}
    row, chunk, head = np.arange(P)[:, None, None], np.arange(CH)[None, :, None], np.arange(PH)[None, None, :]
    t["perf_mask"] = (head == 2 * chunk + row // PM).astype(np.float32)
    inv_freq = (np.float32(1) / np.float32(10000) ** (np.arange(0, HD, 2, dtype=np.float32) / np.float32(HD)))
    angle = np.arange(SEQ, dtype=np.float32)[None, :] * inv_freq.astype(np.float32)[:, None]
    cos, sin = np.cos(angle).astype(np.float32), np.sin(angle).astype(np.float32)
    rows = np.arange(P)
    t["rope_cos"] = np.ascontiguousarray(cos[(rows % HD) // 2])
    t["rope_sin"] = np.ascontiguousarray(sin[(rows % HD) // 2] * np.where(rows % 2, 1, -1)[:, None].astype(np.float32))
    t["expert_rank"] = np.ascontiguousarray(np.broadcast_to(
        np.arange(EXPERTS, 0, -1, dtype=np.float32), (P, QT, EXPERTS)))
    return t


def kernel(**inputs):
    import concourse.bacc as bacc
    from concourse.bass_utils import run_bass_kernel_spmd

    nc = bacc.Bacc("TRN2", target_bir_lowering=False, num_devices=1)
    given = {n: np.ascontiguousarray(inputs[n]) for n in _INS} | tables()
    arrays, d = {}, {}
    for n, a in given.items():
        arrays[f"in_{n}"] = a
        d[n] = nc.dram_tensor(f"in_{n}", a.shape, mybir.dt.from_np(a.dtype), kind="ExternalInput").ap()
    out = nc.dram_tensor("out_x", (BATCHES, SEQ, P), F32, kind="ExternalOutput").ap()
    build(nc, d, out)
    r = run_bass_kernel_spmd(nc, [arrays], core_ids=[0])
    return r.results[0]["out_x"]
```

```python
import math
from contextlib import ExitStack

import numpy as np
import concourse.bass as bass
from concourse import mybir

F32 = mybir.dt.float32
BF16 = mybir.dt.bfloat16
ALU = mybir.AluOpType
ACT = mybir.ActivationFunctionType
AX = mybir.AxisListType
RMAX = bass.bass_isa.ReduceOp.max

P = 128
BATCHES, SEQ = 8, 512
QT = SEQ // P
TILES = BATCHES * QT
HEADS = 16
PH, PD, PM = 16, 64, 64
CH = PH * PM // P
EPS_KERN = 1e-6
FF = 512
FC = FF // P
HD = P // HEADS
GROUPS = 4
GH = HEADS // GROUPS
STEPS = BATCHES * GROUPS
PARTS = 3
ROWS = HD * PARTS * PARTS
STACK = ROWS + PARTS
EPSILONS = (1e-5, 1e-6)
EXPERTS = 8


def at(eng, sem, value):
    if not isinstance(value, int) or value > 0:
        eng.wait_ge(sem, value)


class Store:

    def __init__(self, nc, ctx):
        self.nc, self.ctx, self.sems = nc, ctx, []

    def sb(self, name, shape, dt=F32):
        return self.ctx.enter_context(self.nc.sbuf_tensor(name, shape, dt))

    def sem(self, name):
        self.sems.append(self.nc.alloc_semaphore(name))
        return self.sems[-1]

    def clear(self):
        self.nc.clear_and_free_semaphores(self.sems)
        self.nc.all_engine_barrier()
        self.sems = []


def flat(ap):
    return ap.rearrange("p a c -> p (a c)")


def tile_of(buf, t):
    return flat(buf[:, bass.ds(t, 1), :])


def tiles_of(buf, b, n=QT):
    return buf[:, bass.ds(b * n, n), :]


class Norm:

    def __init__(self, st, c, name, eps):
        self.nc, self.eps, self.half = st.nc, c[f"eps{eps:g}"], c["half"]
        self.gate = st.sb(name + "_gate", [1, 1])
        self.var = st.sb(name + "_var", [P, QT])
        self.eps_done = st.sem(name + "_eps_done")
        self.stats = st.sb(name + "_stats", [P, QT, 6])
        self.mv = st.sb(name + "_mv", [P, QT, 2])
        self.rstd = st.sb(name + "_rstd", [P, QT])
        self.stats_done = st.sem(name + "_stats_done")
        self.var_done = st.sem(name + "_var_done")
        self.rstd_done = st.sem(name + "_rstd_done")

    def vector(self, dve, k, src, dst):
        take_statistics(self, dve, k, src)
        return normalise(self, dve, k, src, dst)

    def pool(self, pool, k):
        pool.wait_ge(self.var_done, k + 1)
        self.nc.gpsimd.tensor_tensor(self.var[:, :], self.mv[:, :, 1], self.eps[:, :], ALU.add).then_inc(self.eps_done, 1)
        pool.wait_ge(self.eps_done, k + 1)
        self.nc.gpsimd.tensor_tensor(self.rstd[:, :], self.var[:, :], self.half[:, :], ALU.pow).then_inc(self.rstd_done, 1)


def take_statistics(norm, dve, k, src):
    nc = norm.nc
    for i in range(QT):
        last = nc.vector.bn_stats(norm.stats[:, i, :], src[i])
    last.then_inc(norm.stats_done, 1)
    dve.wait_ge(norm.stats_done, k + 1)
    nc.vector.tensor_copy(norm.gate[:, :], norm.half[0:1, 0:1])
    for i in range(QT):
        last = nc.vector.bn_aggr(norm.mv[:, i, :], norm.stats[:, i, :])
    last.then_inc(norm.var_done, 1)


def normalise(norm, dve, k, src, dst):
    dve.wait_ge(norm.rstd_done, k + 1)
    dve.wait_ge(norm.var_done, k + 1)
    for i in range(QT):
        last = norm.nc.vector.tensor_scalar(dst[i], src[i], norm.mv[:, i, 0:1], norm.rstd[:, i:i + 1],
                                            ALU.subtract, ALU.mult)
    return last


def build(nc, d, out):
    ctx = ExitStack()
    with ctx:
        st = Store(nc, ctx)
        ps = ctx.enter_context(nc.psum_tensor("ps", [P, 8, 512], F32))
        c = load_constants(nc, st, d)
        c["ps"] = ps
        x_res = st.sb("x_res", [P, TILES, P])
        y_ext = st.sb("y_all", [P, TILES, P + 1])
        y_all = y_ext[:, :, 0:P]
        performer(nc, d, c, ps, x_res, y_ext, y_all)
        with ExitStack() as rest:
            sm = Store(nc, rest)
            v_all = sm.sb("v_all", [P, TILES, P])
            ctx_all = sm.sb("ctx_all", [P, TILES, P])
            ffn, turning = load_later_weights(nc, d, c, sm)
            for layer in range(3):
                rope = layer == 1
                name = f"L{layer}"
                w = turning if rope else ffn
                if rope:
                    swap_pairs(nc, w)
                with ExitStack() as attention:
                    a = attention_memory(nc, c, Store(nc, attention), name)
                    attention_front(nc, name, rope, c, w, a, ps, x_res, y_all, v_all)
                    attention_main(nc, name, rope, c, a, ps, v_all, ctx_all)
                if rope:
                    attention_back(nc, name, c, w, ps, x_res, ctx_all)
                else:
                    experts(nc, name, d, c, w, ps, x_res, y_all, ctx_all, out if layer == 2 else None)


def load_constants(nc, st, d):
    c = {}
    c["ident"] = ident = st.sb("ident", [P, P])
    c["identb"] = identb = st.sb("identb", [P, P], BF16)
    c["ones"] = ones = st.sb("ones", [P, P])
    c["minus"] = st.sb("minus_one", [P, 1])
    for eps in EPSILONS:
        c[f"eps{eps:g}"] = st.sb(f"norm_eps{eps:g}", [P, QT])
    c["half"] = half = st.sb("minus_half", [P, QT])
    c["after_q"] = after_q = st.sb("after_q", [P, P], BF16)
    c["after_k"] = after_k = st.sb("after_k", [P, P], BF16)
    const_ready = st.sem("const_ready")
    with nc.Block() as block:
        @block.gpsimd
        def _(pool):
            g = nc.gpsimd
            g.memset(ident[:], 0.0).then_inc(const_ready, 1)
            g.memset(after_q[:], 0.0).then_inc(const_ready, 1)
            g.memset(after_k[:], 0.0).then_inc(const_ready, 1)
            g.memset(half[:], -0.5)
            g.memset(c["minus"][:], -1.0)
            for eps in EPSILONS:
                g.memset(c[f"eps{eps:g}"][:], eps)
            g.memset(ones[:], 1.0).then_inc(const_ready, 1)
            pool.wait_ge(const_ready, 4)
            g.affine_select(out=ident[:], in_=ident[:], compare_op=ALU.not_equal, fill=1.0, base=0,
                            pattern=[[-1, P]], channel_multiplier=1).then_inc(const_ready, 1)
            g.affine_select(out=after_q[:], in_=after_q[:], compare_op=ALU.is_ge, fill=-4e9, base=0,
                            pattern=[[-1, P]], channel_multiplier=1).then_inc(const_ready, 1)
            g.affine_select(out=after_k[:], in_=after_k[:], compare_op=ALU.is_ge, fill=-4e9, base=0,
                            pattern=[[1, P]], channel_multiplier=-1).then_inc(const_ready, 1)
            pool.wait_ge(const_ready, 7)
            g.tensor_copy(identb[:], ident[:]).then_inc(const_ready, 1)
    return c


def performer(nc, d, c, ps, x_res, y_ext, y_all):
    with ExitStack() as mem:
        st = Store(nc, mem)
        w = performer_weights(nc, st, d, c, ps, x_res)
        k = performer_keys(nc, st, c, w, ps, x_res, y_ext)
        performer_queries(nc, st, c, w, k, ps, x_res, y_all)
        st.clear()


def performer_weights(nc, st, d, c, ps, x_res):
    w = {}
    wide = PH * PD
    w["wq"] = wq = st.sb("a_wq", [P, wide])
    w["wk"] = wk = st.sb("a_wk", [P, wide])
    w["wqp"] = wqp = st.sb("a_wqp", [P, wide])
    w["wkp"] = wkp = st.sb("a_wkp", [P, wide])
    w["wvo"] = wvo = st.sb("a_wvo", [P, PH, P])
    w["w1"] = w1 = st.sb("a_w1", [P, FF])
    w["w2"] = w2 = st.sb("a_w2", [P, FC, P])
    w["b1"] = b1 = st.sb("a_b1", [P, FC])
    w["eps"] = eps = st.sb("a_eps", [P, 1])
    w["mask"] = mask = st.sb("a_mask", [P, CH, PH])
    rows = {}
    for n in ("b2", "ln1_g", "ln1_b", "ln2_g", "ln2_b"):
        w[n] = rows[n] = st.sb("a_" + n, [P, P])
    with ExitStack() as temp:
        t = Store(nc, temp)
        wv = t.sb("a_wv", [P, wide])
        wo = t.sb("a_wo", [P, CH, P])
        wt = t.sb("a_wt", [P, 3, CH, P])
        projp = t.sb("a_projp", [P, P])
        projt = t.sb("a_projt", [P, P])
        loaded = st.sem("a_w_loaded")
        zeroed = st.sem("a_proj_zeroed")
        turned = st.sem("a_w_turned")
        copied = st.sem("a_w_copied")
        product = st.sem("a_w_product")
        rest_loaded = st.sem("a_rest_loaded")
        xv = d["L0_attn_a_x"].rearrange("b (n p) e -> p (b n) e", p=P)
        n_first = 6
        n_rest = 3 + FC + len(rows) + BATCHES
        with nc.Block() as block:
            @block.sync
            def _(sp):
                def load(dst, src, sem=rest_loaded):
                    sp.dma_start(dst, src).then_inc(sem, 16)

                load(wq[:], d["L0_attn_a_Wq"].rearrange("e h k -> e (h k)"), loaded)
                load(wk[:], d["L0_attn_a_Wk"].rearrange("e h k -> e (h k)"), loaded)
                sp.wait_ge(zeroed, 1)
                for h in range(2):
                    load(projp[h * PM:(h + 1) * PM, h * PD:(h + 1) * PD], d["L0_attn_a_proj"], loaded)
                load(wv[:], d["L0_attn_a_Wv"].rearrange("e h k -> e (h k)"), loaded)
                load(wo[:], d["L0_attn_a_Wo"].rearrange("h k o -> (h k) o").rearrange("(c p) o -> p c o", p=P), loaded)
                for b in range(BATCHES):
                    load(x_res[:, b * QT:(b + 1) * QT, :], xv[:, b * QT:(b + 1) * QT, :])
                load(w1[:], d["L0_attn_a_W1"])
                load(w2[:], d["L0_attn_a_W2"].rearrange("(c p) o -> p c o", p=P))
                for f in range(FC):
                    load(b1[:, f:f + 1], d["L0_attn_a_b1"][f * P:(f + 1) * P].rearrange("(p o) -> p o", o=1))
                load(mask[:], d["perf_mask"])
                for n, dst in rows.items():
                    load(dst[:], d["L0_attn_a_" + n].partition_broadcast(P))
                sp.wait_ge(rest_loaded, 16 * n_rest)

            @block.gpsimd
            def _(pool):
                nc.gpsimd.memset(eps[:], EPS_KERN)
                nc.gpsimd.memset(projp[:], 0.0).then_inc(zeroed, 1)

            @block.tensor
            def _(pe):
                pe.wait_ge(loaded, 16 * n_first)
                nc.tensor.transpose(ps[:, 0, 0:P], projp[:], c["ident"][:]).then_inc(turned, 1)
                for i, src in enumerate((wq, wk, wv)):
                    for j in range(CH):
                        last = nc.tensor.transpose(ps[:, 1 + 2 * i + j // 4, (j % 4) * P:(j % 4 + 1) * P],
                                                   src[:, j * P:(j + 1) * P], c["ident"][:])
                    last.then_inc(turned, 1)
                pe.wait_ge(copied, 4)
                for i in range(2):
                    for j in range(CH):
                        last = nc.tensor.matmul(ps[:, 2 * i + j // 4, (j % 4) * P:(j % 4 + 1) * P],
                                                wt[:, i, j, :], projt[:], start=True, stop=True)
                last.then_inc(product, 1)
                for half in range(2):
                    for j in range(CH):
                        last = nc.tensor.matmul(ps[:, 4 + 2 * half + j // 4, (j % 4) * P:(j % 4 + 1) * P],
                                                wt[half * PD:(half + 1) * PD, 2, j, :],
                                                wo[half * PD:(half + 1) * PD, j, :], start=True, stop=True)
                last.then_inc(product, 1)

            @block.vector
            def _(dve):
                dve.wait_ge(turned, 1)
                nc.vector.tensor_scalar(projt[:], ps[:, 0, 0:P], PD ** -0.25, None, ALU.mult).then_inc(copied, 1)
                for i in range(3):
                    dve.wait_ge(turned, 2 + i)
                    nc.vector.tensor_copy(wt[:, i, :, :].rearrange("p c e -> p (c e)"),
                                          ps[:, 1 + 2 * i:3 + 2 * i, :].rearrange("p a b -> p (a b)")).then_inc(copied, 1)
                dve.wait_ge(product, 2)
                for i, dst in enumerate((wqp, wkp)):
                    nc.vector.tensor_copy(dst[:], ps[:, 2 * i:2 * i + 2, :].rearrange("p a b -> p (a b)"))
                for half in range(2):
                    nc.vector.tensor_copy(wvo[:].rearrange("p (c two) o -> p two c o", two=2)[:, half, :, :],
                                          ps[:, 4 + 2 * half:6 + 2 * half, :].rearrange("p a (c o) -> p (a c) o", o=P))
    return w


def performer_keys(nc, st, c, w, ps, x_res, y_ext):
    k = {}
    A = P + 1
    k["sums"] = sums = st.sb("a_sums", [P, BATCHES, CH * A])
    k["ysum"] = ysum = st.sb("a_ysum", [P, BATCHES, A])
    k["peak"] = peak = st.sb("a_peak", [P, BATCHES])
    temp = ExitStack()
    t = Store(nc, temp)
    y = t.sb("k_y", [P, QT, P])
    yt = t.sb("k_yt", [P, 2, SEQ])
    sq = t.sb("k_sq", [P, 2, PH * PD])
    ssq = t.sb("k_ssq", [P, 2, PH])
    e = t.sb("k_e", [P, 2, QT, PH * PM])
    tmax = t.sb("k_tmax", [P, 2, QT])
    bmax = t.sb("k_bmax", [P, 2])
    gate = t.sb("k_gate", [1, 2])
    bpeak = t.sb("k_bpeak", [P, 2])
    nl = t.sb("k_nl", [P, 2])
    norm = Norm(t, c, "k_norm", 1e-5)
    y_ready = t.sem("k_y_ready")
    y_saved = t.sem("k_y_saved")
    yt_ps = t.sem("k_yt_in_psum")
    yt_ready = t.sem("k_yt_ready")
    k_ready = t.sem("k_k_in_psum")
    dd_ready = t.sem("k_dd_in_psum")
    sq_ready = t.sem("k_squares_ready")
    ssq_ready = t.sem("k_ssq_ready")
    max_done = t.sem("k_tile_max_done")
    e_ready = t.sem("k_exponent_ready")
    bmax_ready = t.sem("k_batch_max_ready")
    peak_ready = t.sem("k_batch_peak_ready")
    nl_ready = t.sem("k_neg_peak_ready")
    peak_saved = t.sem("k_peak_saved")
    exp_done = t.sem("k_exp_done")
    g_ready = t.sem("k_sums_in_psum")
    g_saved = t.sem("k_sums_saved")
    ones_set = t.sem("k_ones_set")
    PIECES = [list(range(s, min(s + 3, CH))) for s in range(0, CH, 3)]
    N_PIECES = len(PIECES)

    def is_batch(b):
        return not isinstance(b, int) or 0 <= b < BATCHES

    def batches(eng, batch):
        batch(-1, 1)
        batch(0, 0)
        with eng.Fori(0, (BATCHES - 2) // 2) as u:
            for j in range(2):
                batch(u * 2 + (1 + j), 1 - j)
        batch(BATCHES - 1, 1)
        batch(BATCHES, 0)

    with nc.Block() as block:
        @block.vector
        def _(dve):
            def tile(b, par, i):
                if is_batch(b):
                    n = b * QT + i
                    dve.wait_ge(sq_ready, n + 1)
                    nc.vector.tensor_reduce(ssq[:, i % 2, :], sq[:, i % 2, :].rearrange("p (h k) -> p h k", h=PH),
                                            AX.X, ALU.add).then_inc(ssq_ready, 1)
                    dve.wait_ge(dd_ready, n + 1)
                    nc.vector.tensor_reduce(tmax[:, par, i:i + 1], ps[:, 2:4, :].rearrange("p a b -> p (a b)"),
                                            AX.X, ALU.max).then_inc(max_done, 1)
                    dve.wait_ge(ssq_ready, n + 1)
                    if i == 0:
                        at(dve, g_ready, b * N_PIECES)
                    nc.vector.scalar_tensor_tensor(
                        e[:, par, i, :].rearrange("p (h m) -> p h m", h=PH),
                        ssq[:, i % 2, :].rearrange("p (h o) -> p h o", o=1).to_broadcast([P, PH, PM]), -1.0 / 16,
                        ps[:, 2:4, :].rearrange("p a (h m) -> p (a h) m", m=PM), ALU.mult, ALU.add).then_inc(e_ready, 1)

            def batch(b, par):
                tile(b, par, 0)
                if is_batch(b + 1):
                    xs = [tile_of(x_res, (b + 1) * QT + i) for i in range(QT)]
                    take_statistics(norm, dve, b + 1, xs)
                tile(b, par, 1)
                if is_batch(b + 1):
                    at(dve, y_saved, b + 1)
                    at(dve, yt_ps, b + 1)
                    normalise(norm, dve, b + 1, xs, [y[:, i, :] for i in range(QT)]).then_inc(y_ready, 1)
                tile(b, par, 2)
                tile(b, par, 3)
                if is_batch(b):
                    dve.wait_ge(max_done, b * QT + QT)
                    nc.vector.reduce_max(bmax[:, par:par + 1], tmax[:, par, :], AX.X).then_inc(bmax_ready, 1)

            batches(nc.vector, batch)

        @block.gpsimd
        def _(pool):
            def batch(b, par):
                if is_batch(b + 1):
                    norm.pool(pool, b + 1)
                    pool.wait_ge(y_ready, b + 2)
                    nc.gpsimd.tensor_copy(tiles_of(y_ext, b + 1)[:, :, 0:P], y[:]).then_inc(y_saved, 1)
                if is_batch(b):
                    pool.wait_ge(bmax_ready, b + 1)
                    nc.gpsimd.tensor_tensor(gate[:, par:par + 1], c["minus"][0:1, :], c["minus"][0:1, :], ALU.mult)
                    nc.gpsimd.partition_all_reduce(bpeak[:, par:par + 1], bmax[:, par:par + 1], P, RMAX).then_inc(peak_ready, 1)
                    at(pool, exp_done, b)
                    pool.wait_ge(peak_ready, b + 1)
                    nc.gpsimd.tensor_tensor(nl[:, par:par + 1], bpeak[:, par:par + 1], c["minus"][:], ALU.mult).then_inc(nl_ready, 1)
                    nc.gpsimd.tensor_copy(peak[:, bass.ds(b, 1)], bpeak[:, par:par + 1]).then_inc(peak_saved, 1)

            nc.gpsimd.memset(y_ext[:, :, P:A], 1.0).then_inc(ones_set, 1)
            batches(nc.gpsimd, batch)

        @block.scalar
        def _(act):
            def square(b, i):
                if is_batch(b):
                    n = b * QT + i
                    act.wait_ge(k_ready, n + 1)
                    at(act, ssq_ready, n - 1)
                    nc.scalar.activation(sq[:, i % 2, :], ps[:, 0:2, :].rearrange("p a b -> p (a b)"),
                                         ACT.Square).then_inc(sq_ready, 1)

            def exponential(b, par, half):
                if is_batch(b):
                    act.wait_ge(nl_ready, b + 1)
                    act.wait_ge(e_ready, b * QT + QT)
                    two = e[:, par, 2 * half:2 * half + 2, :].rearrange("p i f -> p (i f)")
                    last = nc.scalar.activation(two, two, ACT.Exp, bias=nl[:, par:par + 1])
                    if half == 1:
                        last.then_inc(exp_done, 1)

            def save_sums(b, s):
                if is_batch(b):
                    act.wait_ge(g_ready, b * N_PIECES + (N_PIECES + s + 1))
                    mine = flat(sums[:, bass.ds(b, 1), :])[:, PIECES[s][0] * A:(PIECES[s][-1] + 1) * A]
                    last = nc.scalar.copy(mine, ps[:, 4 + s, 0:len(PIECES[s]) * A])
                    if s == N_PIECES - 1:
                        last = nc.scalar.copy(flat(ysum[:, bass.ds(b, 1), :]), ps[:, 7, 0:A])
                    last.then_inc(g_saved, 1)

            def batch(b, par):
                square(b, 0)
                exponential(b - 1, 1 - par, 0)
                square(b, 1)
                exponential(b - 1, 1 - par, 1)
                square(b, 2)
                save_sums(b - 1, 0)
                square(b, 3)
                if is_batch(b + 1):
                    act.wait_ge(yt_ps, b + 2)
                    nc.scalar.copy(yt[:, 1 - par, :], ps[:, 7, :]).then_inc(yt_ready, 1)
                save_sums(b - 1, 1)
                save_sums(b - 1, 2)

            act.sem_inc(exp_done, 1)
            act.sem_inc(g_saved, N_PIECES)
            batches(nc.scalar, batch)

        @block.tensor
        def _(pe):
            def tile(b, par, i):
                if is_batch(b):
                    n = b * QT + i
                    cols = yt[:, par, i * P:(i + 1) * P]
                    pe.wait_ge(yt_ready, b + 1)
                    at(pe, sq_ready, n)
                    for half in range(2):
                        last = nc.tensor.matmul(ps[:, half, :], cols, w["wk"][:, half * 512:(half + 1) * 512],
                                                start=True, stop=True)
                    last.then_inc(k_ready, 1)
                    at(pe, e_ready, n)
                    for half in range(2):
                        last = nc.tensor.matmul(ps[:, 2 + half, :], cols, w["wkp"][:, half * 512:(half + 1) * 512],
                                                start=True, stop=True)
                    last.then_inc(dd_ready, 1)

            def add_up(b, par, s):
                if is_batch(b):
                    pe.wait_ge(exp_done, b + 2)
                    pe.wait_ge(y_saved, b + 1)
                    pe.wait_ge(ones_set, 1)
                    pe.wait_ge(g_saved, b * N_PIECES + (s + 1))
                    ys = tiles_of(y_ext, b)
                    for at_col, j in enumerate(PIECES[s]):
                        for i in range(QT):
                            last = nc.tensor.matmul(ps[:, 4 + s, at_col * A:(at_col + 1) * A],
                                                    e[:, par, i, j * P:(j + 1) * P], ys[:, i, :],
                                                    start=i == 0, stop=i == QT - 1)
                    if s == N_PIECES - 1:
                        if is_batch(b + 2):
                            pe.wait_ge(yt_ready, b + 3)
                        for i in range(QT):
                            last = nc.tensor.matmul(ps[:, 7, 0:A], c["ones"][:], ys[:, i, :],
                                                    start=i == 0, stop=i == QT - 1)
                    last.then_inc(g_ready, 1)

            def batch(b, par):
                tile(b, par, 0)
                tile(b, par, 1)
                add_up(b - 1, 1 - par, 0)
                tile(b, par, 2)
                if is_batch(b + 1):
                    pe.wait_ge(y_ready, b + 2)
                    at(pe, g_saved, b * N_PIECES)
                    for i in range(QT):
                        last = nc.tensor.transpose(ps[:, 7, i * P:(i + 1) * P], y[:, i, :], c["ident"][:])
                    last.then_inc(yt_ps, 1)
                add_up(b - 1, 1 - par, 1)
                tile(b, par, 3)
                add_up(b - 1, 1 - par, 2)

            pe.sem_inc(g_ready, N_PIECES)
            batches(nc.tensor, batch)
    t.clear()
    temp.close()
    return k


def performer_queries(nc, st, c, w, k, ps, x_res, y_all):
    A = P + 1
    sums, ysum, peak = k["sums"], k["ysum"], k["peak"]
    gmax = st.sb("q_gmax", [P, 1])
    shift = st.sb("q_shift", [P, BATCHES])
    y = st.sb("q_y", [P, QT, P])
    yt = st.sb("q_yt", [P, SEQ])
    es = st.sb("q_es", [P, A])
    gf = st.sb("q_gf", [P, CH, A])
    gt = st.sb("q_gt", [P, CH * P])
    ksd = st.sb("q_ksd", [P, BATCHES * CH, PH])
    sq = st.sb("q_sq", [P, PH * PD])
    ssq = st.sb("q_ssq", [P, PH])
    mx = st.sb("q_mx", [P, PH])
    cc = st.sb("q_cc", [P, PH])
    e = st.sb("q_e", [P, 2, PH * PM])
    qf = st.sb("q_qf", [P, 2, CH, P])
    rec = st.sb("q_rec", [P, PH])
    wide = st.sb("q_wide", [P, PH * PM])
    r1 = st.sb("q_r1", [P, QT, P])
    kept = st.sb("q_kept", [P, QT, P])
    gate = st.sb("q_gate", [1, 1])
    o1 = st.sb("q_o1", [P, QT, P])
    o1t = st.sb("q_o1t", [P, SEQ])
    pos = st.sb("q_pos", [P, 2, SEQ])
    neg = st.sb("q_neg", [P, 2, SEQ])
    ht = st.sb("q_ht", [P, FC, SEQ])
    f2 = st.sb("q_f2", [P, QT, P])
    norm1 = Norm(st, c, "q_norm1", 1e-6)
    norm2 = Norm(st, c, "q_norm2", 1e-6)
    gmax_ready = st.sem("q_gmax_ready")
    gap_ready = st.sem("q_gap_ready")
    shift_ready = st.sem("q_shift_ready")
    y_ready = st.sem("q_y_ready")
    yt_ps = st.sem("q_yt_in_psum")
    yt_ready = st.sem("q_yt_ready")
    es_ready = st.sem("q_es_ready")
    gf_ready = st.sem("q_gf_ready")
    ksd_ready = st.sem("q_ksd_ready")
    gt_ps = st.sem("q_gt_in_psum")
    gt_ready = st.sem("q_gt_ready")
    pv_ps = st.sem("q_pv_in_psum")
    pv_ready = st.sem("q_pv_ready")
    r1_ready = st.sem("q_r1_ready")
    n1_ready = st.sem("q_n1_ready")
    g1_ready = st.sem("q_g1_ready")
    o1_ready = st.sem("q_o1_ready")
    o1_kept = st.sem("q_o1_kept")
    o1t_ps = st.sem("q_o1t_in_psum")
    o1t_ready = st.sem("q_o1t_ready")
    down_ps = st.sem("q_down_in_psum")
    f_ready = st.sem("q_f_ready")
    n2_ready = st.sem("q_n2_ready")
    g2_ready = st.sem("q_g2_ready")
    o2_ready = st.sem("q_o2_ready")
    x_done = st.sem("q_x_done")
    q_ready = st.sem("q_q_in_psum")
    dd_ready = st.sem("q_dd_in_psum")
    sq_ready = st.sem("q_squares_ready")
    ssq_ready = st.sem("q_ssq_ready")
    mx_ready = st.sem("q_mx_ready")
    c_ready = st.sem("q_c_ready")
    e_ready = st.sem("q_e_ready")
    exp_done = st.sem("q_exp_done")
    turned = st.sem("q_features_in_psum")
    qf_ready = st.sem("q_features_ready")
    den_ps = st.sem("q_den_in_psum")
    rec_ready = st.sem("q_rec_ready")
    wide_ready = st.sem("q_wide_ready")
    spread = st.sem("q_rec_spread")
    scaled = st.sem("q_features_scaled")
    out_ps = st.sem("q_attention_in_psum")
    up_ps = st.sem("q_up_in_psum")
    neg_ready = st.sem("q_neg_ready")
    pos_ready = st.sem("q_pos_ready")
    elu_exp = st.sem("q_elu_exp_done")
    h_ready = st.sem("q_h_ready")

    def is_batch(b):
        return not isinstance(b, int) or 0 <= b < BATCHES

    def is_tile(n):
        return not isinstance(n, int) or 0 <= n < TILES

    def batches(eng, batch):
        for b in (-1, 0, 1):
            batch(b)
        with eng.Fori(2, BATCHES - 1) as b:
            batch(b)
        for b in (BATCHES - 1, BATCHES, BATCHES + 1):
            batch(b)

    def wide_row(name):
        return w[name][:].rearrange("p (o e) -> p o e", o=1).to_broadcast([P, QT, P])

    with nc.Block() as block:
        @block.gpsimd
        def _(pool):
            g = nc.gpsimd

            def batch(b):
                if is_batch(b + 1):
                    at(pool, yt_ps, b + 1)
                    g.tensor_copy(y[:], tiles_of(y_all, b + 1)).then_inc(y_ready, 1)
                if is_batch(b - 1):
                    norm1.pool(pool, b - 1)
                    pool.wait_ge(n1_ready, b)
                    g.tensor_tensor(r1[:], r1[:], wide_row("ln1_g"), ALU.mult).then_inc(g1_ready, 1)
                    pool.wait_ge(g1_ready, b)
                    at(pool, o1t_ps, b - 1)
                    g.tensor_tensor(o1[:], r1[:], wide_row("ln1_b"), ALU.add).then_inc(o1_ready, 1)
                    pool.wait_ge(o1_ready, b)
                    at(pool, f_ready, b - 1)
                    g.tensor_tensor(kept[:], o1[:], wide_row("b2"), ALU.add).then_inc(o1_kept, 1)
                if is_batch(b - 2):
                    norm2.pool(pool, b - 2)
                    pool.wait_ge(n2_ready, b - 1)
                    g.tensor_tensor(f2[:], f2[:], wide_row("ln2_g"), ALU.mult).then_inc(g2_ready, 1)
                    pool.wait_ge(g2_ready, b - 1)
                    g.tensor_tensor(f2[:], f2[:], wide_row("ln2_b"), ALU.add).then_inc(o2_ready, 1)
                    pool.wait_ge(o2_ready, b - 1)
                    g.tensor_tensor(gate[:], c["minus"][0:1, :], c["minus"][0:1, :], ALU.mult)
                    g.tensor_tensor(tiles_of(x_res, b - 2), tiles_of(x_res, b - 2), f2[:], ALU.add).then_inc(x_done, 1)

            pool.sem_inc(x_done, 1)
            batches(pool, batch)

        @block.vector
        def _(dve):
            v = nc.vector
            dd = ps[:, 2:4, :].rearrange("p a (h m) -> p (a h) m", m=PM)

            def maximum(n):
                if is_tile(n):
                    dve.wait_ge(dd_ready, n + 1)
                    v.tensor_reduce(mx[:], dd, AX.X, ALU.max).then_inc(mx_ready, 1)

            def exponent(n, i):
                if is_tile(n):
                    dve.wait_ge(sq_ready, n + 1)
                    v.tensor_reduce(ssq[:], sq[:].rearrange("p (h k) -> p h k", h=PH), AX.X, ALU.add).then_inc(ssq_ready, 1)
                    dve.wait_ge(mx_ready, n + 1)
                    dve.wait_ge(ssq_ready, n + 1)
                    v.scalar_tensor_tensor(cc[:], ssq[:], 1.0 / 16, mx[:], ALU.mult, ALU.add).then_inc(c_ready, 1)
                    dve.wait_ge(c_ready, n + 1)
                    at(dve, turned, n - 1)
                    v.tensor_tensor(e[:, i % 2, :].rearrange("p (h m) -> p h m", h=PH), dd,
                                    cc[:].rearrange("p (h o) -> p h o", o=1).to_broadcast([P, PH, PM]),
                                    ALU.subtract).then_inc(e_ready, 1)

            def reciprocal(n):
                if is_tile(n):
                    dve.wait_ge(den_ps, n + 1)
                    at(dve, wide_ready, n)
                    v.reciprocal(rec[:], ps[:, 4, 0:PH]).then_inc(rec_ready, 1)

            def scale(n, i):
                if is_tile(n):
                    dve.wait_ge(spread, n + 1)
                    mine = qf[:, i % 2, :, :].rearrange("p c e -> p (c e)")
                    v.tensor_tensor(mine, mine, ps[:, 4:6, :].rearrange("p a b -> p (a b)"), ALU.mult).then_inc(scaled, 1)

            def keys_sums(b):
                v.tensor_scalar(es[:], flat(ysum[:, bass.ds(b, 1), :]), EPS_KERN, None, ALU.mult).then_inc(es_ready, 1)
                dve.wait_ge(es_ready, b + 1)
                at(dve, gt_ps, b)
                v.scalar_tensor_tensor(
                    gf[:], sums[:, bass.ds(b, 1), :].rearrange("p a (c e) -> p (a c) e", c=CH),
                    shift[:, bass.ds(b, 1)], es[:].rearrange("p (o e) -> p o e", o=1).to_broadcast([P, CH, A]),
                    ALU.mult, ALU.add).then_inc(gf_ready, 1)
                dve.wait_ge(gf_ready, b + 1)
                v.tensor_tensor(tiles_of(ksd, b, CH), w["mask"][:], gf[:, :, P:A].to_broadcast([P, CH, PH]),
                                ALU.mult).then_inc(ksd_ready, 1)

            def negatives(b, pair):
                for f in (pair, pair + 1):
                    dve.wait_ge(up_ps, b * FC + (f + 1))
                    dve.wait_ge(h_ready, b * FC + (pair + 1))
                    v.tensor_scalar(neg[:, f % 2, :], ps[:, f % 2, :], w["b1"][:, f:f + 1], 0.0,
                                    ALU.add, ALU.min).then_inc(neg_ready, 1)

            def elus(b, pair):
                dve.wait_ge(down_ps, b + 1)
                for f in (pair, pair + 1):
                    dve.wait_ge(elu_exp, b * FC + (f + 1))
                    dve.wait_ge(pos_ready, b * FC + (f + 1))
                    v.scalar_tensor_tensor(ht[:, f, :], neg[:, f % 2, :], -1.0, pos[:, f % 2, :],
                                           ALU.add, ALU.add).then_inc(h_ready, 1)

            def batch(b):
                n = b * QT
                first = [r1[:, i, :] for i in range(QT)]
                second = [f2[:, i, :] for i in range(QT)]
                maximum(n)
                scale(n - 2, 0)
                exponent(n, 0)
                reciprocal(n - 1)
                if is_batch(b - 2):
                    negatives(b - 2, 0)
                if is_batch(b + 1):
                    keys_sums(b + 1)
                maximum(n + 1)
                scale(n - 1, 1)
                if is_batch(b - 2):
                    elus(b - 2, 0)
                exponent(n + 1, 1)
                reciprocal(n)
                if is_batch(b - 2):
                    negatives(b - 2, 2)
                maximum(n + 2)
                scale(n, 0)
                if is_batch(b - 2):
                    elus(b - 2, 2)
                if is_batch(b - 1):
                    dve.wait_ge(out_ps, n)
                    at(dve, o1_ready, b - 1)
                    v.tensor_tensor(r1[:], tiles_of(y_all, b - 1),
                                    ps[:, 6, :].rearrange("p (i e) -> p i e", i=QT), ALU.add).then_inc(r1_ready, 1)
                    dve.wait_ge(r1_ready, b)
                    take_statistics(norm1, dve, b - 1, first)
                exponent(n + 2, 2)
                if is_batch(b - 1):
                    normalise(norm1, dve, b - 1, first, first).then_inc(n1_ready, 1)
                reciprocal(n + 1)
                maximum(n + 3)
                scale(n + 1, 1)
                if is_batch(b - 2):
                    dve.wait_ge(down_ps, b)
                    dve.wait_ge(o1_kept, b - 1)
                    dve.wait_ge(x_done, b - 1)
                    v.tensor_tensor(f2[:], kept[:], ps[:, 7, :].rearrange("p (i e) -> p i e", i=QT),
                                    ALU.add).then_inc(f_ready, 1)
                    dve.wait_ge(f_ready, b - 1)
                    take_statistics(norm2, dve, b - 2, second)
                exponent(n + 3, 3)
                if is_batch(b - 2):
                    normalise(norm2, dve, b - 2, second, second).then_inc(n2_ready, 1)
                reciprocal(n + 2)

            v.reduce_max(gmax[:], peak[:], AX.X).then_inc(gmax_ready, 1)
            dve.wait_ge(gmax_ready, 1)
            v.tensor_scalar(shift[:], peak[:], gmax[:], None, ALU.subtract).then_inc(gap_ready, 1)
            dve.wait_ge(shift_ready, 1)
            dve.sem_inc(h_ready, 1)
            batches(dve, batch)

        @block.scalar
        def _(act):
            s = nc.scalar

            def square(n):
                if is_tile(n):
                    act.wait_ge(q_ready, n + 1)
                    at(act, ssq_ready, n)
                    s.activation(sq[:], ps[:, 0:2, :].rearrange("p a b -> p (a b)"), ACT.Square).then_inc(sq_ready, 1)

            def features(n, i):
                if is_tile(n):
                    act.wait_ge(turned, n + 1)
                    at(act, out_ps, n - 1)
                    s.activation(qf[:, i % 2, :, :], ps[:, 4:6, :].rearrange("p a (c e) -> p (a c) e", e=P),
                                 ACT.Identity, bias=w["eps"][:, 0:1]).then_inc(qf_ready, 1)

            def exponential(n, i):
                if is_tile(n):
                    act.wait_ge(e_ready, n + 1)
                    s.activation(e[:, i % 2, :], e[:, i % 2, :], ACT.Exp).then_inc(exp_done, 1)

            def widen(n):
                if is_tile(n):
                    act.wait_ge(rec_ready, n + 1)
                    at(act, spread, n)
                    s.copy(wide[:].rearrange("p (h m) -> p h m", h=PH),
                           rec[:].rearrange("p (h o) -> p h o", o=1).to_broadcast([P, PH, PM])).then_inc(wide_ready, 1)

            def elu_parts(b, pair):
                if is_batch(b):
                    for f in (pair, pair + 1):
                        act.wait_ge(neg_ready, b * FC + (f + 1))
                        s.activation(pos[:, f % 2, :], ps[:, f % 2, :], ACT.Relu, bias=w["b1"][:, f:f + 1]).then_inc(pos_ready, 1)
                    for f in (pair, pair + 1):
                        s.activation(neg[:, f % 2, :], neg[:, f % 2, :], ACT.Exp).then_inc(elu_exp, 1)

            def batch(b):
                n = b * QT
                square(n)
                features(n - 1, 1)
                exponential(n, 0)
                widen(n - 1)
                elu_parts(b - 2, 0)
                square(n + 1)
                features(n, 0)
                exponential(n + 1, 1)
                widen(n)
                elu_parts(b - 2, 2)
                square(n + 2)
                features(n + 1, 1)
                if is_batch(b + 1):
                    act.wait_ge(gt_ps, b + 2)
                    s.copy(gt[:], ps[:, 0:2, :].rearrange("p a b -> p (a b)")).then_inc(gt_ready, 1)
                exponential(n + 2, 0)
                widen(n + 1)
                square(n + 3)
                if is_batch(b + 1):
                    act.wait_ge(yt_ps, b + 2)
                    s.copy(yt[:], ps[:, 7, :]).then_inc(yt_ready, 1)
                features(n + 2, 0)
                if is_batch(b + 1):
                    act.wait_ge(pv_ps, b + 2)
                    s.copy(flat(sums[:, bass.ds(b + 1, 1), 0:CH * P]),
                           ps[:, 0:2, :].rearrange("p a b -> p (a b)")).then_inc(pv_ready, 1)
                exponential(n + 3, 1)
                widen(n + 2)
                if is_batch(b - 1):
                    act.wait_ge(o1t_ps, b)
                    s.copy(o1t[:], ps[:, 7, :]).then_inc(o1t_ready, 1)

            act.wait_ge(gap_ready, 1)
            s.activation(shift[:], shift[:], ACT.Exp).then_inc(shift_ready, 1)
            batches(act, batch)

        @block.tensor
        def _(pe):
            def fill_used(b, i):
                if i == 0 and is_batch(b):
                    at(pe, pv_ready, b + 1)
                if i in (1, 2) and is_batch(b - 2):
                    pe.wait_ge(pos_ready, (b - 2) * FC + 2 * i)
                if i == 3 and is_batch(b + 1):
                    pe.wait_ge(gt_ready, b + 2)

            def spread_out(n):
                if is_tile(n):
                    pe.wait_ge(wide_ready, n + 1)
                    for j in range(CH):
                        last = nc.tensor.transpose(ps[:, 4 + j // 4, (j % 4) * P:(j % 4 + 1) * P],
                                                   wide[:, j * P:(j + 1) * P], c["ident"][:])
                    last.then_inc(spread, 1)

            def products(b, n, i):
                if is_tile(n):
                    tile = yt[:, i * P:(i + 1) * P]
                    pe.wait_ge(yt_ready, b + 1)
                    at(pe, e_ready, n)
                    for half in range(2):
                        last = nc.tensor.matmul(ps[:, 2 + half, :], tile, w["wqp"][:, half * 512:(half + 1) * 512],
                                                start=True, stop=True)
                    last.then_inc(dd_ready, 1)
                spread_out(n - 2)
                if is_tile(n):
                    at(pe, sq_ready, n)
                    fill_used(b, i)
                    for half in range(2):
                        last = nc.tensor.matmul(ps[:, half, :], tile, w["wq"][:, half * 512:(half + 1) * 512],
                                                start=True, stop=True)
                    last.then_inc(q_ready, 1)

            def before_fill(b, n, i):
                if is_tile(n):
                    pe.wait_ge(sq_ready, n + 1)
                else:
                    fill_used(b, i)

            def turn(n, i):
                if is_tile(n):
                    pe.wait_ge(exp_done, n + 1)
                    at(pe, scaled, n)
                    for j in range(CH):
                        last = nc.tensor.transpose(ps[:, 4 + j // 4, (j % 4) * P:(j % 4 + 1) * P],
                                                   e[:, i % 2, j * P:(j + 1) * P], c["ident"][:])
                    last.then_inc(turned, 1)

            def denominators(b, n, i):
                if is_tile(n):
                    pe.wait_ge(qf_ready, n + 1)
                    pe.wait_ge(ksd_ready, b + 1)
                    ks = tiles_of(ksd, b, CH)
                    for j in range(CH):
                        last = nc.tensor.matmul(ps[:, 4, 0:PH], qf[:, i % 2, j, :], ks[:, j, :],
                                                start=j == 0, stop=j == CH - 1)
                    last.then_inc(den_ps, 1)

            def attend(b, n, i):
                if is_tile(n):
                    pe.wait_ge(scaled, n + 1)
                    pe.wait_ge(pv_ready, b + 1)
                    if i == 0:
                        at(pe, r1_ready, b)
                    pv = sums[:, bass.ds(b, 1), 0:CH * P].rearrange("p a (c e) -> p (a c) e", c=CH)
                    for j in range(CH):
                        last = nc.tensor.matmul(ps[:, 6, i * P:(i + 1) * P], qf[:, i % 2, j, :], pv[:, j, :],
                                                start=j == 0, stop=j == CH - 1)
                    last.then_inc(out_ps, 1)

            def up(b, pair):
                pe.wait_ge(o1t_ready, b + 1)
                for f in (pair, pair + 1):
                    nc.tensor.matmul(ps[:, f % 2, :], w["w1"][:, f * P:(f + 1) * P], o1t[:],
                                     start=True, stop=True).then_inc(up_ps, 1)

            def batch(b):
                n = b * QT
                products(b, n, 0)
                turn(n - 1, 1)
                if is_batch(b - 2):
                    before_fill(b, n, 0)
                    up(b - 2, 0)
                denominators(b - 1, n - 1, 3)
                attend(b - 1, n - 2, 2)
                products(b, n + 1, 1)
                turn(n, 0)
                if is_batch(b - 2):
                    before_fill(b, n + 1, 1)
                    up(b - 2, 2)
                denominators(b, n, 0)
                attend(b - 1, n - 1, 3)
                products(b, n + 2, 2)
                turn(n + 1, 1)
                if is_batch(b + 1):
                    before_fill(b, n + 2, 2)
                    pe.wait_ge(gf_ready, b + 2)
                    for j in range(CH):
                        last = nc.tensor.transpose(ps[:, j // 4, (j % 4) * P:(j % 4 + 1) * P], gf[:, j, 0:P], c["ident"][:])
                    last.then_inc(gt_ps, 1)
                denominators(b, n + 1, 1)
                attend(b, n, 0)
                if is_batch(b - 2):
                    pe.wait_ge(h_ready, (b - 2) * FC + (FC + 1))
                    for i in range(QT):
                        for f in range(FC):
                            last = nc.tensor.matmul(ps[:, 7, i * P:(i + 1) * P], ht[:, f, i * P:(i + 1) * P], w["w2"][:, f, :],
                                                    start=f == 0, stop=f == FC - 1)
                    last.then_inc(down_ps, 1)
                products(b, n + 3, 3)
                if is_batch(b + 1):
                    pe.wait_ge(y_ready, b + 2)
                    if is_batch(b - 2):
                        pe.wait_ge(f_ready, b - 1)
                    elif is_batch(b - 1):
                        pe.wait_ge(o1t_ready, b - 1)
                    for i in range(QT):
                        last = nc.tensor.transpose(ps[:, 7, i * P:(i + 1) * P], y[:, i, :], c["ident"][:])
                    last.then_inc(yt_ps, 1)
                turn(n + 2, 0)
                if is_batch(b + 1):
                    before_fill(b, n + 3, 3)
                    pe.wait_ge(gt_ready, b + 2)
                    for h in range(PH):
                        r, j = (h % 2) * PM, h // 2
                        last = nc.tensor.matmul(ps[r:r + PM, j // 4, (j % 4) * P:(j % 4 + 1) * P],
                                                gt[:, h * PM:(h + 1) * PM], w["wvo"][:, h, :], start=True, stop=True)
                    last.then_inc(pv_ps, 1)
                denominators(b, n + 2, 2)
                attend(b, n + 1, 1)
                if is_batch(b - 1):
                    pe.wait_ge(o1_ready, b)
                    if is_batch(b + 1):
                        pe.wait_ge(yt_ready, b + 2)
                    elif is_batch(b - 2):
                        pe.wait_ge(f_ready, b - 1)
                    for i in range(QT):
                        last = nc.tensor.transpose(ps[:, 7, i * P:(i + 1) * P], o1[:, i, :], c["ident"][:])
                    last.then_inc(o1t_ps, 1)

            pe.sem_inc(down_ps, 1)
            batches(pe, batch)


def attention_memory(nc, c, st, name):
    a = {}
    a["q_dram"] = nc.dram_tensor(name + "_q_stacks", [BATCHES, P, PARTS, SEQ], BF16, kind="Internal").ap()
    a["k_dram"] = nc.dram_tensor(name + "_k_stacks", [BATCHES, PARTS, P, PARTS, SEQ], BF16, kind="Internal").ap()
    a["qs"] = st.sb(name + "_q_stack", [P, GROUPS, GH, SEQ], BF16)
    a["ks"], a["vs"] = c["ks"], c["vs"]
    a["pt"] = st.sb(name + "_probs_t", [P, 4, 2, SEQ])
    a["ot"] = st.sb(name + "_out_t", [P, SEQ])
    a["mx"] = st.sb(name + "_row_max", [P, 2, GH * QT])
    a["mp"] = st.sb(name + "_max_parts", [GH * QT, 2, PARTS, P], BF16)
    a["mr"] = st.sb(name + "_max_rest", [GH * QT, P])
    a["rec"] = st.sb(name + "_recip_sum", [P, QT, GH, 1])
    a["y"] = st.sb(name + "_front_y", [P, QT, P])
    a["z"] = st.sb(name + "_front_z", [P, QT, P])
    a["ht"] = st.sb(name + "_front_ht", [P, SEQ])
    a["full"] = st.sb(name + "_front_qk", [P, 2, SEQ])
    a["rest"] = st.sb(name + "_front_rest", [P, 2, SEQ])
    a["parts"] = st.sb(name + "_front_parts", [P, 2, 2, PARTS, SEQ], BF16)
    return a


def load_later_weights(nc, d, c, st):
    w = {"arrived": st.sem("later_w_arrived")}
    r = {"arrived": st.sem("rope_w_arrived"), "loads": 0}
    now, later, later_rope = [], [], []

    def column(v):
        return v.rearrange("(p o) -> p o", o=1)

    def add(into, key, shape, src, prefix, loads):
        into[key] = st.sb(f"{prefix}_{key}", shape)
        loads.append((into[key][:], src))

    for n in "qkvo":
        add(w, "w" + n, [P, P], d["L0_ffn_W" + n], "ffn", now)
    for n in ("ln1_g", "ln1_b", "ln2_g", "ln2_b"):
        add(w, n, [P, 1], column(d["L0_ffn_" + n]), "ffn", now)
    add(w, "b1r", [EXPERTS * FC, P], d["L0_ffn_b1"].rearrange("e (c p) -> (e c) p", p=P), "ffn", now)
    w["b1"] = st.sb("ffn_b1", [P, EXPERTS * FC])
    add(w, "w1", [P, EXPERTS, FF], d["L0_ffn_W1"].rearrange("e p f -> p e f"), "ffn", later)
    add(w, "w2", [P, EXPERTS * FC, P], d["L0_ffn_W2"].rearrange("e (c p) o -> p (e c) o", p=P), "ffn", later)
    add(w, "wg", [P, EXPERTS], d["L0_ffn_Wg"], "ffn", later)
    add(w, "b2", [EXPERTS, P], d["L0_ffn_b2"], "ffn", later)
    add(w, "rev", [P, QT, EXPERTS], d["expert_rank"], "ffn", later)
    w["loads"] = len(later)

    for n in "qkvo":
        add(r, "w" + n, [P, P], d["L0_attn_b_w" + n], "rope", later_rope)
    add(r, "cos", [P, SEQ], d["rope_cos"], "rope", later_rope)
    add(r, "sin", [P, SEQ], d["rope_sin"], "rope", later_rope)
    for n in "qk":
        add(r, "b" + n, [P, 1], column(d["L0_attn_b_b" + n]), "rope", later_rope)
        r["w" + n + "s"] = st.sb(f"rope_w{n}s", [P, P])
        other = r["b" + n + "s"] = st.sb(f"rope_b{n}s", [P, 1])
        pairs = d["L0_attn_b_b" + n].rearrange("(a two o) -> a two o", two=2, o=1)
        for half in range(2):
            later_rope.append((other[half:P:2, :], pairs[:, 1 - half, :]))
    add(r, "bv", [P, P], d["L0_attn_b_bv"].partition_broadcast(P), "rope", later_rope)
    add(r, "bo", [P, P], d["L0_attn_b_bo"].partition_broadcast(P), "rope", later_rope)
    r["loads"] = len(later_rope)

    c["ks"] = ks = st.sb("k_stack", [P, GROUPS, GH, SEQ], BF16)
    c["vs"] = vs = st.sb("v_stack", [P, GROUPS, QT, GH, 32])
    loaded = st.sem("ffn_w_loaded")
    turned = st.sem("ffn_b1_turned")
    zeroed = st.sem("v_stack_zeroed")
    with nc.Block() as block:
        @block.sync
        def _(sp):
            for dst, src in now:
                sp.dma_start(dst, src).then_inc(loaded, 16)
            for dst, src in later:
                sp.dma_start(dst, src).then_inc(w["arrived"], 16)
            for dst, src in later_rope:
                sp.dma_start(dst, src, allow_slow_non_contiguous=True).then_inc(r["arrived"], 16)
            sp.wait_ge(loaded, 16 * len(now))

        @block.tensor
        def _(pe):
            pe.wait_ge(loaded, 16 * len(now))
            nc.tensor.transpose(c["ps"][:, 0, 0:EXPERTS * FC], w["b1r"][:], c["ident"][0:EXPERTS * FC, 0:EXPERTS * FC]).then_inc(turned, 1)

        @block.vector
        def _(dve):
            nc.vector.memset(ks[64:P, :, :, :], 1.0)
            dve.wait_ge(turned, 1)
            nc.vector.tensor_copy(w["b1"][:], c["ps"][:, 0, 0:EXPERTS * FC])

        @block.gpsimd
        def _(pool):
            nc.gpsimd.memset(vs[:], 0.0).then_inc(zeroed, 1)
            pool.wait_ge(zeroed, 1)
            nc.gpsimd.memset(vs[:, :, :, :, HD:HD + 1], 1.0)
    return w, r


def swap_pairs(nc, w):
    with nc.Block() as block:
        @block.vector
        def _(dve):
            dve.wait_ge(w["arrived"], 16 * w["loads"])
            for n in "qk":
                src = w["w" + n][:].rearrange("p (a two) -> p a two", two=2)
                dst = w["w" + n + "s"][:].rearrange("p (a two) -> p a two", two=2)
                for half in range(2):
                    nc.vector.tensor_copy(dst[:, :, half], src[:, :, 1 - half])


def attention_front(nc, name, rope, c, w, a, ps, x_res, y_all, v_all):
    mem = ExitStack()
    st = Store(nc, mem)
    name += "f_"
    norm = Norm(st, c, name + "norm", 1e-5)
    norms = 1 if rope else 2
    y, z, ht, full, rest, parts = (a[n] for n in ("y", "z", "ht", "full", "rest", "parts"))
    if rope:
        z = y
    y_ready = st.sem(name + "y_ready")
    y_saved = st.sem(name + "y_saved")
    z_ready = st.sem(name + "z_ready")
    zt_ps = st.sem(name + "zt_in_psum")
    ht_ready = st.sem(name + "ht_ready")
    qk_ps = st.sem(name + "qk_in_psum")
    v_ps = st.sem(name + "v_in_psum")
    v_saved = st.sem(name + "v_saved")
    full_ready = st.sem(name + "qk_ready")
    turn_step = st.sem(name + "rope_step")
    part1 = st.sem(name + "part1_ready")
    rest_ready = st.sem(name + "rest_ready")
    part2 = st.sem(name + "part2_ready")
    part3 = st.sem(name + "part3_ready")
    unsent = Store(nc, mem)
    a["sent"] = sent = [unsent.sem(f"{name}stacks_sent{par}") for par in range(2)]
    a["unsent"] = unsent
    SENDS = 1 + PARTS
    a["all_sent"] = 16 * SENDS * (BATCHES // 2) + 1

    with nc.Block() as block:
        @block.vector
        def _(dve):
            ys = [y[:, i, :] for i in range(QT)]
            zs = [z[:, i, :] for i in range(QT)]

            def measure_x(b):
                take_statistics(norm, dve, b * norms, [tile_of(x_res, b * QT + i) for i in range(QT)])

            def norm_x(b, first=False):
                if not first:
                    dve.wait_ge(zt_ps if rope else y_saved, b)
                normalise(norm, dve, b * norms, [tile_of(x_res, b * QT + i) for i in range(QT)],
                           ys).then_inc(z_ready if rope else y_ready, 1)

            def measure_y(b):
                dve.wait_ge(y_ready, b + 1)
                take_statistics(norm, dve, b * 2 + 1, ys)

            def norm_y(b, first=False):
                if not first:
                    dve.wait_ge(zt_ps, b)
                normalise(norm, dve, b * 2 + 1, ys, zs).then_inc(z_ready, 1)

            def rotate(b):
                dve.wait_ge(qk_ps, b + 1)
                for x in range(2):
                    bias, other = w["bq" if x == 0 else "bk"], w["bqs" if x == 0 else "bks"]
                    nc.vector.scalar_tensor_tensor(full[:, x, :], ps[:, 1 + x, :], bias[:, 0:1], w["cos"][:],
                                                   ALU.add, ALU.mult)
                    nc.vector.scalar_tensor_tensor(rest[:, x, :], ps[:, 4 + x, :], other[:, 0:1], w["sin"][:],
                                                   ALU.add, ALU.mult).then_inc(turn_step, 1)
                for x in range(2):
                    dve.wait_ge(turn_step, b * 2 + (x + 1))
                    nc.vector.tensor_tensor(full[:, x, :], full[:, x, :], rest[:, x, :], ALU.add).then_inc(full_ready, 1)
                dve.wait_ge(v_ps, b + 1)
                nc.vector.tensor_tensor(tiles_of(v_all, b), ps[:, 3, :].rearrange("p (i e) -> p i e", i=QT),
                                        w["bv"][:].rearrange("p (o e) -> p o e", o=1).to_broadcast([P, QT, P]),
                                        ALU.add).then_inc(v_saved, 1)
                dve.wait_ge(full_ready, b * 2 + 3)

            def second_part(b, par):
                for x in range(2):
                    dve.wait_ge(part1, b * 2 + (x + 1))
                    nc.vector.tensor_tensor(rest[:, x, :], full[:, x, :], parts[:, par, x, 0, :], ALU.subtract).then_inc(rest_ready, 1)

            def third_part(b, par):
                for x in range(2):
                    dve.wait_ge(part2, b * 2 + (x + 1))
                    nc.vector.tensor_tensor(parts[:, par, x, 2, :], rest[:, x, :], parts[:, par, x, 1, :],
                                            ALU.subtract).then_inc(part3, 1)
                dve.wait_ge(part3, b * 2 + 2)

            if rope:
                dve.sem_inc(full_ready, 1)
                dve.sem_inc(v_saved, 1)
            dve.sem_inc(rest_ready, 1)
            measure_x(0)
            norm_x(0, True)
            if not rope:
                measure_y(0)
                norm_y(0, True)
            def batch(b, par):
                more = not isinstance(b, int) or b < BATCHES - 1
                before = not isinstance(b, int) or b > 0
                if more:
                    measure_x(b + 1)
                if before:
                    second_part(b - 1, 1 - par)
                if more:
                    norm_x(b + 1)
                    if not rope:
                        measure_y(b + 1)
                if before:
                    third_part(b - 1, 1 - par)
                if rope:
                    rotate(b)
                elif more:
                    norm_y(b + 1)

            batch(0, 0)
            with nc.vector.Fori(0, BATCHES // 2 - 1) as u:
                for j in range(2):
                    batch(u * 2 + (1 + j), 1 - j)
            batch(BATCHES - 1, 1)
            second_part(BATCHES - 1, 1)
            third_part(BATCHES - 1, 1)

        @block.gpsimd
        def _(pool):
            with nc.gpsimd.Fori(0, BATCHES) as b:
                for i in range(norms):
                    norm.pool(pool, b * norms + i)
                if not rope:
                    pool.wait_ge(y_ready, b + 1)
                    nc.gpsimd.tensor_copy(tiles_of(y_all, b), y[:]).then_inc(y_saved, 1)

        @block.scalar
        def _(act):
            if not rope:
                act.sem_inc(full_ready, 1)
                act.sem_inc(v_saved, 1)

            def second_parts(b, par):
                for x in range(2):
                    act.wait_ge(rest_ready, b * 2 + (x + 2))
                    nc.scalar.copy(parts[:, par, x, 1, :], rest[:, x, :]).then_inc(part2, 1)

            def batch(b, u, par):
                act.wait_ge(zt_ps, b + 1)
                if rope:
                    nc.scalar.copy(ht[:], ps[:, 0, :]).then_inc(ht_ready, 1)
                else:
                    nc.scalar.activation(ht[:], ps[:, 0, :], ACT.Identity, bias=w["ln1_b"][:, 0:1],
                                         scale=w["ln1_g"][:, 0:1]).then_inc(ht_ready, 1)
                if not isinstance(b, int) or b > 0:
                    second_parts(b - 1, 1 - par)
                if not rope:
                    act.wait_ge(qk_ps, b + 1)
                    for x in range(2):
                        nc.scalar.copy(full[:, x, :], ps[:, 1 + x, :]).then_inc(full_ready, 1)
                act.wait_ge(sent[par], u * (16 * SENDS) + 1)
                for x in range(2):
                    act.wait_ge(full_ready, b * 2 + (x + 2))
                    nc.scalar.copy(parts[:, par, x, 0, :], full[:, x, :]).then_inc(part1, 1)
                if not rope:
                    act.wait_ge(v_ps, b + 1)
                    nc.scalar.copy(tiles_of(v_all, b), ps[:, 3, :].rearrange("p (i e) -> p i e", i=QT)).then_inc(v_saved, 1)

            batch(0, 0, 0)
            with nc.scalar.Fori(0, BATCHES // 2 - 1) as u:
                batch(u * 2 + 1, u, 1)
                batch(u * 2 + 2, u + 1, 0)
            batch(BATCHES - 1, BATCHES // 2 - 1, 1)
            second_parts(BATCHES - 1, 1)

        @block.tensor
        def _(pe):
            with nc.tensor.Fori(0, BATCHES) as b:
                pe.wait_ge(z_ready, b + 1)
                for i in range(QT):
                    last = nc.tensor.transpose(ps[:, 0, i * P:(i + 1) * P], z[:, i, :], c["ident"][:])
                last.then_inc(zt_ps, 1)
                pe.wait_ge(ht_ready, b + 1)
                pe.wait_ge(full_ready, b * 2 + 1)
                for x, m in enumerate(("wq", "wk")):
                    last = nc.tensor.matmul(ps[:, 1 + x, :], w[m][:], ht[:], start=True, stop=True)
                    if rope:
                        last = nc.tensor.matmul(ps[:, 4 + x, :], w[m + "s"][:], ht[:], start=True, stop=True)
                last.then_inc(qk_ps, 1)
                pe.wait_ge(v_saved, b + 1)
                for i in range(QT):
                    last = nc.tensor.matmul(ps[:, 3, i * P:(i + 1) * P], ht[:, i * P:(i + 1) * P], w["wv"][:],
                                            start=True, stop=True)
                last.then_inc(v_ps, 1)

        @block.sync
        def _(sp):
            for par in range(2):
                sp.sem_inc(sent[par], 1)
            q_pairs = a["q_dram"].rearrange("(u two) d i t -> u two d i t", two=2)
            k_pairs = a["k_dram"].rearrange("(u two) j d i t -> u two j d i t", two=2)
            with nc.sync.Fori(0, BATCHES // 2) as u:
                for par in range(2):
                    b = u * 2 + par
                    sp.wait_ge(part3, b * 2 + 2)
                    sp.dma_start(q_pairs[bass.ds(u, 1), par, :, :, :].rearrange("a d i t -> (a d) i t"),
                                 parts[:, par, 0, :, :]).then_inc(sent[par], 16)
                    for i in range(PARTS):
                        sp.dma_start(k_pairs[bass.ds(u, 1), par, :, :, i, :].rearrange("a j d t -> d (a j) t"),
                                     parts[:, par, 1, :, :]).then_inc(sent[par], 16)
    st.clear()
    mem.close()


def attention_main(nc, name, causal, c, a, ps, v_all, ctx_all):
    st = Store(nc, ExitStack())
    name += "m_"
    qs, ks, vs, pt, ot, mx, mp, mr, rec = (a[n] for n in ("qs", "ks", "vs", "pt", "ot", "mx", "mp", "mr", "rec"))
    UNITS = 2 * QT
    MAXES = GH * QT
    OUT_BANK = 6
    TURN_MAX, TURN_OUT = 2, 9
    USES = MAXES + 2
    BANKS = (0, 1, 7)
    max_uses = [u for u in range(USES) if u not in (TURN_MAX, TURN_OUT)]
    scale = HD ** -0.5
    loaded = [st.sem(f"{name}stacks_loaded{g}") for g in range(GROUPS)]
    m_loaded = [st.sem(f"{name}max_loaded{g}") for g in range(GROUPS)]
    use_ready = st.sem(name + "bank_written")
    use_done = st.sem(name + "bank_read")
    m_step = st.sem(name + "max_split_step")
    m_split = st.sem(name + "max_split")
    st_ready = st.sem(name + "scores_t_ready")
    exp_done = st.sem(name + "exp_done")
    vs_ready = st.sem(name + "v_ready")
    pv_done = st.sem(name + "pv_done")
    ot_ready = st.sem(name + "out_copied")
    rec_ready = st.sem(name + "recip_ready")

    def keys(i):
        return (i + 1) * P if causal else SEQ

    def first_query(kt):
        return kt * P if causal else 0

    def used(t, use):
        if not isinstance(t, int):
            return (t - 1) * USES + (used(1, 0) + use)
        count = 0
        for t2 in range(-2, t + 1):
            for u in range(USES if t2 < t else use):
                ahead = 1 if u == TURN_MAX else -1 if u == TURN_OUT else 2
                count += 0 <= t2 + ahead < STEPS
        return count

    def bank(use):
        return BANKS[use % len(BANKS)]

    def steps(eng, step):
        for t in (-2, -1, 0):
            step(t, t % GROUPS)
        with eng.Fori(0, BATCHES - 1) as b:
            for g in range(GROUPS):
                step(b * GROUPS + (g + 1), (g + 1) % GROUPS)
        for t in range(STEPS - 3, STEPS + 1):
            step(t, t % GROUPS)

    def has(t, ahead):
        return not isinstance(t, int) or 0 <= t + ahead < STEPS

    with nc.Block() as block:
        @block.sync
        def _(sp):
            def load(b, g):
                mine = slice(g * GH * HD, (g + 1) * GH * HD)
                for j in range(PARTS):
                    rows = slice(j * HD * PARTS, (j + 1) * HD * PARTS)
                    sp.dma_start(qs[rows, g, :, :], a["q_dram"][bass.ds(b, 1), mine, :, :].rearrange(
                        "a (h e) i t -> (a e i) h t", h=GH)).then_inc(loaded[g], 16)
                    sp.dma_start(ks[rows, g, :, :], a["k_dram"][bass.ds(b, 1), j, mine, :, :].rearrange(
                        "a (h e) i t -> (a e i) h t", h=GH)).then_inc(loaded[g], 16)

            def send_max(s, g):
                sp.wait_ge(m_split, s + 1)
                for i in range(PARTS):
                    sp.dma_start(qs[ROWS + i:ROWS + i + 1, g, :, :].rearrange("p h (i q) -> p (h i) q", i=QT),
                                 mp[:, g % 2, i, :]).then_inc(m_loaded[g], 16)

            for g in range(GROUPS):
                load(0, g)
            send_max(0, 0)
            for par in range(2):
                sp.wait_ge(a["sent"][par], a["all_sent"])
            with nc.sync.Fori(0, BATCHES - 1) as b:
                for g in range(GROUPS):
                    t = b * GROUPS + g
                    send_max(t + 1, (g + 1) % GROUPS)
                    sp.wait_ge(st_ready, (t + 1) * UNITS)
                    load(b + 1, g)
            for t in range(STEPS - GROUPS, STEPS - 1):
                send_max(t + 1, (t + 1) % GROUPS)
            for g in range(GROUPS):
                sp.wait_ge(m_loaded[g], 16 * PARTS * BATCHES)

        @block.gpsimd
        def _(pool):
            def v_stack(b, g, wait):
                if wait:
                    pool.wait_ge(pv_done, (b * GROUPS + (g - GROUPS + 1)) * QT)
                last = nc.gpsimd.tensor_copy(
                    vs[:, g, :, :, 0:HD],
                    tiles_of(v_all, b)[:, :, g * GH * HD:(g + 1) * GH * HD].rearrange("p i (h e) -> p i h e", h=GH))
                last.then_inc(vs_ready, 1)

            for g in range(GROUPS):
                v_stack(0, g, False)
            with nc.gpsimd.Fori(0, BATCHES - 1) as b:
                for g in range(GROUPS):
                    v_stack(b + 1, g, True)

        @block.vector
        def _(dve):
            def maximum(t, g, u):
                s, i, h, use = t + 2, u // GH, u % GH, max_uses[u]
                dve.wait_ge(use_ready, used(t, use) + 1)
                nc.vector.reduce_max(mx[:, g % 2, h * QT + i:h * QT + i + 1], ps[:, bank(use), 0:keys(i)],
                                     AX.X).then_inc(use_done, 1)

            def split_max(s, g):
                if not isinstance(s, int) or s >= 2:
                    g2 = (g - 2) % GROUPS
                    dve.wait_ge(m_loaded[g2], sent_before(s, g))
                dve.wait_ge(use_ready, used(s - 1, TURN_MAX) + 1)
                m = ps[0:MAXES, bank(TURN_MAX), 0:P]
                p1 = mp[:, g % 2, 0, :]
                nc.vector.tensor_scalar(p1, m, -1.0, None, ALU.mult).then_inc(m_step, 1)
                dve.wait_ge(m_step, s * 2 + 1)
                nc.vector.scalar_tensor_tensor(mr[:], m, -1.0, p1, ALU.mult, ALU.subtract).then_inc(use_done, 1)

            def second_max_part(s, g):
                dve.wait_ge(use_done, used(s - 1, TURN_MAX) + 1)
                nc.vector.tensor_copy(mp[:, g % 2, 1, :], mr[:]).then_inc(m_step, 1)

            def third_max_part(s, g):
                dve.wait_ge(m_step, s * 2 + 2)
                nc.vector.tensor_tensor(mp[:, g % 2, 2, :], mr[:], mp[:, g % 2, 1, :], ALU.subtract).then_inc(m_split, 1)

            def sent_before(s, g):
                if isinstance(s, int):
                    return 16 * PARTS * ((s - 2) // GROUPS + 1)
                return (s - (2 + (g - 2) % GROUPS)) * (16 * PARTS // GROUPS) + 16 * PARTS

            def context(t, g):
                dve.wait_ge(use_ready, used(t + 1, TURN_OUT) + 1)
                o = ps[:, bank(TURN_OUT), :].rearrange("p (i h e) -> p i h e", i=QT, h=GH)
                nc.vector.reciprocal(rec[:], o[:, :, :, HD:HD + 1]).then_inc(rec_ready, 1)
                dve.wait_ge(rec_ready, t + 1)
                dst = ctx_all[:, bass.ds(t - g, QT), g * GH * HD:(g + 1) * GH * HD].rearrange("p i (h e) -> p i h e", h=GH)
                nc.vector.tensor_tensor(dst, o[:, :, :, 0:HD], rec[:].to_broadcast([P, QT, GH, HD]), ALU.mult).then_inc(use_done, 1)

            def step(t, g):
                for u in range(UNITS):
                    if has(t, 2):
                        maximum(t, (g + 2) % GROUPS, 2 * u)
                    if u == 1 and has(t, 1):
                        second_max_part(t + 1, (g + 1) % GROUPS)
                    if has(t, 2):
                        maximum(t, (g + 2) % GROUPS, 2 * u + 1)
                    if u == 1 and has(t, 1):
                        third_max_part(t + 1, (g + 1) % GROUPS)
                    if u == 0 and has(t, 1):
                        split_max(t + 1, (g + 1) % GROUPS)
                    if u == 3 and has(t, -1):
                        context(t - 1, (g - 1) % GROUPS)

            steps(nc.vector, step)

        @block.scalar
        def _(act):
            def exponential(t, g, u):
                kt, q0 = u // 2, first_query(u // 2)
                act.wait_ge(st_ready, t * UNITS + (u + 1))
                at(act, pv_done, t * QT + (kt - 1))
                nc.scalar.activation(pt[:, u % 4, :, q0:SEQ], ps[:, 2 + 2 * (u % 2):4 + 2 * (u % 2), q0:SEQ],
                                     ACT.Exp, scale=scale).then_inc(exp_done, 1)

            def copy_out(t):
                act.wait_ge(pv_done, (t + 1) * QT)
                act.wait_ge(use_ready, used(t, TURN_OUT) + 1 if not isinstance(t, int) or t > 0 else 1)
                nc.scalar.copy(ot[:], ps[:, OUT_BANK, :]).then_inc(ot_ready, 1)

            def step(t, g):
                for u in range(UNITS):
                    if has(t, 0):
                        exponential(t, g, u)
                    if u == 1 and has(t, -1):
                        copy_out(t - 1)

            steps(nc.scalar, step)

        @block.tensor
        def _(pe):
            def first_pass(t, g, u, b_count):
                i, h, use = u // GH, u % GH, max_uses[u]
                if u == 0:
                    pe.wait_ge(loaded[g], b_count * (2 * PARTS * 16))
                bank_free(t, use)
                q = qs[0:ROWS, g, h, i * P:(i + 1) * P]
                last = nc.tensor.matmul(ps[:, bank(use), 0:keys(i)], q, ks[0:ROWS, g, h, 0:keys(i)],
                                        start=True, stop=not causal)
                if causal:
                    last = nc.tensor.matmul(ps[:, bank(use), i * P:(i + 1) * P], c["identb"][:], c["after_q"][:],
                                            start=False, stop=True)
                last.then_inc(use_ready, 1)

            def bank_free(t, use):
                at(pe, use_done, used(t, use - len(BANKS) + 1) if use >= len(BANKS) - 1 or not isinstance(t, int)
                   else used(t - 1, USES + use - len(BANKS) + 1) if t > -2 else 0)

            def turn_max(s, g):
                pe.wait_ge(use_done, used(s - 1, 0))
                bank_free(s - 1, TURN_MAX)
                nc.tensor.transpose(ps[0:MAXES, bank(TURN_MAX), 0:P], mx[:, g % 2, :], c["ident"][:]).then_inc(use_ready, 1)

            def second_pass(t, g, u, b_count):
                kt, q0 = u // 2, first_query(u // 2)
                if u == 0:
                    pe.wait_ge(m_loaded[g], b_count * (16 * PARTS))
                at(pe, exp_done, t * UNITS + (u - 1))
                for n in range(2):
                    h = 2 * (u % 2) + n
                    pair = 2 + 2 * (u % 2) + n
                    last = nc.tensor.matmul(ps[:, pair, q0:SEQ], ks[0:STACK, g, h, kt * P:(kt + 1) * P],
                                            qs[0:STACK, g, h, q0:SEQ], start=True, stop=not causal)
                    if causal:
                        last = nc.tensor.matmul(ps[:, pair, q0:q0 + P], c["identb"][:], c["after_k"][:],
                                                start=False, stop=True)
                last.then_inc(st_ready, 1)

            def values(t, g, kt):
                q0 = first_query(kt)
                pe.wait_ge(exp_done, t * UNITS + (2 * kt + 2))
                if kt == 0:
                    pe.wait_ge(vs_ready, t + 1)
                    at(pe, ot_ready, t)
                for h in range(GH):
                    last = nc.tensor.matmul(ps[32 * h:32 * h + 32, OUT_BANK, q0:SEQ], vs[:, g, kt, h, :],
                                            pt[:, 2 * (kt % 2) + h // 2, h % 2, q0:SEQ],
                                            start=kt == 0, stop=kt == QT - 1)
                last.then_inc(pv_done, 1)

            def turn_out(t):
                pe.wait_ge(ot_ready, t + 1)
                bank_free(t + 1, TURN_OUT)
                for i in range(QT):
                    last = nc.tensor.transpose(ps[:, bank(TURN_OUT), i * P:(i + 1) * P], ot[:, i * P:(i + 1) * P], c["ident"][:])
                last.then_inc(use_ready, 1)

            def step(t, g):
                for u in range(UNITS):
                    if has(t, 2):
                        first_pass(t, (g + 2) % GROUPS, 2 * u, uses(t + 2, (g + 2) % GROUPS))
                    if has(t, 0):
                        second_pass(t, g, u, uses(t, g))
                    if has(t, 2):
                        first_pass(t, (g + 2) % GROUPS, 2 * u + 1, uses(t + 2, (g + 2) % GROUPS))
                    if u == 0 and has(t, 1):
                        turn_max(t + 1, (g + 1) % GROUPS)
                    if u == 1 and has(t, -1):
                        values(t - 1, (g - 1) % GROUPS, QT - 1)
                    if u == 3 and has(t, -1):
                        turn_out(t - 1)
                    if u % 2 == 1 and u > 1 and has(t, 0):
                        values(t, g, u // 2 - 1)

            def uses(t, g):
                if isinstance(t, int):
                    return t // GROUPS + 1
                return Quotient(t - g)

            steps(nc.tensor, step)
    a["unsent"].clear()
    st.clear()


class Quotient:

    def __init__(self, t):
        self.t = t

    def __mul__(self, by):
        assert by % GROUPS == 0
        return self.t * (by // GROUPS) + by


def attention_back(nc, name, c, w, ps, x_res, ctx_all):
    mem = ExitStack()
    st = Store(nc, mem)
    name += "b_"
    cs = st.sb(name + "ctx", [P, QT, P])
    ct = st.sb(name + "ctx_t", [P, SEQ])
    sub = st.sb(name + "sum", [P, QT, P])
    cs_ready = st.sem(name + "ctx_ready")
    ct_ps = st.sem(name + "ctx_t_in_psum")
    ct_ready = st.sem(name + "ctx_t_ready")
    o_ps = st.sem(name + "out_in_psum")
    sub_ready = st.sem(name + "sum_ready")
    x_done = st.sem(name + "x_done")
    with nc.Block() as block:
        @block.gpsimd
        def _(pool):
            nc.gpsimd.tensor_copy(cs[:], tiles_of(ctx_all, 0)).then_inc(cs_ready, 1)
            with nc.gpsimd.Fori(1, BATCHES) as b:
                pool.wait_ge(ct_ps, b)
                nc.gpsimd.tensor_copy(cs[:], tiles_of(ctx_all, b)).then_inc(cs_ready, 1)

        @block.tensor
        def _(pe):
            with nc.tensor.Fori(0, BATCHES) as b:
                pe.wait_ge(cs_ready, b + 1)
                for i in range(QT):
                    last = nc.tensor.transpose(ps[:, 0, i * P:(i + 1) * P], cs[:, i, :], c["ident"][:])
                last.then_inc(ct_ps, 1)
                pe.wait_ge(ct_ready, b + 1)
                pe.wait_ge(sub_ready, b + 1)
                for i in range(QT):
                    last = nc.tensor.matmul(ps[:, 1, i * P:(i + 1) * P], ct[:, i * P:(i + 1) * P], w["wo"][:],
                                            start=True, stop=True)
                last.then_inc(o_ps, 1)

        @block.scalar
        def _(act):
            with nc.scalar.Fori(0, BATCHES) as b:
                act.wait_ge(ct_ps, b + 1)
                nc.scalar.copy(ct[:], ps[:, 0, :]).then_inc(ct_ready, 1)

        @block.vector
        def _(dve):
            dve.sem_inc(sub_ready, 1)
            with nc.vector.Fori(0, BATCHES) as b:
                dve.wait_ge(o_ps, b + 1)
                nc.vector.tensor_tensor(sub[:], ps[:, 1, :].rearrange("p (i e) -> p i e", i=QT),
                                        w["bo"][:].rearrange("p (o e) -> p o e", o=1).to_broadcast([P, QT, P]),
                                        ALU.add).then_inc(sub_ready, 1)
                dve.wait_ge(sub_ready, b + 2)
                nc.vector.tensor_tensor(tiles_of(x_res, b), tiles_of(x_res, b), sub[:], ALU.add).then_inc(x_done, 1)
                dve.wait_ge(x_done, b + 1)
    st.clear()
    mem.close()


def experts(nc, name, d, c, w, ps, x_res, y_all, ctx_all, out):
    mem = ExitStack()
    st = Store(nc, mem)
    name += "e_"
    SLOTS = EXPERTS
    cs = st.sb(name + "ctx", [P, QT, P])
    ct = st.sb(name + "ctx_t", [P, SEQ])
    x2 = st.sb(name + "x2", [P, QT, P])
    z = st.sb(name + "z", [P, QT, P])
    xt = st.sb(name + "xt", [P, 2, SEQ])
    acc = st.sb(name + "acc", [P, 2, QT, P])
    gate = st.sb(name + "gate", [P, 2, QT, EXPERTS])
    gt = st.sb(name + "gate_t", [EXPERTS, SEQ])
    ht = st.sb(name + "ht", [P, 2, FC, SEQ])
    lg = st.sb(name + "logits", [P, QT, EXPERTS])
    eq = st.sb(name + "equal", [P, QT, EXPERTS])
    key = st.sb(name + "key", [P, QT, EXPERTS])
    pick1 = st.sb(name + "pick1", [P, QT, EXPERTS])
    pick2 = st.sb(name + "pick2", [P, QT, EXPERTS])
    left = st.sb(name + "left", [P, QT, EXPERTS])
    top = st.sb(name + "top", [P, 2, QT])
    rank = st.sb(name + "rank", [P, 2, QT])
    gap = st.sb(name + "gap", [P, QT])
    share = st.sb(name + "share", [P, 2, QT])
    norm = Norm(st, c, name + "norm", 1e-5)
    cs_ready = st.sem(name + "ctx_ready")
    ct_ps = st.sem(name + "ctx_t_in_psum")
    ct_ready = st.sem(name + "ctx_t_ready")
    o_ps = st.sem(name + "out_in_psum")
    x2_ready = st.sem(name + "x2_ready")
    z_ready = st.sem(name + "z_ready")
    zt_ps = st.sem(name + "zt_in_psum")
    xt_ready = st.sem(name + "xt_ready")
    lg_ps = st.sem(name + "logits_in_psum")
    g_step = st.sem(name + "gate_step")
    gap_ready = st.sem(name + "gap_ready")
    tanh_done = st.sem(name + "tanh_done")
    share_done = st.sem(name + "share_done")
    gate_ready = st.sem(name + "gate_ready")
    gt_ps = st.sem(name + "gate_t_in_psum")
    gt_ready = st.sem(name + "gate_t_ready")
    b2_ps = st.sem(name + "bias_in_psum")
    sum_ready = st.sem(name + "acc_start")
    acc_ready = st.sem(name + "acc_ready")
    up_ps = st.sem(name + "up_in_psum")
    h_ready = st.sem(name + "h_ready")
    down_ps = st.sem(name + "down_in_psum")
    added = st.sem(name + "added")
    x_done = st.sem(name + "x_done")
    stored = st.sem(name + "stored")
    G_STEPS = 13
    UP_BANKS = (2, 3, 6, 7)

    def batches(eng, batch):
        with eng.Fori(0, (BATCHES - 2) // 2) as u:
            for j in range(2):
                batch(u * 2 + j, j, True)
        batch(BATCHES - 2, 0, True)
        batch(BATCHES - 1, 1, False)

    with nc.Block() as block:
        @block.gpsimd
        def _(pool):
            nc.gpsimd.tensor_copy(cs[:], tiles_of(ctx_all, 0)).then_inc(cs_ready, 1)
            norm.pool(pool, 0)
            with nc.gpsimd.Fori(1, BATCHES) as b:
                pool.wait_ge(ct_ps, b)
                nc.gpsimd.tensor_copy(cs[:], tiles_of(ctx_all, b)).then_inc(cs_ready, 1)
                norm.pool(pool, b)

        @block.tensor
        def _(pe):
            def prepare(b, par, slot):
                if slot == 0:
                    pe.wait_ge(cs_ready, b + 1)
                    at(pe, acc_ready, b)
                    for i in range(QT):
                        last = nc.tensor.transpose(ps[:, 0, i * P:(i + 1) * P], cs[:, i, :], c["ident"][:])
                    last.then_inc(ct_ps, 1)
                if slot == 1:
                    pe.wait_ge(ct_ready, b + 1)
                    at(pe, gt_ready, b)
                    for i in range(QT):
                        last = nc.tensor.matmul(ps[:, 1, i * P:(i + 1) * P], ct[:, i * P:(i + 1) * P], w["wo"][:],
                                                start=True, stop=True)
                    last.then_inc(o_ps, 1)
                if slot == 3:
                    pe.wait_ge(z_ready, b + 1)
                    for i in range(QT):
                        last = nc.tensor.transpose(ps[:, 0, i * P:(i + 1) * P], z[:, i, :], c["ident"][:])
                    last.then_inc(zt_ps, 1)
                if slot == 4:
                    pe.wait_ge(xt_ready, b + 1)
                    pe.wait_ge(x2_ready, b + 1)
                    for i in range(QT):
                        last = nc.tensor.matmul(ps[:, 1, i * EXPERTS:(i + 1) * EXPERTS], xt[:, par, i * P:(i + 1) * P],
                                                w["wg"][:], start=True, stop=True)
                    last.then_inc(lg_ps, 1)
                if slot == 6:
                    pe.wait_ge(gate_ready, b + 1)
                    for i in range(QT):
                        last = nc.tensor.transpose(ps[0:EXPERTS, 1, i * P:(i + 1) * P], gate[:, par, i, :], c["ident"][:])
                    last.then_inc(gt_ps, 1)
                if slot == 7:
                    pe.wait_ge(gt_ready, b + 1)
                    for i in range(QT):
                        last = nc.tensor.matmul(ps[:, 0, i * P:(i + 1) * P], gt[:, i * P:(i + 1) * P], w["b2"][:],
                                                start=True, stop=True)
                    last.then_inc(b2_ps, 1)

            def up(b, par, e, n):
                if e == 0:
                    pe.wait_ge(xt_ready, b + 1)
                for f in range(FC):
                    at(pe, h_ready, n * FC + (f - FC + 1))
                    nc.tensor.matmul(ps[:, UP_BANKS[f], :], w["w1"][:, e, f * P:(f + 1) * P], xt[:, par, :],
                                     start=True, stop=True).then_inc(up_ps, 1)

            def down(e, n):
                pe.wait_ge(h_ready, n * FC + FC)
                pe.wait_ge(added, n + 1)
                for i in range(QT):
                    for f in range(FC):
                        last = nc.tensor.matmul(ps[:, 4 + e % 2, i * P:(i + 1) * P], ht[:, e % 2, f, i * P:(i + 1) * P],
                                                w["w2"][:, e * FC + f, :], start=f == 0, stop=f == FC - 1)
                last.then_inc(down_ps, 1)

            def batch(b, par, more):
                for e in range(EXPERTS):
                    n = b * EXPERTS + e
                    if more and e < EXPERTS:
                        prepare(b + 1, 1 - par, e)
                    if e + 1 < EXPERTS:
                        up(b, par, e + 1, n + 1)
                    elif more:
                        up(b + 1, 1 - par, 0, n + 1)
                    down(e, n)

            pe.sem_inc(down_ps, 1)
            pe.wait_ge(w["arrived"], 16 * w["loads"])
            for slot in range(SLOTS):
                prepare(0, 0, slot)
            up(0, 0, 0, 0)
            batches(nc.tensor, batch)

        @block.scalar
        def _(act):
            def prepare(b, par, slot):
                if slot == 0:
                    act.wait_ge(ct_ps, b + 1)
                    nc.scalar.copy(ct[:], ps[:, 0, :]).then_inc(ct_ready, 1)
                if slot == 3:
                    act.wait_ge(zt_ps, b + 1)
                    nc.scalar.activation(xt[:, par, :], ps[:, 0, :], ACT.Identity, bias=w["ln2_b"][:, 0:1],
                                         scale=w["ln2_g"][:, 0:1]).then_inc(xt_ready, 1)
                if slot == 5:
                    act.wait_ge(gap_ready, b + 1)
                    nc.scalar.activation(gap[:], gap[:], ACT.Tanh, scale=0.5).then_inc(tanh_done, 1)
                if slot == 6:
                    act.wait_ge(gt_ps, b + 1)
                    nc.scalar.copy(gt[:], ps[0:EXPERTS, 1, :]).then_inc(gt_ready, 1)

            def gelu(e, n):
                at(act, down_ps, n)
                for f in range(FC):
                    act.wait_ge(up_ps, n * FC + (f + 1))
                    nc.scalar.activation(ht[:, e % 2, f, :], ps[:, UP_BANKS[f], :], ACT.Gelu_apprx_tanh,
                                         bias=w["b1"][:, e * FC + f:e * FC + f + 1]).then_inc(h_ready, 1)

            def batch(b, par, more):
                for e in range(EXPERTS):
                    if more:
                        prepare(b + 1, 1 - par, e)
                    if e + 1 < EXPERTS or more:
                        gelu((e + 1) % EXPERTS, b * EXPERTS + (e + 1))

            for slot in range(SLOTS):
                prepare(0, 0, slot)
            gelu(0, 0)
            batches(nc.scalar, batch)

        @block.vector
        def _(dve):
            v = nc.vector

            def per_token(ap):
                return ap.rearrange("p (i o) -> p i o", o=1).to_broadcast([P, QT, EXPERTS])

            steps = [0]

            def step(b, ins):
                steps[0] = steps[0] % G_STEPS + 1
                ins.then_inc(g_step, 1)
                dve.wait_ge(g_step, b * G_STEPS + steps[0])

            def choose(b):
                dve.wait_ge(lg_ps, b + 1)
                step(b, v.tensor_copy(lg[:], ps[:, 1, 0:QT * EXPERTS].rearrange("p (i e) -> p i e", i=QT)))
                for j, (src, pick) in enumerate(((lg, pick1), (left, pick2))):
                    step(b, v.tensor_reduce(top[:, j, :], src[:], AX.X, ALU.max))
                    step(b, v.tensor_tensor(eq[:], src[:], per_token(top[:, j, :]), ALU.is_equal))
                    step(b, v.tensor_tensor(key[:], eq[:], w["rev"][:], ALU.mult))
                    step(b, v.tensor_reduce(rank[:, j, :], key[:], AX.X, ALU.max))
                    step(b, v.tensor_tensor(pick[:], key[:], per_token(rank[:, j, :]), ALU.is_equal))
                    if j == 0:
                        step(b, v.scalar_tensor_tensor(left[:], pick1[:], -3e38, lg[:], ALU.mult, ALU.add))
                v.tensor_tensor(gap[:], top[:, 0, :], top[:, 1, :], ALU.subtract).then_inc(gap_ready, 1)

            def shares(b, par):
                dve.wait_ge(tanh_done, b + 1)
                v.tensor_scalar(share[:, 0, :], gap[:], 0.5, 0.5, ALU.mult, ALU.add)
                step(b, v.tensor_scalar(share[:, 1, :], gap[:], -0.5, 0.5, ALU.mult, ALU.add))
                v.tensor_tensor(pick1[:], pick1[:], per_token(share[:, 0, :]), ALU.mult)
                v.tensor_tensor(pick2[:], pick2[:], per_token(share[:, 1, :]), ALU.mult).then_inc(share_done, 1)
                dve.wait_ge(share_done, b + 1)
                v.tensor_tensor(gate[:, par, :, :], pick1[:], pick2[:], ALU.add).then_inc(gate_ready, 1)
                assert steps[0] == G_STEPS, steps

            def prepare(b, par, slot):
                if slot == 1:
                    dve.wait_ge(o_ps, b + 1)
                    v.tensor_tensor(x2[:], tiles_of(y_all, b), ps[:, 1, :].rearrange("p (i e) -> p i e", i=QT),
                                    ALU.add).then_inc(x2_ready, 1)
                    dve.wait_ge(x2_ready, b + 1)
                    norm.vector(dve, b, [x2[:, i, :] for i in range(QT)], [z[:, i, :] for i in range(QT)]).then_inc(z_ready, 1)
                if slot == 4:
                    choose(b)
                if slot == 5:
                    shares(b, par)
                if slot == 7:
                    dve.wait_ge(b2_ps, b + 1)
                    v.tensor_tensor(acc[:, par, :, :], x2[:], ps[:, 0, :].rearrange("p (i e) -> p i e", i=QT),
                                    ALU.add).then_inc(sum_ready, 1)
                    dve.wait_ge(sum_ready, b + 1)
                    v.tensor_tensor(acc[:, par, :, :], acc[:, par, :, :], tiles_of(x_res, b), ALU.add).then_inc(acc_ready, 1)

            def add(b, par, e, n):
                dve.wait_ge(down_ps, n + 2)
                if e == 0:
                    dve.wait_ge(acc_ready, b + 1)
                    dve.wait_ge(gate_ready, b + 1)
                else:
                    dve.wait_ge(added, n + 2)
                for i in range(QT):
                    dst = acc[:, par, i, :] if e < EXPERTS - 1 else tile_of(x_res, b * QT + i)
                    last = v.scalar_tensor_tensor(dst, ps[:, 4 + e % 2, i * P:(i + 1) * P], gate[:, par, i, e:e + 1],
                                                  acc[:, par, i, :], ALU.mult, ALU.add)
                last.then_inc(added, 1)

            def batch(b, par, more):
                for e in range(EXPERTS):
                    if more:
                        prepare(b + 1, 1 - par, e)
                    add(b, par, e, b * EXPERTS + e)

            dve.wait_ge(w["arrived"], 16 * w["loads"])
            dve.sem_inc(added, 2)
            for slot in range(SLOTS):
                prepare(0, 0, slot)
            batches(nc.vector, batch)

        if out is not None:
            out_v = out.rearrange("b (i p) e -> p b i e", p=P)

            @block.sync
            def _(sp):
                with nc.sync.Fori(0, BATCHES) as b:
                    sp.wait_ge(added, b * EXPERTS + (EXPERTS + 2))
                    sp.dma_start(out_v[:, bass.ds(b, 1), :, :].rearrange("p a i e -> p (a i) e"),
                                 tiles_of(x_res, b)).then_inc(stored, 16)
                sp.wait_ge(stored, 16 * BATCHES)
    st.clear()
    mem.close()


_INS = ["L0_attn_a_x", "L0_attn_a_Wq", "L0_attn_a_Wk", "L0_attn_a_Wv", "L0_attn_a_Wo", "L0_attn_a_proj",
        "L0_attn_a_W1", "L0_attn_a_b1", "L0_attn_a_W2", "L0_attn_a_b2", "L0_attn_a_ln1_g", "L0_attn_a_ln1_b",
        "L0_attn_a_ln2_g", "L0_attn_a_ln2_b", "L0_attn_b_wq", "L0_attn_b_bq", "L0_attn_b_wk", "L0_attn_b_bk",
        "L0_attn_b_wv", "L0_attn_b_bv", "L0_attn_b_wo", "L0_attn_b_bo", "L0_ffn_ln1_g", "L0_ffn_ln1_b",
        "L0_ffn_ln2_g", "L0_ffn_ln2_b", "L0_ffn_Wq", "L0_ffn_Wk", "L0_ffn_Wv", "L0_ffn_Wo", "L0_ffn_Wg",
        "L0_ffn_W1", "L0_ffn_b1", "L0_ffn_W2", "L0_ffn_b2"]


def tables():
    t = {}
    row, chunk, head = np.arange(P)[:, None, None], np.arange(CH)[None, :, None], np.arange(PH)[None, None, :]
    t["perf_mask"] = (head == 2 * chunk + row // PM).astype(np.float32)
    inv_freq = (np.float32(1) / np.float32(10000) ** (np.arange(0, HD, 2, dtype=np.float32) / np.float32(HD)))
    angle = np.arange(SEQ, dtype=np.float32)[None, :] * inv_freq.astype(np.float32)[:, None]
    cos, sin = np.cos(angle).astype(np.float32), np.sin(angle).astype(np.float32)
    rows = np.arange(P)
    t["rope_cos"] = np.ascontiguousarray(cos[(rows % HD) // 2])
    t["rope_sin"] = np.ascontiguousarray(sin[(rows % HD) // 2] * np.where(rows % 2, 1, -1)[:, None].astype(np.float32))
    t["expert_rank"] = np.ascontiguousarray(np.broadcast_to(
        np.arange(EXPERTS, 0, -1, dtype=np.float32), (P, QT, EXPERTS)))
    return t


def kernel(**inputs):
    import concourse.bacc as bacc
    from concourse.bass_utils import run_bass_kernel_spmd

    nc = bacc.Bacc("TRN2", target_bir_lowering=False, num_devices=1)
    given = {n: np.ascontiguousarray(inputs[n]) for n in _INS} | tables()
    arrays, d = {}, {}
    for n, a in given.items():
        arrays[f"in_{n}"] = a
        d[n] = nc.dram_tensor(f"in_{n}", a.shape, mybir.dt.from_np(a.dtype), kind="ExternalInput").ap()
    out = nc.dram_tensor("out_x", (BATCHES, SEQ, P), F32, kind="ExternalOutput").ap()
    build(nc, d, out)
    r = run_bass_kernel_spmd(nc, [arrays], core_ids=[0])
    return r.results[0]["out_x"]
```
